# Optimizing a Trainium2 kernel written in Bass

```python
import numpy as np
import jax
import jax.numpy as jnp

def _softmax(x, axis=-1):
    return jax.nn.softmax(x, axis=axis)

def _gelu(x):
    return jax.nn.gelu(x, approximate=True)

def _silu(x):
    return jax.nn.silu(x)

def _sigmoid(x):
    return jax.nn.sigmoid(x)

def _layernorm(x, axis=-1, eps=1e-05):
    m = jnp.mean(x, axis=axis, keepdims=True)
    v = jnp.var(x, axis=axis, keepdims=True)
    return (x - m) / jnp.sqrt(v + eps)

def _scatter_add(tgt, idx, src, axis=0):
    return tgt.at[idx].add(src)

def _segment_sum(src, seg, n):
    return jax.ops.segment_sum(src, seg, n)
kernel_name = 'mk_decoder_postln_d2_seqx_r4_c60be5'

def setup_inputs(seed: int=0):
    np.random.seed(seed)
    _w = jnp.asarray

    def _rec_inputs():
        import jax
        import jax.numpy as jnp
        _rk = jax.random.key(seed)
        x = 7.22e-05 + 1 * jax.random.normal(jax.random.fold_in(_rk, 1), (8, 512, 256), jnp.float32)
        _lenS = 512 - jax.random.randint(jax.random.fold_in(_rk, 7), (8,), 0, max(1, 512 // 4) + 1, jnp.int32)
        _lenS2 = 64 - jax.random.randint(jax.random.fold_in(_rk, 8), (8,), 0, max(1, 64 // 4) + 1, jnp.int32)
        _ctx_1024P = jax.random.normal(jax.random.fold_in(_rk, 11), (8, 16, 256), jnp.float32)
        _ctx_1024c = jax.random.dirichlet(jax.random.fold_in(_rk, 511), 0.3 * jnp.ones((16,), jnp.float32), (8, 64))
        _ctx_1024t = jnp.einsum('bsk,bkd->bsd', _ctx_1024c, _ctx_1024P)
        _ctx_1024t = _ctx_1024t * jax.lax.rsqrt(jnp.mean(jnp.square(_ctx_1024t)) + 1e-12) * 0.953939
        ctx_1024 = 4.13588e-05 + 0.999923 * (_ctx_1024t + 0.3 * jax.random.normal(jax.random.fold_in(_rk, 611), (8, 64, 256), jnp.float32))
        return (x, ctx_1024)
    x, ctx_1024 = _rec_inputs()

    def _L0_attn_setup():
        import jax, jax.numpy as jnp
        import numpy as np
        EPS = 1e-06

        def _feature_map(x):
            return jax.nn.elu(x) + 1.0
        key = jax.random.key(seed)
        ks = jax.random.split(key, 4)
        B, L, C = (4, 2048, 256)
        s = 1.0 / np.sqrt(C)
        x = jax.random.normal(ks[0], (B, L, C), dtype=jnp.float32)
        Wq = jax.random.normal(ks[1], (C, C), dtype=jnp.float32) * s
        Wk = jax.random.normal(ks[2], (C, C), dtype=jnp.float32) * s
        Wv = jax.random.normal(ks[3], (C, C), dtype=jnp.float32) * s
        bq = jnp.zeros((C,), jnp.float32)
        bk = jnp.zeros((C,), jnp.float32)
        bv = jnp.zeros((C,), jnp.float32)
        return {'x': x, 'Wq': Wq, 'bq': bq, 'Wk': Wk, 'bk': bk, 'Wv': Wv, 'bv': bv}
    _L0_attn_all = _L0_attn_setup()
    _L0_attn_in = {k: v for k, v in _L0_attn_all.items() if k in ('Wq', 'bq', 'Wk', 'bk', 'Wv', 'bv')}
    del _L0_attn_all

    def _L0_xattn_setup():
        import jax, jax.numpy as jnp
        import numpy as np
        HEADS = 16
        EMBED = 256
        HEAD_DIM = EMBED // HEADS
        key = jax.random.key(seed)
        ks = jax.random.split(key, 11)
        B, S, E = (4, 512, EMBED)
        s = 1.0 / np.sqrt(E)
        return {'query': jax.random.normal(ks[0], (B, S, E), jnp.float32), 'key': jax.random.normal(ks[1], (B, S, E), jnp.float32), 'value': jax.random.normal(ks[2], (B, S, E), jnp.float32), 'Wq': jax.random.normal(ks[3], (E, E), jnp.float32) * s, 'bq': jax.random.normal(ks[4], (E,), jnp.float32) * s, 'Wk': jax.random.normal(ks[5], (E, E), jnp.float32) * s, 'bk': jax.random.normal(ks[6], (E,), jnp.float32) * s, 'Wv': jax.random.normal(ks[7], (E, E), jnp.float32) * s, 'bv': jax.random.normal(ks[8], (E,), jnp.float32) * s, 'Wo': jax.random.normal(ks[9], (E, E), jnp.float32) * s, 'bo': jax.random.normal(ks[10], (E,), jnp.float32) * s}
    _L0_xattn_all = _L0_xattn_setup()
    _L0_xattn_in = {k: v for k, v in _L0_xattn_all.items() if k in ('Wq', 'bq', 'Wk', 'bk', 'Wv', 'bv', 'Wo', 'bo')}
    del _L0_xattn_all

    def _L0_ffn_setup():
        import jax, jax.numpy as jnp
        import numpy as np
        BLOCK = 32
        W_BITS = 4
        ACT_BITS = 16

        def act_qdq(x):
            qmax = 2.0 ** (ACT_BITS - 1) - 1.0
            scale = jnp.maximum(jnp.max(jnp.abs(x)) / qmax, 1e-12)
            return jnp.clip(jnp.round(x / scale), -qmax - 1.0, qmax) * scale

        def fixed_qdq_u16(x):
            scale = 1.0 / 65536.0
            return jnp.clip(jnp.round(x / scale), 0.0, 65535.0) * scale

        def lpbq_dequant(w):
            O, I = w.shape
            qmax = 2.0 ** (W_BITS - 1) - 1.0
            wb = w.reshape(O, I // BLOCK, BLOCK)
            s = jnp.maximum(jnp.max(jnp.abs(wb), axis=-1, keepdims=True) / qmax, 1e-12)
            wq = jnp.clip(jnp.round(wb / s), -qmax - 1.0, qmax) * s
            return wq.reshape(O, I)
        key = jax.random.key(seed)
        k1, k2, k3, k4 = jax.random.split(key, 4)
        B, S, H, I = (2, 1024, 256, 768)
        x = jax.random.normal(k1, (B, S, H), jnp.float32)
        w_gate = jax.random.normal(k2, (I, H), jnp.float32) * 0.02
        w_up = jax.random.normal(k3, (I, H), jnp.float32) * 0.02
        w_down = jax.random.normal(k4, (H, I), jnp.float32) * 0.02
        return {'x': x, 'w_gate': w_gate, 'w_up': w_up, 'w_down': w_down}
    _L0_ffn_all = _L0_ffn_setup()
    _L0_ffn_in = {k: v for k, v in _L0_ffn_all.items() if k in ('w_gate', 'w_up', 'w_down')}
    del _L0_ffn_all

    def _L1_attn_setup():
        import jax, jax.numpy as jnp
        import numpy as np
        import math
        B, W, C, N = (4, 512, 256, 16)
        K = C // N
        key = jax.random.key(seed)
        k1, k2, k3, k4, k5 = jax.random.split(key, 5)
        return {'in_sequence_bwc': jax.random.normal(k1, (B, W, C), dtype=jnp.float32), 'W_proj': jax.random.normal(k2, (C, C), dtype=jnp.float32) * 0.02, 'pre_metric_nkk': jax.random.normal(k3, (N, K, K), dtype=jnp.float32) * 0.1, 'transforms_nkk': jax.random.normal(k4, (N, K, K), dtype=jnp.float32) * 0.1, 'W_mixer': jax.random.normal(k5, (C, C), dtype=jnp.float32) * 0.02}
    _L1_attn_all = _L1_attn_setup()
    _L1_attn_in = {k: v for k, v in _L1_attn_all.items() if k in ('W_proj', 'pre_metric_nkk', 'transforms_nkk', 'W_mixer')}
    del _L1_attn_all

    def _L1_xattn_setup():
        import jax, jax.numpy as jnp
        import numpy as np
        B, N, M = (4, 512, 512)
        DIM = 256
        HEADS = 16
        DIM_HEAD = 64
        INNER = HEADS * DIM_HEAD
        SCALE = 8.0

        def layer_norm(x, g, eps=1e-05):
            mean = jnp.mean(x, axis=-1, keepdims=True)
            var = jnp.mean((x - mean) ** 2, axis=-1, keepdims=True)
            return (x - mean) * jax.lax.rsqrt(var + eps) * g

        def l2norm(t, eps=1e-12):
            n = jnp.maximum(jnp.linalg.norm(t, axis=-1, keepdims=True), eps)
            return t / n
        key = jax.random.key(seed)
        ks = jax.random.split(key, 8)
        x = jax.random.normal(ks[0], (B, N, DIM), dtype=jnp.float32)
        context = jax.random.normal(ks[1], (B, M, DIM), dtype=jnp.float32)
        g_norm = jnp.ones((DIM,), dtype=jnp.float32)
        null_kv = jax.random.normal(ks[2], (2, DIM_HEAD), dtype=jnp.float32)
        Wq = jax.random.normal(ks[3], (DIM, INNER), dtype=jnp.float32) / np.sqrt(DIM)
        Wkv = jax.random.normal(ks[4], (DIM, 2 * INNER), dtype=jnp.float32) / np.sqrt(DIM)
        q_scale = jnp.ones((DIM_HEAD,), dtype=jnp.float32)
        k_scale = jnp.ones((DIM_HEAD,), dtype=jnp.float32)
        Wout = jax.random.normal(ks[5], (INNER, DIM), dtype=jnp.float32) / np.sqrt(INNER)
        g_out = jnp.ones((DIM,), dtype=jnp.float32)
        return {'x': x, 'context': context, 'g_norm': g_norm, 'null_kv': null_kv, 'Wq': Wq, 'Wkv': Wkv, 'q_scale': q_scale, 'k_scale': k_scale, 'Wout': Wout, 'g_out': g_out}
    _L1_xattn_all = _L1_xattn_setup()
    _L1_xattn_in = {k: v for k, v in _L1_xattn_all.items() if k in ('g_norm', 'null_kv', 'Wq', 'Wkv', 'q_scale', 'k_scale', 'Wout', 'g_out')}
    del _L1_xattn_all

    def _L1_ffn_setup():
        import jax, jax.numpy as jnp
        import numpy as np
        B, N, D = (4, 512, 256)
        SPARSITY = 0.01
        key = jax.random.key(seed)
        k1, k2, k3 = jax.random.split(key, 3)
        x = jax.random.normal(k1, (B, N, D), dtype=jnp.float32)
        spatial = jax.random.normal(k2, (D, D), dtype=jnp.float32) * 0.02
        freq = jnp.fft.fft(spatial, axis=-1)
        k = int(D * SPARSITY)
        mag = jnp.abs(freq)
        kth = jax.lax.top_k(mag, k)[0][:, -1:]
        w_sparse = jnp.where(mag >= kth, freq, 0.0 + 0j)
        bias = jax.random.normal(k3, (D,), dtype=jnp.float32) * 0.01
        return {'x': x, 'w_freq_real': jnp.real(w_sparse).astype(jnp.float32), 'w_freq_imag': jnp.imag(w_sparse).astype(jnp.float32), 'bias': bias}
    _L1_ffn_all = _L1_ffn_setup()
    _L1_ffn_in = {k: v for k, v in _L1_ffn_all.items() if k in ('w_freq_real', 'w_freq_imag', 'bias')}
    del _L1_ffn_all
    return {'x': x, 'ctx_1024': ctx_1024, 'L0_attn_Wq': _L0_attn_in['Wq'], 'L0_attn_bq': _L0_attn_in['bq'], 'L0_attn_Wk': _L0_attn_in['Wk'], 'L0_attn_bk': _L0_attn_in['bk'], 'L0_attn_Wv': _L0_attn_in['Wv'], 'L0_attn_bv': _L0_attn_in['bv'], 'L0_xattn_Wq': _L0_xattn_in['Wq'], 'L0_xattn_bq': _L0_xattn_in['bq'], 'L0_xattn_Wk': _L0_xattn_in['Wk'], 'L0_xattn_bk': _L0_xattn_in['bk'], 'L0_xattn_Wv': _L0_xattn_in['Wv'], 'L0_xattn_bv': _L0_xattn_in['bv'], 'L0_xattn_Wo': _L0_xattn_in['Wo'], 'L0_xattn_bo': _L0_xattn_in['bo'], 'L0_ffn_w_gate': _L0_ffn_in['w_gate'], 'L0_ffn_w_up': _L0_ffn_in['w_up'], 'L0_ffn_w_down': _L0_ffn_in['w_down'], 'L1_attn_W_proj': _L1_attn_in['W_proj'], 'L1_attn_pre_metric_nkk': _L1_attn_in['pre_metric_nkk'], 'L1_attn_transforms_nkk': _L1_attn_in['transforms_nkk'], 'L1_attn_W_mixer': _L1_attn_in['W_mixer'], 'L1_xattn_g_norm': _L1_xattn_in['g_norm'], 'L1_xattn_null_kv': _L1_xattn_in['null_kv'], 'L1_xattn_Wq': _L1_xattn_in['Wq'], 'L1_xattn_Wkv': _L1_xattn_in['Wkv'], 'L1_xattn_q_scale': _L1_xattn_in['q_scale'], 'L1_xattn_k_scale': _L1_xattn_in['k_scale'], 'L1_xattn_Wout': _L1_xattn_in['Wout'], 'L1_xattn_g_out': _L1_xattn_in['g_out'], 'L1_ffn_w_freq_real': _L1_ffn_in['w_freq_real'], 'L1_ffn_w_freq_imag': _L1_ffn_in['w_freq_imag'], 'L1_ffn_bias': _L1_ffn_in['bias']}

def reference(x, ctx_1024, L0_attn_Wq, L0_attn_bq, L0_attn_Wk, L0_attn_bk, L0_attn_Wv, L0_attn_bv, L0_xattn_Wq, L0_xattn_bq, L0_xattn_Wk, L0_xattn_bk, L0_xattn_Wv, L0_xattn_bv, L0_xattn_Wo, L0_xattn_bo, L0_ffn_w_gate, L0_ffn_w_up, L0_ffn_w_down, L1_attn_W_proj, L1_attn_pre_metric_nkk, L1_attn_transforms_nkk, L1_attn_W_mixer, L1_xattn_g_norm, L1_xattn_null_kv, L1_xattn_Wq, L1_xattn_Wkv, L1_xattn_q_scale, L1_xattn_k_scale, L1_xattn_Wout, L1_xattn_g_out, L1_ffn_w_freq_real, L1_ffn_w_freq_imag, L1_ffn_bias):
    import jax
    import jax.numpy as jnp

    def _L0_attn_ref(x, Wq, bq, Wk, bk, Wv, bv):
        import jax, jax.numpy as jnp
        import numpy as np
        EPS = 1e-06

        def _feature_map(x):
            return jax.nn.elu(x) + 1.0
        B, L, C = x.shape
        H = 8
        D = C // H
        q = x @ Wq + bq
        k = x @ Wk + bk
        v = x @ Wv + bv
        q = q.reshape(B, L, H, D)
        k = k.reshape(B, L, H, D)
        v = v.reshape(B, L, H, D)
        Q = _feature_map(q)
        K = _feature_map(k)
        v_len = jnp.asarray(L, v.dtype)
        v_scaled = v / v_len
        KV = jnp.einsum('nshd,nshv->nhdv', K, v_scaled)
        Z = 1.0 / (jnp.einsum('nlhd,nhd->nlh', Q, K.sum(axis=1)) + EPS)
        out = jnp.einsum('nlhd,nhdv,nlh->nlhv', Q, KV, Z) * v_len
        return out.reshape(B, L, C)

    def _L0_xattn_ref(query, key, value, Wq, bq, Wk, bk, Wv, bv, Wo, bo):
        import jax, jax.numpy as jnp
        import numpy as np
        HEADS = 16
        EMBED = 256
        HEAD_DIM = EMBED // HEADS
        B, Sq, E = query.shape
        Sk = key.shape[1]
        H, D = (HEADS, HEAD_DIM)
        q = (query @ Wq.T + bq).reshape(B, Sq, H, D)
        k = (key @ Wk.T + bk).reshape(B, Sk, H, D)
        v = (value @ Wv.T + bv).reshape(B, Sk, H, D)
        scores = jnp.einsum('bqhd,bkhd->bhqk', q, k) / np.sqrt(D).astype(jnp.float32)
        attn = jax.nn.softmax(scores, axis=-1)
        out = jnp.einsum('bhqk,bkhd->bqhd', attn, v).reshape(B, Sq, E)
        return out @ Wo.T + bo

    def _L0_ffn_ref(x, w_gate, w_up, w_down):
        import jax, jax.numpy as jnp
        import numpy as np
        BLOCK = 32
        W_BITS = 4
        ACT_BITS = 16

        def act_qdq(x):
            qmax = 2.0 ** (ACT_BITS - 1) - 1.0
            scale = jnp.maximum(jnp.max(jnp.abs(x)) / qmax, 1e-12)
            return jnp.clip(jnp.round(x / scale), -qmax - 1.0, qmax) * scale

        def fixed_qdq_u16(x):
            scale = 1.0 / 65536.0
            return jnp.clip(jnp.round(x / scale), 0.0, 65535.0) * scale

        def lpbq_dequant(w):
            O, I = w.shape
            qmax = 2.0 ** (W_BITS - 1) - 1.0
            wb = w.reshape(O, I // BLOCK, BLOCK)
            s = jnp.maximum(jnp.max(jnp.abs(wb), axis=-1, keepdims=True) / qmax, 1e-12)
            wq = jnp.clip(jnp.round(wb / s), -qmax - 1.0, qmax) * s
            return wq.reshape(O, I)
        x = act_qdq(x)
        up = act_qdq(x @ lpbq_dequant(w_up).T)
        gate = act_qdq(x @ lpbq_dequant(w_gate).T)
        sig = fixed_qdq_u16(jax.nn.sigmoid(gate))
        gate = act_qdq(gate * sig)
        o = act_qdq(gate * up)
        return o @ lpbq_dequant(w_down).T

    def _L1_attn_ref(in_sequence_bwc, W_proj, pre_metric_nkk, transforms_nkk, W_mixer):
        import jax, jax.numpy as jnp
        import numpy as np
        import math
        B, W, C, N = (4, 512, 256, 16)
        K = C // N
        b, w, c = in_sequence_bwc.shape
        metric_nkk = jnp.einsum('nij,nkj->nik', pre_metric_nkk, pre_metric_nkk)
        proj_bwc = in_sequence_bwc @ W_proj.T
        proj_bnwk = proj_bwc.reshape(b, w, N, K).transpose(0, 2, 1, 3)
        qm_bnwk = jnp.einsum('bnwk,nkj->bnwj', proj_bnwk, metric_nkk)
        scores_bnww = jnp.einsum('bnwk,bnvk->bnwv', qm_bnwk, proj_bnwk) / math.sqrt(K)
        mask_ww = jnp.tril(jnp.ones((w, w), dtype=scores_bnww.dtype))
        scores_bnww = scores_bnww * mask_ww
        nudged_bnwk = jnp.einsum('bnwv,bnvk->bnwk', scores_bnww, proj_bnwk)
        nudged_bnwk = jnp.einsum('bnwk,nkj->bnwj', nudged_bnwk, transforms_nkk)
        nudged_bwc = nudged_bnwk.transpose(0, 2, 1, 3).reshape(b, w, c)
        return nudged_bwc @ W_mixer.T

    def _L1_xattn_ref(x, context, g_norm, null_kv, Wq, Wkv, q_scale, k_scale, Wout, g_out):
        import jax, jax.numpy as jnp
        import numpy as np
        B, N, M = (4, 512, 512)
        DIM = 256
        HEADS = 16
        DIM_HEAD = 64
        INNER = HEADS * DIM_HEAD
        SCALE = 8.0

        def layer_norm(x, g, eps=1e-05):
            mean = jnp.mean(x, axis=-1, keepdims=True)
            var = jnp.mean((x - mean) ** 2, axis=-1, keepdims=True)
            return (x - mean) * jax.lax.rsqrt(var + eps) * g

        def l2norm(t, eps=1e-12):
            n = jnp.maximum(jnp.linalg.norm(t, axis=-1, keepdims=True), eps)
            return t / n
        b = x.shape[0]
        xn = layer_norm(x, g_norm)
        ctx = context
        q = xn @ Wq
        kv = ctx @ Wkv
        k, v = jnp.split(kv, 2, axis=-1)
        split_heads = lambda t: t.reshape(b, t.shape[1], HEADS, DIM_HEAD).transpose(0, 2, 1, 3)
        q, k, v = map(split_heads, (q, k, v))
        nk = jnp.broadcast_to(null_kv[0], (b, HEADS, 1, DIM_HEAD))
        nv = jnp.broadcast_to(null_kv[1], (b, HEADS, 1, DIM_HEAD))
        k = jnp.concatenate([nk, k], axis=2)
        v = jnp.concatenate([nv, v], axis=2)
        q = l2norm(q) * q_scale
        k = l2norm(k) * k_scale
        sim = jnp.einsum('bhid,bhjd->bhij', q, k) * SCALE
        attn = jax.nn.softmax(sim.astype(jnp.float32), axis=-1).astype(sim.dtype)
        out = jnp.einsum('bhij,bhjd->bhid', attn, v)
        out = out.transpose(0, 2, 1, 3).reshape(b, -1, INNER)
        out = out @ Wout
        return layer_norm(out, g_out)

    def _L1_ffn_ref(x, w_freq_real, w_freq_imag, bias):
        import jax, jax.numpy as jnp
        import numpy as np
        B, N, D = (4, 512, 256)
        SPARSITY = 0.01
        w = jax.lax.complex(w_freq_real, w_freq_imag)
        x_freq = jnp.fft.fft(x, axis=-1)
        y_freq = jnp.einsum('bnd,do->bno', x_freq, w)
        y = jnp.real(jnp.fft.ifft(y_freq, axis=-1))
        return y + bias
    x = _layernorm(x + _L0_attn_ref(x, L0_attn_Wq, L0_attn_bq, L0_attn_Wk, L0_attn_bk, L0_attn_Wv, L0_attn_bv), axis=-1)
    x = _layernorm(x + _L0_xattn_ref(x, ctx_1024, ctx_1024, L0_xattn_Wq, L0_xattn_bq, L0_xattn_Wk, L0_xattn_bk, L0_xattn_Wv, L0_xattn_bv, L0_xattn_Wo, L0_xattn_bo), axis=-1)
    x = _layernorm(x + _L0_ffn_ref(x, L0_ffn_w_gate, L0_ffn_w_up, L0_ffn_w_down), axis=-1)
    x = _layernorm(x + _L1_attn_ref(x, L1_attn_W_proj, L1_attn_pre_metric_nkk, L1_attn_transforms_nkk, L1_attn_W_mixer), axis=-1)
    x = _layernorm(x + _L1_xattn_ref(x, ctx_1024, L1_xattn_g_norm, L1_xattn_null_kv, L1_xattn_Wq, L1_xattn_Wkv, L1_xattn_q_scale, L1_xattn_k_scale, L1_xattn_Wout, L1_xattn_g_out), axis=-1)
    x = _layernorm(x + _L1_ffn_ref(x, L1_ffn_w_freq_real, L1_ffn_w_freq_imag, L1_ffn_bias), axis=-1)
    return x

_drawn_inputs = setup_inputs


def setup_inputs(seed=0):
    import zlib

    import numpy as np

    out = dict(_drawn_inputs(seed))
    spreads = {'L0_attn_bq': (0.0, 2.0),
     'L0_attn_bk': (0.0, 2.0),
     'L0_attn_bv': (0.0, 0.1),
     'L1_xattn_g_norm': (1.0, 0.2),
     'L1_xattn_q_scale': (1.0, 0.2),
     'L1_xattn_k_scale': (1.0, 0.2),
     'L1_xattn_g_out': (1.0, 0.2)}
    factors = {'L0_attn_Wq': 106.31,
     'L0_attn_Wk': 58.615,
     'L0_xattn_bq': 5.538,
     'L0_xattn_bk': 200.0,
     'L1_ffn_bias': 7.032}
    for name, (base, spread) in spreads.items():
        noise = np.random.default_rng([zlib.crc32(name.encode()), seed]).standard_normal(out[name].shape)
        drawn = base * np.exp(spread * noise) if base else spread * noise
        out[name] = jnp.asarray(drawn.astype(out[name].dtype))
    for name, factor in factors.items():
        out[name] = (out[name] * factor).astype(out[name].dtype)
    return out
```

```python
import numpy as np
import concourse.bass as bass
from concourse import mybir
from contextlib import ExitStack

F32 = mybir.dt.float32
I16 = mybir.dt.int16
U16 = mybir.dt.uint16
ALU = mybir.AluOpType
ACT = mybir.ActivationFunctionType
AX = mybir.AxisListType

P = 128
B, T, C = 8, 512, 256
NT = T // P
NC = C // P
TC = 64
LH, LD = 8, 32
H = 16
HD = C // H
GH = P // HD
FF = 768
NF = FF // P
BLK = 32
CD = 64
INNER = H * CD
NP = H // 2
EPS = 1e-5
QMAX = 32767.0
MAGIC = 12582912.0


class Batch:

    def __init__(self, off, reg=None):
        self.off, self.reg = off, reg

    def lin(self, k, c):
        return k * self.off + c if self.reg is None else self.reg * (2 * k) + (k * self.off + c)

    def half(self, k, c):
        return (k * (self.off // 2) + c if self.reg is None
                else self.reg * k + (k * (self.off // 2) + c))

    def before(self, n):
        return self.reg is None and self.off < n

    def first(self):
        return self.reg is None and self.off == 0

    def last(self):
        return self.reg is None and self.off == B - 1


class Signal:

    def __init__(self, sem, per, base=0):
        self.sem, self.per, self.base = sem, per, base

    def at(self, b, j):
        return b.lin(self.per, self.base + j)


CONTINUES = {
    "ffn_x_turned": "lin_x_turned", "ffn_x_copied": "lin_x_copied",
    "dn_turned": "lin_y_turned", "dn_copied": "lin_y_copied", "y3_ready": "y1_ready", "y5_ready": "y2_ready",
    "met_q_done": "lin_q_projected", "met_q_ready": "lin_q_ready", "met_state_done": "lin_state_done",
    "met_states_ready": "lin_kv_ready", "met_added": "lin_added", "met_stats": "lin_stats",
    "met_rstd": "lin_rstd", "met_projected": "xat_q_projected", "met_p_ready": "xat_q_biased",
    "dn_projected": "lin_kv_projected", "dn_v_scaled": "lin_kv_biased", "dn_v_rounded": "lin_scaled",
    "cos_scored": "xat_scored", "cos_shifted": "xat_shifted", "cos_exp_done": "xat_exp_done",
    "cos_turned": "xat_probs_turned", "cos_pt_copied": "xat_probs_copied",
    "cos_out_done": "xat_weighted", "cos_o_copied": "xat_normed", "spec_done": "xat_out_projected",
    "spec_added": "xat_out_added", "cos_stats": "xat_stats", "cos_rstd": "xat_rstd",
    "y_stored": "x3_stored", "ffn_peaked": "lin_q_negative",
    "sigmoid_done": "lin_q_exp", "up_rounded": "lin_k_ready", "ffn_x_scaled": "lin_k_exp",
    "cos_x_turned": "xat_o_turned", "cos_x_copied": "xat_o_copied", "cos_probs_ready": "lin_out_done",
}
MOVES_ON = {"ffn_x_loaded": ("x_loaded", 1), "up_loaded": ("x_loaded", 2), "dn_x_loaded": ("x_loaded", 3),
            "up_stored": ("ck_stored", 1), "v_stored": ("ck_stored", 2)}


class Chain:

    def __init__(self, eng, sem, per, after=None):
        self.eng, self.per = eng, per
        self.base = after.base + B * after.per if after else 0
        self.sem = after.sem if after else sem

    def begin(self, b):
        self.b, self.j = b, 0

    def link(self, ins):
        self.j += 1
        ins.then_inc(self.sem, 1)
        self.eng.wait_ge(self.sem, self.b.lin(self.per, self.base + self.j))

    def end(self):
        assert self.j == self.per, (self.sem, self.j, self.per)


def pipeline(eng, steps):
    last = max(s for s, _ in steps)
    first = last + last % 2 if last > 1 else 2

    def peeled(n):
        for skew, fn in steps:
            if 0 <= n - skew < B:
                fn(Batch(n - skew), (n - skew) % 2)

    for n in range(first):
        peeled(n)
    with eng.Fori(first // 2, B // 2) as i:
        for half in range(2):
            for skew, fn in steps:
                fn(Batch(half - skew, i), (half - skew) % 2)
    for n in range(B, B + last):
        peeled(n)


class Arena:

    def __init__(self, tensor, words):
        self.t, self.words, self.at, self.top = tensor, words, 0, 0

    def take(self, *dims, dtype=F32):
        n = int(np.prod(dims))
        words = n if dtype == F32 else (n + 1) // 2
        a = self.t[:, self.at:self.at + words]
        self.at += words
        self.top = max(self.top, self.at)
        assert self.at <= self.words, (self.at, self.words)
        if dtype != F32:
            a = a.bitcast(dtype)
        names = "abcdef"[:len(dims)]
        if len(dims) > 1:
            kw = {x: d for x, d in zip(names, dims)}
            a = a.rearrange(f"p ({' '.join(names)}) -> p {' '.join(names)}", **kw)
        return a


PACK_IDENT = [("ident", (P,)), ("ones", (P,))]
PACK_LIN = [("lin_wq", (NC, C)), ("lin_wkv", (NC, 2 * C)), ("lin_bq", (NC,)), ("lin_bkv", (2 * C,)),
            ("xat_wq", (NC, C)), ("xat_bq", (NC,)), ("xat_wo", (NC, C)), ("xat_bo", (C,)),
            ("blk32", (P,))]
PACK_CTX = [("ctx", (B * TC // P, C)), ("xat_wk", (NC, C)), ("xat_bk", (NC,)), ("xat_wv", (NC, C)),
            ("xat_bv", (C,)), ("head16", (GH,)), ("pair16", (2 * HD + 2,)),
            ("cos_wk", (NC, INNER)), ("cos_wv", (NC, INNER)), ("q_scale", (1,)), ("k_scale", (1,)),
            ("blk64", (P,)),
            ("null_row", (CD,)), ("q_row", (CD,)), ("k_row", (CD,))]
PACK_FFN = [("w_up", (NF, C)), ("w_gate", (NF, C)), ("w_down", (NC, FF))]
PACK_L1 = [("met_wp", (NC, C)), ("cos_wq", (NC, INNER)), ("cos_gn", (NC,)), ("cos_wo", (NP, C)),
           ("cos_go", (C,)), ("half64", (2,)), ("blk16", (P,)), ("causal", (P,)), ("spec_b", (C,)),
           ("mhead16", (GH,))]
PACK_PREP = [("met_pt", (NC, P)), ("met_tt", (NC, P)), ("met_wm", (NC, C)), ("null_v", (NP, H)),
             ("dft_r", (NC, C)), ("dft_i", (NC, C)), ("dft_ni", (NC, C)),
             ("spec_wr", (NC, C)), ("spec_wi", (NC, C))]
PACKS = {"pack_ident": PACK_IDENT, "pack_lin": PACK_LIN, "pack_ctx": PACK_CTX, "pack_ffn": PACK_FFN,
         "pack_l1": PACK_L1, "pack_prep": PACK_PREP}


def width(pack):
    return sum(int(np.prod(d)) for _, d in pack)


def decoder(nc, x_in, pack_ident, pack_lin, pack_ctx, pack_ffn, pack_l1, pack_prep, out):
    packs_in = dict(pack_ident=pack_ident, pack_lin=pack_lin, pack_ctx=pack_ctx, pack_ffn=pack_ffn,
                    pack_l1=pack_l1, pack_prep=pack_prep)
    x_rows = x_in.rearrange("b (t p) c -> b p t c", p=P)
    out_rows = out.rearrange("b (t p) c -> b p t c", p=P)
    ctx = ExitStack()
    with ctx:
        def sem(name):
            return ctx.enter_context(nc.semaphore(name))

        x3_d = nc.dram_tensor("x3_scratch", (B, P, NT * C), F32).ap()
        up_d = nc.dram_tensor("up_scratch", (B, P, NF * T), F32).ap()
        v_d = nc.dram_tensor("v_scratch", (B, NT * P, NF * P), F32).ap()
        ck_d = nc.dram_tensor("ck_scratch", (P, NP, B * TC), F32).ap()
        cv_d = nc.dram_tensor("cv_scratch", (P, NP, B * TC), F32).ap()

        WORDS = 52900
        arena_t = ctx.enter_context(nc.sbuf_tensor("arena", [P, WORDS], F32))
        ar = Arena(arena_t, WORDS)
        ps = ctx.enter_context(nc.psum_tensor("ps", [P, 8, 512], F32))

        def take_pack(pack):
            base = ar.at
            views = {n: ar.take(*d) for n, d in pack}
            return arena_t[:, base:ar.at], views

        def bank(k, n=1):
            return ps[:, k:k + n, :]

        ident_all, w = take_pack(PACK_IDENT)
        ident = w["ident"]
        small = ar.take(64)
        quant = {n: small[:, k:k + 1] for k, n in enumerate(
            ["tmp", "x_max", "up_max", "gate_max", "t_max", "v_max", "floor",
             "x_all", "up_all", "gate_all", "t_all", "v_all",
             "x_scale", "up_scale", "gate_scale", "t_scale", "v_scale",
             "x_mult", "up_mult", "gate_mult", "t_mult", "v_mult", "t_raw", "v_raw"])}
        peaks = small[:, 32:34]
        neghalf = ar.take(64)
        spare = ar.take(1)
        wup_t = ar.take(NC, FF)
        wgate_t = ar.take(NC, FF)
        wdown_t = ar.take(NF, C)
        l1_all, w1 = take_pack(PACK_L1)
        w.update(w1)
        met_m = ar.take(NC, P)
        met_wo = ar.take(NC, C)
        spec_m = ar.take(NC, C)
        null_w = ar.take(C)
        null_wq = ar.take(NC, H)
        keep = ar.at

        kbd = ar.take(NC, B, GH, TC)
        vbd = ar.take(B, NP, 2 * HD + 2)
        lin_all, w2 = take_pack(PACK_LIN)
        w.update(w2)
        loop1 = ar.at
        ctx_all, w3 = take_pack(PACK_CTX)
        w.update(w3)
        prep_all, w4 = take_pack(PACK_PREP)
        w.update(w4)
        ffn_all, w5 = take_pack(PACK_FFN)
        w.update(w5)
        ctx_t = ar.take(NC, B, TC)
        ctx_t2 = ar.take(NC, B, 2, TC)
        kt = ar.take(NC, B, TC)
        vst = kt.rearrange("p a b c -> p a (b c)")
        kraw = ar.take(2, B * TC)
        ksq = ar.take(2, B * TC)
        krn = ar.take(2, B * TC)
        kst = ar.take(2, B * TC)
        qmag = ar.take(NF * C // BLK)
        qrec = ar.take(NF * C // BLK)
        vtmp = ar.take(B, C)
        wq = vtmp.rearrange("p a b -> p (a b)")[:, 0:NF * C]
        at_r = ar.take(NC, C)
        at_i = ar.take(NC, C)
        gk = ar.take(1)
        null_k = ar.take(CD)
        null_n = ar.take(1)
        null_p = vtmp.rearrange("p a b -> p (a b)")[:, 0:INNER].rearrange("p (h k) -> p h k", h=H)
        ar.at = loop1
        lin_x = ar.take(2, NT, C)
        lin_xt = ar.take(2, NC, T)
        lin_zq = ar.take(NC, T)
        lin_eq = ar.take(NC, T)
        lin_q = ar.take(NC, T)
        lin_z = ar.take(NT, 2 * C)
        lin_ek = ar.take(NT, C)
        lin_k = ar.take(NT, C)
        lin_kv = ar.take(NC, P + P // LD)
        lin_den = ar.take(2, NC, P // LD)
        lin_r = ar.take(NT, C)
        y1 = ar.take(2, NT, C)
        xt1 = ar.take(NC, T)
        xat_q = ar.take(NC, T)
        xat_s = ar.take(2, H, TC)
        xat_mx = ar.take(2, H)
        xat_pt = ar.take(NP, P)
        xat_rec = ar.take(H)
        xat_o = ar.take(NT, C)
        xat_ot = ar.take(NC, T)
        xat_r = ar.take(NT, C)
        y2 = ar.take(2, NT, C)
        lin_st = ar.take(NT, 6)
        lin_mv = ar.take(NT, 2)
        lin_rs = ar.take(NT)
        xat_st = ar.take(NT, 6)
        xat_mv = ar.take(NT, 2)
        xat_rs = ar.take(NT)


        ar.at = keep
        gated = ar.take(B, NT * NF * P)
        passes = ar.at
        ffn_x = ar.take(2, NT, C)
        ffn_xt = ar.take(2, NC, T)
        ffn_up = ar.take(2, NT, NF, P)
        ar.at = passes
        gate_i = ar.take(2, NF * T, dtype=I16)
        sig_f = ar.take(2, NF * T)
        sig_i = ar.take(2, NF * T, dtype=U16)
        ar.at = passes
        up_f = ar.take(2, NF * T)
        v_f = ar.take(2, NF * T)
        up_i = ar.take(NF * T, dtype=I16)
        t_i = ar.take(NF * T, dtype=I16)
        ar.at = keep
        dn_v = ar.take(2, NF, P)
        dn_x = ar.take(2, NT, C)
        y3 = ar.take(2, NT, C)
        xt3 = ar.take(NC, T)
        met_p = ar.take(NC, T)
        met_pr = ar.take(NT, C)
        met_q = ar.take(NC, T)
        met_qh = ar.take(GH, T)
        met_st = ar.take(NC, NT - 1, P)
        met_s = ar.take(2, 4, P)
        met_o = ar.take(NT, C)
        met_ot = ar.take(NC, T)
        met_r = ar.take(NT, C)
        y4 = ar.take(2, NT, C)
        xn4 = met_r
        xt4 = ar.take(NC, T)
        cos_kb = ar.take(2, NP, P)
        cos_vb = ar.take(2, NP, P)
        cos_vw = ar.take(NP, C)
        cos_q = ar.take(NP, T)
        cos_sq = ar.take(2, T)
        cos_nn = ar.take(NT, 2 * H)
        cos_s = ar.take(2, H * TC + H)
        cos_mx = ar.take(2, H)
        cos_pt = ar.take(NP, P)
        cos_p0 = ar.take(P)
        cos_o = ar.take(NT, C)
        cos_r = spec_r = cos_o
        y5 = ar.take(NT, C)
        xt5 = ar.take(NC, T)
        y6 = ar.take(NT, C)
        norms = {n: (ar.take(NT, 6), ar.take(NT, 2), ar.take(NT)) for n in
                 ("dn", "met", "met2", "cos_o", "cos", "spec")}
        sems = {}

        def ev(name):
            if name not in sems:
                sems[name] = sem(name)
            return sems[name]

        loaded = {n: sem(f"{n}_loaded") for n in PACKS}
        sigs = {}

        def sig(name, per=1):
            if name not in sigs:
                if name in CONTINUES:
                    before = sig(CONTINUES[name], per)
                    sigs[name] = Signal(before.sem, per, before.base + B * per)
                else:
                    sigs[name] = Signal(sem(name), per)
            assert sigs[name].per == per, name
            return sigs[name]

        def wait(eng, name, b, j=None, per=1):
            s = sig(name, per)
            eng.wait_ge(s.sem, s.at(b, per if j is None else j))

        def wait_previous(eng, name, b, per=1):
            if not b.first():
                eng.wait_ge(sig(name, per).sem, sig(name, per).at(b, 0))

        QUANTIZED = {n: k + 1 for k, n in enumerate(("x", "up", "gate", "t", "v"))}
        WEIGHTS = {n: k + 1 for k, n in enumerate(("w_up", "w_gate", "w_down"))}

        def moved(name, par):
            return ev(f"{MOVES_ON.get(name, (name, 0))[0]}_{par}")

        def moved_before(name):
            return 16 * (B // 2) * MOVES_ON.get(name, (name, 0))[1]

        def wait_moved(eng, name, b, par, back=0):
            if not b.before(back):
                eng.wait_ge(moved(name, par), b.half(16, moved_before(name) + 16 - 8 * back))

        def wait_all_moved(eng, name):
            for par in range(2):
                eng.wait_ge(moved(name, par), moved_before(name) + 16 * (B // 2))

        def wait_back(eng, name, b, back, per=1):
            if not b.before(back):
                eng.wait_ge(sig(name, per).sem, sig(name, per).at(b, per * (1 - back)))

        def wait_next(eng, name, b, j=1, per=1):
            if not b.last():
                eng.wait_ge(sig(name, per).sem, sig(name, per).at(b, per + j))

        def at_tile(name, b, t):
            return b.lin(8 * NT, 16 * (t // 2 + 1))

        def at_batch(ap, b):
            return ap[b.off] if b.reg is None else ap[bass.ds(b.lin(1, 0), 1)].squeeze(0)

        def at_cols(ap, b):
            return ap[:, b.off] if b.reg is None else ap[:, bass.ds(b.lin(1, 0), 1)].squeeze(1)

        block = ctx.enter_context(nc.Block())

        class Line:

            def __init__(self, eng, name):
                self.eng, self.sem, self.n = eng, sem(name), 0

            def link(self, ins):
                self.n += 1
                ins.then_inc(self.sem, 1)
                self.eng.wait_ge(self.sem, self.n)

        def rows2(k, n=2):
            return bank(k, n).rearrange("p a (b c) -> p (a b) c", c=C)

        def flat(k, n=1):
            return bank(k, n).rearrange("p a c -> p (a c)")

        @block.sync
        def _(sp):
            sp.dma_start(ident_all, pack_ident).then_inc(loaded["pack_ident"], 16)
            sp.dma_start(ctx_all, pack_ctx).then_inc(loaded["pack_ctx"], 16)
            sp.dma_start(lin_all, pack_lin).then_inc(loaded["pack_lin"], 16)
            sp.dma_start(prep_all, pack_prep).then_inc(loaded["pack_prep"], 16)
            for p in range(NP):
                sp.wait_ge(ev("cos_k_scaled"), p + 1)
                sp.dma_start(ck_d[:, p, :], kst[:, p % 2, :]).then_inc(moved("ck_stored", p % 2), 16)

            sp.wait_ge(ev("prep_done"), 3)
            wait_all_moved(sp, "ck_stored")
            wait_all_moved(sp, "cv_stored")

            def load_x(b, par):
                wait_back(sp, "y1_ready", b, 2)
                sp.dma_start(lin_x[:, par], at_batch(x_rows, b)).then_inc(moved("x_loaded", par), 16)

            def store_x3(b, par):
                wait(sp, "y2_ready", b)
                sp.dma_start(at_batch(x3_d, b), y2[:, par]).then_inc(sig("x3_stored", 16).sem, 16)

            pipeline(sp, [(0, load_x), (1, store_x3)])
            sp.wait_ge(sig("x3_stored", 16).sem, 16 * B)

            sp.wait_ge(ev("scale_ready"), QUANTIZED["x"])

            def ffn_load_x(b, par):
                wait_back(sp, "ffn_x_turned", b, 2)
                sp.dma_start(ffn_x[:, par].rearrange("p a b -> p (a b)"), at_batch(x3_d, b))\
                    .then_inc(moved("ffn_x_loaded", par), 16)

            def ffn_store_up(b, par):
                wait(sp, "up_copied", b, NF, NF)
                sp.dma_start(at_batch(up_d, b), ffn_up[:, par].rearrange("p a b c -> p (a b c)"))\
                    .then_inc(moved("up_stored", par), 16)

            pipeline(sp, [(0, ffn_load_x), (1, ffn_store_up)])
            wait_all_moved(sp, "up_stored")
            sp.wait_ge(ev("scale_ready"), QUANTIZED["t"])

            def ffn_load_up(b, par):
                wait_back(sp, "up_rounded", b, 2)
                sp.dma_start(up_f[:, par], at_batch(up_d, b)).then_inc(moved("up_loaded", par), 16)

            v_rows = v_d.rearrange("b (t p) n -> b p t n", t=NT)

            def ffn_store_v(b, par):
                wait(sp, "v_ready", b)
                sp.dma_start(at_batch(v_rows, b), v_f[:, par].rearrange("p (t n) -> p t n", t=NT)).then_inc(moved("v_stored", par), 16)

            pipeline(sp, [(0, ffn_load_up), (1, ffn_store_v)])
            wait_all_moved(sp, "v_stored")

            sp.wait_ge(ev("scale_ready"), QUANTIZED["v"])
            sp.wait_ge(ev("pads_cleared"), 2)

            v_tiles = v_d.rearrange("b (t p) n -> (b t) p n", t=NT)

            def dn_load(b, par):
                tiles = [b.lin(NT, t) if b.reg is None else sp.snap(b.lin(NT, t)) for t in range(NT)]
                wait_back(sp, "y3_ready", b, 2)
                sp.dma_start(dn_x[:, par].rearrange("p a b -> p (a b)"), at_batch(x3_d, b))\
                    .then_inc(moved("dn_x_loaded", par), 16)
                for t in range(NT):
                    if t >= 2:
                        wait(sp, "dn_projected", b, t - 1, NT)
                    else:
                        if not b.first():
                            sp.wait_ge(sig("dn_projected", NT).sem, sig("dn_projected", NT).at(b, t - 1))
                    sp.dma_start(dn_v[:, t % 2].rearrange("p a b -> p (a b)"), v_tiles[bass.ds(tiles[t], 1)].squeeze(0))\
                        .then_inc(moved("v_loaded", t % 2), 16)

            def cos_load(b, par):
                at = bass.ds(b.lin(TC, 0) if b.reg is None else sp.snap(b.lin(TC, 0)), TC)
                wait_back(sp, "cos_scored", b, 2, NT)
                for lo, hi in ((0, CD), (CD, P)):
                    sp.dma_start(cos_kb[lo:hi, par, :, lo:hi], ck_d[lo:hi, :, at])\
                        .then_inc(moved("cos_kv_loaded", par), 16)
                    sp.dma_start(cos_vb[lo:hi, par, :, lo:hi], cv_d[lo:hi, :, at])\
                        .then_inc(moved("cos_kv_loaded", par), 16)

            def store_y(b, par):
                wait(sp, "y6_ready", b)
                sp.dma_start(at_batch(out_rows, b), y6).then_inc(sig("y_stored", 16).sem, 16)

            pipeline(sp, [(2, cos_load), (0, dn_load), (3, store_y)])
            sp.wait_ge(sig("y_stored", 16).sem, 2 * 16 * B)

        @block.tensor
        def _(pe):
            mm = nc.tensor.matmul
            tr = nc.tensor.transpose

            pe.wait_ge(loaded["pack_ident"], 16)
            pe.wait_ge(loaded["pack_ctx"], 16)
            for c in range(NC):
                for t in range(NT):
                    last = tr(bank(c)[:, 0, t * P:(t + 1) * P], w["ctx"][:, t, c * P:(c + 1) * P], ident)
            last.then_inc(ev("ctx_transposed"), 1)
            pe.wait_ge(ev("ctx_t_ready"), 1)

            def from_ctx(out_ap, lhs, c0, n=P, rhs=None):
                for k in range(NC):
                    r = mm(out_ap, lhs[:, k, c0:c0 + n], ctx_t[:, k].rearrange("p a b -> p (a b)"),
                           start=k == 0, stop=k == NC - 1)
                return r

            for c in range(NC):
                last = from_ctx(flat(2 + c), w["xat_wk"], c * P)
            last.then_inc(ev("xat_k_projected"), 1)
            for p in range(NP + 1):
                if p < NP:
                    if p >= 2:
                        pe.wait_ge(ev("cos_k_squared"), p - 1)
                    from_ctx(flat(4 + p % 2), w["cos_wk"], p * P).then_inc(ev("cos_k_projected"), 1)
                if p >= 1:
                    pe.wait_ge(ev("cos_k_squared"), p)
                    if p >= 3:
                        pe.wait_ge(ev("cos_k_floored"), p - 2)
                    mm(flat(6 + (p - 1) % 2), w["blk64"], ksq[:, (p - 1) % 2, :], start=True,
                       stop=True).then_inc(ev("cos_k_normed"), 1)
            for p in range(NP):
                if p >= 2:
                    pe.wait_ge(ev("cos_v_copied"), p - 1)
                from_ctx(flat(p % 2), w["cos_wv"], p * P).then_inc(ev("cos_v_projected"), 1)
            pe.wait_ge(ev("ctx_t2_ready"), NC)
            pe.wait_ge(ev("cos_k_floored"), NP)
            for b in range(B):
                for k in range(NC):
                    last = mm(rows2(4, 4)[:, b, :], ctx_t2[:, k, b].rearrange("p a b -> p (a b)"),
                              w["xat_wv"][:, k, :], start=k == 0, stop=k == NC - 1)
            last.then_inc(ev("xat_v_projected"), 1)
            pe.wait_ge(loaded["pack_prep"], 16)
            pe.wait_ge(loaded["pack_l1"], 16)
            pe.wait_ge(ev("xat_k_biased"), 1)
            for c in range(NC):
                mm(flat(3)[:, c * P:(c + 1) * P], w["met_pt"][:, c], w["met_pt"][:, c], start=True, stop=True)
            for p in range(NP):
                last = mm(flat(3)[0:H, C:2 * C], w["null_v"][:, p, :], w["cos_wo"][:, p, :],
                          start=p == 0, stop=p == NP - 1)
            last.then_inc(ev("metric_product"), 1)
            pe.wait_ge(ev("xat_v_biased"), 1)
            for c in range(NC):
                last = mm(rows2(7, 1)[:, c], w["met_tt"][:, c], w["met_wm"][:, c], start=True, stop=True)
            last.then_inc(ev("mixer_product"), 1)
            for o in range(NC):
                for n, (wt, dft) in enumerate((("spec_wr", "dft_r"), ("spec_wi", "dft_ni"))):
                    for k in range(NC):
                        mm(rows2(5, 1)[:, o], w[wt][:, k, o * P:(o + 1) * P], w[dft][:, k],
                           start=n == k == 0, stop=n == k == 1)
            for o in range(NC):
                for n, (wt, dft) in enumerate((("spec_wr", "dft_i"), ("spec_wi", "dft_r"))):
                    for k in range(NC):
                        last = mm(rows2(6, 1)[:, o], w[wt][:, k, o * P:(o + 1) * P], w[dft][:, k],
                                  start=n == k == 0, stop=n == k == 1)
            last.then_inc(ev("spec_forward"), 1)
            pe.wait_ge(ev("cos_v_copied"), NP)

            def turn(first, name, rows, cols):
                pe.wait_ge(ev("weight_quantized"), WEIGHTS[name])
                src = wq.rearrange("p (a b) -> p a b", a=rows)
                for k in range(cols):
                    for r in range(rows):
                        at = (k * rows + r) * P
                        last = tr(flat(first, 3)[:, at:at + P], src[:, r, k * P:(k + 1) * P], ident)
                last.then_inc(ev("weight_turned"), 1)

            turn(0, "w_up", NF, NC)
            pe.wait_ge(ev("weight_copied"), WEIGHTS["w_up"])
            turn(0, "w_gate", NF, NC)
            pe.wait_ge(ev("weight_copied"), WEIGHTS["w_gate"])
            turn(0, "w_down", NC, NF)
            pe.wait_ge(ev("spec_forward_copied"), 2)
            for i in range(NC):
                for n, at in enumerate((at_r, at_i)):
                    for k in range(NC):
                        last = mm(rows2(4, 1)[:, i], at[:, k, i * P:(i + 1) * P],
                                  w[("dft_r", "dft_i")[n]][:, k], start=n == k == 0, stop=n == k == 1)
            last.then_inc(ev("spec_product"), 1)

            pe.wait_ge(ev("prep_done"), 3)
            pe.wait_ge(loaded["pack_lin"], 16)
            pe.wait_ge(ev("kbd_ready"), 1)

            def lin_turn_x(b, par):
                wait_moved(pe, "x_loaded", b, par)
                wait_previous(pe, "lin_y_copied", b)
                for c in range(NC):
                    for t in range(NT):
                        last = tr(flat(c)[:, t * P:(t + 1) * P], lin_x[:, par, t, c * P:(c + 1) * P], ident)
                last.then_inc(sig("lin_x_turned").sem, 1)

            def lin_project_q(b, par):
                wait(pe, "lin_x_copied", b)
                for c in range(NC):
                    for k in range(NC):
                        last = mm(flat(2 + c), w["lin_wq"][:, k, c * P:(c + 1) * P], lin_xt[:, par, k],
                                  start=k == 0, stop=k == NC - 1)
                last.then_inc(sig("lin_q_projected").sem, 1)

            def lin_project_kv(b, par):
                for t in range(NT):
                    if t >= 2:
                        wait(pe, "lin_kv_biased", b, t - 1, NT)
                    for k in range(NC):
                        last = mm(flat(t % 2), lin_xt[:, par, k, t * P:(t + 1) * P], w["lin_wkv"][:, k],
                                  start=k == 0, stop=k == NC - 1)
                    last.then_inc(sig("lin_kv_projected", NT).sem, 1)

            def lin_state(b, par):
                wait(pe, "lin_k_ready", b)
                wait(pe, "lin_q_biased", b)
                for c in range(NC):
                    for t in range(NT):
                        mm(flat(2)[:, c * P:(c + 1) * P], lin_k[:, t, c * P:(c + 1) * P],
                           lin_z[:, t, C + c * P:C + (c + 1) * P], start=t == 0, stop=t == NT - 1)
                for c in range(NC):
                    for t in range(NT):
                        last = mm(flat(2)[:, C + c:C + c + 1], lin_k[:, t, c * P:(c + 1) * P],
                                  w["ones"][:, 0:1], start=t == 0, stop=t == NT - 1)
                last.then_inc(sig("lin_state_done").sem, 1)

            def lin_out(b, par):
                wait(pe, "lin_kv_ready", b)
                wait(pe, "lin_q_ready", b)
                for t in range(NT):
                    for c in range(NC):
                        last = mm(flat((3, 0, 1, 2)[t])[:, c * 132:c * 132 + 132],
                                  lin_q[:, c, t * P:(t + 1) * P], lin_kv[:, c], start=True, stop=True)
                    last.then_inc(sig("lin_out_done", NT).sem, 1)

            def lin_turn_y(b, par):
                wait(pe, "y1_ready", b)
                for c in range(NC):
                    for t in range(NT):
                        last = tr(flat(c)[:, t * P:(t + 1) * P], y1[:, par, t, c * P:(c + 1) * P], ident)
                last.then_inc(sig("lin_y_turned").sem, 1)

            def xat_project_q(b, par):
                wait(pe, "lin_y_copied", b)
                wait_previous(pe, "xat_out_added", b)
                for c in range(NC):
                    for k in range(NC):
                        last = mm(flat(4 + c), w["xat_wq"][:, k, c * P:(c + 1) * P], xt1[:, k],
                                  start=k == 0, stop=k == NC - 1)
                last.then_inc(sig("xat_q_projected").sem, 1)

            def xat_scores(t):
                def step(b, par):
                    if t == 0:
                        wait(pe, "xat_q_biased", b)
                    else:
                        wait(pe, "xat_shifted", b, t, NT)
                    for c in range(NC):
                        keys = (kbd[:, c, bass.ds(b.lin(1, 0), 1)] if b.reg is not None
                                else kbd[:, c, b.off:b.off + 1])
                        last = mm(flat(4 + c), xat_q[:, c, t * P:(t + 1) * P],
                                  keys.rearrange("p o h k -> p (o h k)"), start=True, stop=True)
                    last.then_inc(sig("xat_scored", NT).sem, 1)
                return step

            def xat_turn_probs(t):
                def step(b, par):
                    wait(pe, "xat_exp_done", b, t + 1, NT)
                    if t > 0:
                        wait(pe, "xat_normed", b, t, NT)
                    else:
                        wait_previous(pe, "xat_o_copied", b)
                    for p in range(NP):
                        last = tr(flat(6, 2)[:, p * P:(p + 1) * P],
                                  xat_s[:, t % 2, 2 * p:2 * p + 2].rearrange("p a b -> p (a b)"), ident)
                    last.then_inc(sig("xat_probs_turned", NT).sem, 1)
                return step

            def xat_values(t):
                def step(b, par):
                    wait(pe, "xat_probs_copied", b, t + 1, NT)
                    for p in range(NP):
                        vals = (vbd[:, bass.ds(b.lin(1, 0), 1), p] if b.reg is not None
                                else vbd[:, b.off:b.off + 1, p])
                        last = mm(flat(6)[:, p * 34:p * 34 + 34], xat_pt[:, p],
                                  vals.rearrange("p o n -> p (o n)"), start=True, stop=True)
                    last.then_inc(sig("xat_weighted", NT).sem, 1)
                return step

            def xat_turn_o(b, par):
                wait(pe, "xat_normed", b, NT, NT)
                for c in range(NC):
                    for t in range(NT):
                        last = tr(flat(6 + c)[:, t * P:(t + 1) * P], xat_o[:, t, c * P:(c + 1) * P], ident)
                last.then_inc(sig("xat_o_turned").sem, 1)

            def xat_project_o(b, par):
                wait(pe, "xat_o_copied", b)
                for t in range(NT):
                    for k in range(NC):
                        last = mm(rows2(4)[:, t], xat_ot[:, k, t * P:(t + 1) * P], w["xat_wo"][:, k],
                                  start=k == 0, stop=k == NC - 1)
                last.then_inc(sig("xat_out_projected").sem, 1)

            pipeline(pe, [(0, lin_turn_x), (1, xat_project_q), (0, lin_project_q), (1, xat_scores(0)),
                          (0, lin_project_kv), (1, xat_scores(1)), (1, xat_turn_probs(0)),
                          (1, xat_scores(2)), (1, xat_values(0)), (1, xat_turn_probs(1)),
                          (1, xat_scores(3)), (1, xat_values(1)), (1, xat_turn_probs(2)),
                          (0, lin_state), (1, xat_values(2)), (1, xat_turn_probs(3)), (0, lin_out),
                          (1, xat_values(3)), (1, xat_turn_o), (1, xat_project_o), (0, lin_turn_y)])

            def ffn_turn_x(b, par):
                wait(pe, "ffn_x_rounded", b)
                wait_previous(pe, "ffn_x_copied", b)
                for c in range(NC):
                    for t in range(NT):
                        last = tr(flat(c)[:, t * P:(t + 1) * P], ffn_x[:, par, t, c * P:(c + 1) * P], ident)
                last.then_inc(sig("ffn_x_turned").sem, 1)

            def ffn_up_gate(b, par):
                wait(pe, "ffn_x_copied", b)
                for j in range(NF):
                    for g, (wt, done) in enumerate(((wup_t, "up"), (wgate_t, "gate"))):
                        if not (b.first() and j < 3):
                            wait(pe, done + "_copied", b, j - 2, NF)
                        for k in range(NC):
                            last = mm(flat(2 + (2 * j + g) % 6), wt[:, k, j * P:(j + 1) * P], ffn_xt[:, par, k],
                                      start=k == 0, stop=k == NC - 1)
                        last.then_inc(sig(done + "_done", NF).sem, 1)

            pipeline(pe, [(0, ffn_turn_x), (1, ffn_up_gate)])

            pe.wait_ge(ev("scale_ready"), QUANTIZED["v"])

            def turn_rows(first, rows, done):
                for c in range(NC):
                    for t in range(NT):
                        last = tr(flat(first + c)[:, t * P:(t + 1) * P], rows[:, t, c * P:(c + 1) * P], ident)
                last.then_inc(sig(done).sem, 1)

            def dn_project(b, par):
                wait_back(pe, "met_added", b, 2)
                wait_previous(pe, "dn_copied", b)
                for t in range(NT):
                    wait(pe, "dn_v_rounded", b, t + 1, NT)
                    for j in range(NF):
                        last = mm(rows2(5)[:, t], dn_v[:, t % 2, j], wdown_t[:, j], start=j == 0, stop=j == NF - 1)
                    last.then_inc(sig("dn_projected", NT).sem, 1)

            def dn_turn(b, par):
                wait(pe, "y3_ready", b)
                wait_previous(pe, "met_states_ready", b)
                turn_rows(5, y3[:, par], "dn_turned")

            def met_project(b, par):
                wait(pe, "dn_copied", b)
                wait_next(pe, "dn_added", b)
                for c in range(NC):
                    for k in range(NC):
                        last = mm(flat(5 + c), w["met_wp"][:, k, c * P:(c + 1) * P], xt3[:, k],
                                  start=k == 0, stop=k == NC - 1)
                last.then_inc(sig("met_projected").sem, 1)

            def met_turn_p(b, par):
                wait(pe, "met_p_ready", b)
                wait_previous(pe, "met_x_copied", b)
                for t in range(NT):
                    for c in range(NC):
                        last = tr(rows2(5)[:, t, c * P:(c + 1) * P], met_p[:, c, t * P:(t + 1) * P], ident)
                last.then_inc(sig("met_p_turned").sem, 1)

            def met_queries(b, par):
                wait(pe, "met_pr_ready", b)
                for c in range(NC):
                    last = mm(flat(5 + c), met_m[:, c], met_p[:, c], start=True, stop=True)
                last.then_inc(sig("met_q_done").sem, 1)

            def met_state(b, par):
                wait(pe, "met_q_ready", b)
                for c in range(NC):
                    for t in range(NT - 1):
                        rows = met_pr[:, t, c * P:(c + 1) * P]
                        last = mm(flat(5 + c)[:, t * P:(t + 1) * P], rows, rows, start=True, stop=True)
                last.then_inc(sig("met_state_done").sem, 1)

            def met_scores(n):
                c, t, half = n // 8, n // 2 % 4, n % 2

                def step(b, par):
                    if n == 0:
                        wait(pe, "met_states_ready", b)
                        wait_next(pe, "dn_copied", b)
                    if n % 8 == 0:
                        wait(pe, "met_qh_ready", b, c + 1, 2)
                    if n >= 2:
                        wait(pe, "met_masked", b, n - 1, 16)
                    mm(flat(5 + half), met_p[:, c, t * P:(t + 1) * P],
                       met_qh[:, 4 * half:4 * half + 4, t * P:(t + 1) * P], start=True, stop=True)\
                        .then_inc(sig("met_scored", 16).sem, 1)
                return step

            def met_out(n):
                c, t, half = n // 8, n // 2 % 4, n % 2

                def step(b, par):
                    if n == 8:
                        wait(pe, "met_o_copied", b, 1, 2)
                    if n == 0:
                        wait_previous(pe, "met_o_copied", b, 2)
                    o = flat(7)[:, t * P:(t + 1) * P]
                    if half == 0 and t > 0:
                        mm(o, met_q[:, c, t * P:(t + 1) * P], met_st[:, c, t - 1], start=True, stop=False,
                           skip_group_check=True)
                    wait(pe, "met_masked", b, n + 1, 16)
                    for i in range(4):
                        h = 4 * half + i
                        last = mm(o[:, h * HD:(h + 1) * HD], met_s[:, n % 2, i],
                                  met_pr[:, t, c * P + h * HD:c * P + (h + 1) * HD],
                                  start=t == 0 and h == 0, stop=h == GH - 1, skip_group_check=True)
                    last.then_inc(sig("met_weighted", 16).sem, 1)
                return step

            def met_turn_o(b, par):
                wait(pe, "met_o_copied", b, 2, 2)
                turn_rows(5, met_o, "met_o_turned")

            def met_mix(b, par):
                wait(pe, "met_ot_ready", b)
                for t in range(NT):
                    for k in range(NC):
                        last = mm(rows2(5)[:, t], met_ot[:, k, t * P:(t + 1) * P], met_wo[:, k],
                                  start=k == 0, stop=k == NC - 1)
                last.then_inc(sig("met_mixed").sem, 1)

            def met_turn_x(b, par):
                wait(pe, "xn4_ready", b)
                wait_next(pe, "met_p_ready", b)
                turn_rows(5, xn4, "met_x_turned")

            def cos_vw_half(n):
                def step(b, par):
                    if n == 0:
                        pe.wait_ge(moved("cos_kv_loaded", par), b.half(64, 64))
                        wait_previous(pe, "cos_pt_copied", b, NT)
                    else:
                        wait(pe, "cos_vw_copied", b, 1, 2)
                        wait_previous(pe, "cos_x_copied", b)
                    for i in range(4):
                        last = mm(rows2(2)[:, i], cos_vb[:, par, 4 * n + i], w["cos_wo"][:, 4 * n + i],
                                  start=True, stop=True)
                    last.then_inc(sig("cos_vw_done", 2).sem, 1)
                return step

            def cos_nulls(b, par):
                wait(pe, "met_x_copied", b)
                wait_previous(pe, "cos_o_copied", b, NT)
                for t in range(NT):
                    for k in range(NC):
                        mm(flat(4)[:, t * 32 + H:t * 32 + 2 * H], xt4[:, k, t * P:(t + 1) * P], null_wq[:, k],
                           start=k == 0, stop=k == NC - 1)

            def cos_query(p):
                def step(b, par):
                    if p == 0:
                        wait_previous(pe, "spec_added", b)
                    if 2 <= p < NP:
                        wait(pe, "cos_q_squared", b, p - 1, NP)
                    if p < NP:
                        for k in range(NC):
                            last = mm(flat(p % 2), w["cos_wq"][:, k, p * P:(p + 1) * P], xt4[:, k],
                                      start=k == 0, stop=k == NC - 1)
                        last.then_inc(sig("cos_q_done", NP).sem, 1)
                    if p >= 1:
                        q = p - 1
                        wait(pe, "cos_q_squared", b, p, NP)
                        for t in range(NT):
                            last = mm(flat(4)[:, t * 32 + 2 * q:t * 32 + 2 * q + 2],
                                      cos_sq[:, q % 2, t * P:(t + 1) * P], w["half64"], start=True, stop=True)
                        last.then_inc(sig("cos_q_normed", NP).sem, 1)
                return step

            def cos_scores(t):
                def step(b, par):
                    if t:
                        wait(pe, "cos_scaled", b, t, NT)
                    for p in range(NP):
                        last = mm(flat(0, 2)[:, p * P:(p + 1) * P], cos_q[:, p, t * P:(t + 1) * P],
                                  cos_kb[:, par, p], start=True, stop=True)
                    last.then_inc(sig("cos_scored", NT).sem, 1)
                return step

            def cos_turn(t):
                def step(b, par):
                    wait(pe, "cos_probs_ready", b, t + 1, NT)
                    if t == 0:
                        wait(pe, "cos_vw_copied", b, 2, 2)
                        wait(pe, "cos_floored", b)
                    else:
                        wait(pe, "cos_o_copied", b, t, NT)
                    for p in range(NP):
                        tr(flat(2, 2)[:, p * P:(p + 1) * P], cos_s[:, t % 2, p * P:(p + 1) * P], ident)
                    tr(flat(4)[0:H, 0:P], cos_s[:, t % 2, H * TC:], ident)\
                        .then_inc(sig("cos_turned", NT).sem, 1)
                return step

            def cos_out(t):
                def step(b, par):
                    wait(pe, "cos_pt_copied", b, t + 1, NT)
                    for p in range(NP):
                        mm(flat(4)[:, C:2 * C], cos_pt[:, p], cos_vw[:, p], start=p == 0, stop=False)
                    mm(flat(4)[:, C:2 * C], cos_p0[0:H], null_w[0:H], start=False, stop=True)\
                        .then_inc(sig("cos_out_done", NT).sem, 1)
                return step

            def cos_turn_x(b, par):
                wait(pe, "y5_ready", b)
                wait_next(pe, "cos_vw_copied", b, 1, 2)
                turn_rows(2, y5, "cos_x_turned")

            def spec_project(b, par):
                wait(pe, "cos_x_copied", b)
                for t in range(NT):
                    for k in range(NC):
                        last = mm(rows2(0)[:, t], xt5[:, k, t * P:(t + 1) * P], spec_m[:, k],
                                  start=k == 0, stop=k == NC - 1)
                last.then_inc(sig("spec_done").sem, 1)

            def quarter(lo):
                out_steps = []
                for n in range(lo, lo + 4):
                    out_steps.append((1, met_scores(n)))
                    if n:
                        out_steps.append((1, met_out(n - 1)))
                return out_steps

            pipeline(pe, [(2, cos_vw_half(0)), (0, dn_project), (3, cos_turn_x), (2, cos_vw_half(1)),
                          (3, spec_project), (1, met_project), (2, met_turn_x), (1, met_turn_p),
                          (2, cos_nulls), (2, cos_query(0)), (1, met_queries),
                          (2, cos_query(1)), (2, cos_query(2)), (1, met_state), (2, cos_query(3)),
                          (2, cos_query(4)), (0, dn_turn), *[(2, cos_query(p)) for p in range(5, NP + 1)],
                          (2, cos_scores(0)), *quarter(0)[:2], (2, cos_scores(1)), *quarter(0)[2:],
                          (2, cos_turn(0)), (2, cos_scores(2)), (2, cos_out(0)), *quarter(4),
                          (2, cos_turn(1)), (2, cos_scores(3)), (2, cos_out(1)), *quarter(8),
                          (2, cos_turn(2)), (1, met_scores(12)), (1, met_out(11)), (2, cos_out(2)),
                          *quarter(12)[2:], (1, met_out(15)),
                          (2, cos_turn(3)), (1, met_turn_o), (2, cos_out(3)), (1, met_mix)])

        @block.scalar
        def _(act):
            f = nc.scalar.activation

            act.dma_start(ffn_all, pack_ffn).then_inc(loaded["pack_ffn"], 16)
            act.dma_start(l1_all, pack_l1).then_inc(loaded["pack_l1"], 16)
            act.wait_ge(ev("ctx_transposed"), 1)
            f(ctx_t.rearrange("p a b c -> p (a b c)"), flat(0, 2), ACT.Copy).then_inc(ev("ctx_t_ready"), 1)
            act.wait_ge(ev("xat_k_projected"), 1)
            for c in range(NC):
                last = f(kt[:, c].rearrange("p a b -> p (a b)"), flat(2 + c), ACT.Identity,
                         bias=w["xat_bk"][:, c:c + 1])
            last.then_inc(ev("xat_k_biased"), 1)
            for p in range(NP):
                act.wait_ge(ev("cos_k_projected"), p + 1)
                if p >= 1:
                    act.wait_ge(ev("cos_k_floored"), p)
                    f(krn[:, (p - 1) % 2], krn[:, (p - 1) % 2], ACT.Sqrt).then_inc(ev("cos_k_rooted"), 1)
                if p >= 2:
                    act.wait_ge(ev("cos_k_scaled"), p - 1)
                f(kraw[:, p % 2], flat(4 + p % 2), ACT.Copy)
                f(ksq[:, p % 2], flat(4 + p % 2), ACT.Square).then_inc(ev("cos_k_squared"), 1)
            act.wait_ge(ev("cos_k_floored"), NP)
            f(krn[:, 1], krn[:, 1], ACT.Sqrt).then_inc(ev("cos_k_rooted"), 1)
            act.wait_ge(ev("kbd_ready"), 1)
            for p in range(NP):
                act.wait_ge(ev("cos_v_projected"), p + 1)
                if p >= 2:
                    act.wait_ge(moved("cv_stored", p % 2), 16 * (p // 2))
                f(vst[:, p % 2], flat(p % 2), ACT.Copy).then_inc(ev("cos_v_copied"), 1)
                act.wait_ge(ev("cos_v_copied"), p + 1)
                act.dma_start(cv_d[:, p, :], vst[:, p % 2]).then_inc(moved("cv_stored", p % 2), 16)
            act.wait_ge(ev("metric_product"), 1)
            f(met_m.rearrange("p a b -> p (a b)"), flat(3)[:, 0:C], ACT.Copy, scale=HD ** -0.5)
            f(null_w[0:H, :], flat(3)[0:H, C:2 * C], ACT.Copy)
            act.wait_ge(ev("mixer_product"), 1)
            f(met_wo.rearrange("p a b -> p (a b)"), flat(7), ACT.Copy)
            act.wait_ge(ev("spec_forward"), 1)
            f(at_r.rearrange("p a b -> p (a b)"), flat(5), ACT.Copy).then_inc(ev("spec_forward_copied"), 1)
            f(at_i.rearrange("p a b -> p (a b)"), flat(6), ACT.Copy).then_inc(ev("spec_forward_copied"), 1)
            for name, dst in (("w_up", wup_t), ("w_gate", wgate_t), ("w_down", wdown_t)):
                act.wait_ge(ev("weight_turned"), WEIGHTS[name])
                f(dst.rearrange("p a b -> p (a b)"), flat(0, 3), ACT.Copy).then_inc(ev("weight_copied"), 1)
            act.wait_ge(ev("spec_product"), 1)
            f(spec_m.rearrange("p a b -> p (a b)"), flat(4), ACT.Copy, scale=1.0 / C).then_inc(ev("prep_done"), 1)
            act.wait_ge(ev("prep_done"), 3)

            def lin_copy_x(b, par):
                wait(act, "lin_x_turned", b)
                f(lin_xt[:, par].rearrange("p a b -> p (a b)"), flat(0, 2), ACT.Copy)\
                    .then_inc(sig("lin_x_copied").sem, 1)

            def lin_bias_q(b, par):
                wait(act, "lin_q_projected", b)
                for c in range(NC):
                    last = f(lin_zq[:, c], flat(2 + c), ACT.Identity, bias=w["lin_bq"][:, c:c + 1])
                last.then_inc(sig("lin_q_biased").sem, 1)

            def lin_exp_q(b, par):
                wait(act, "lin_q_negative", b)
                f(lin_eq, lin_eq, ACT.Exp).then_inc(sig("lin_q_exp").sem, 1)

            def lin_exp_k(b, par):
                wait(act, "lin_k_negative", b)
                f(lin_ek, lin_ek, ACT.Exp).then_inc(sig("lin_k_exp").sem, 1)

            def lin_copy_y(b, par):
                wait(act, "lin_y_turned", b)
                f(xt1.rearrange("p a b -> p (a b)"), flat(0, 2), ACT.Copy)\
                    .then_inc(sig("lin_y_copied").sem, 1)

            def xat_bias_q(b, par):
                wait(act, "xat_q_projected", b)
                for c in range(NC):
                    last = f(xat_q[:, c], flat(4 + c), ACT.Identity, bias=w["xat_bq"][:, c:c + 1])
                last.then_inc(sig("xat_q_biased").sem, 1)

            def xat_exp(t):
                def step(b, par):
                    wait(act, "xat_shifted", b, t + 1, NT)
                    s = xat_s[:, t % 2].rearrange("p a b -> p (a b)")
                    f(s, s, ACT.Exp, scale=HD ** -0.5).then_inc(sig("xat_exp_done", NT).sem, 1)
                return step

            def xat_copy_probs(t):
                def step(b, par):
                    wait(act, "xat_probs_turned", b, t + 1, NT)
                    f(xat_pt.rearrange("p a b -> p (a b)"), flat(6, 2), ACT.Copy)\
                        .then_inc(sig("xat_probs_copied", NT).sem, 1)
                return step

            def xat_copy_o(b, par):
                wait(act, "xat_o_turned", b)
                f(xat_ot.rearrange("p a b -> p (a b)"), flat(6, 2), ACT.Copy)\
                    .then_inc(sig("xat_o_copied").sem, 1)

            pipeline(act, [(0, lin_copy_x), (1, xat_bias_q), (0, lin_bias_q), (0, lin_exp_q),
                           (1, xat_exp(0)), (1, xat_exp(1)), (0, lin_exp_k), (1, xat_copy_probs(0)),
                           (1, xat_exp(2)), (1, xat_copy_probs(1)), (1, xat_exp(3)),
                           (1, xat_copy_probs(2)), (1, xat_copy_probs(3)), (1, xat_copy_o),
                           (0, lin_copy_y)])

            act.wait_ge(ev("scale_ready"), QUANTIZED["x"])

            def ffn_copy_x(b, par):
                wait(act, "ffn_x_turned", b)
                f(ffn_xt[:, par].rearrange("p a b -> p (a b)"), flat(0, 2), ACT.Copy)\
                    .then_inc(sig("ffn_x_copied").sem, 1)

            def ffn_copy_products(b, par):
                wait_moved(act, "up_stored", b, par, 2)
                wait_back(act, "ffn_peaked", b, 2)
                g_b = at_cols(gated, b).rearrange("p (t j n) -> p t j n", t=NT, j=NF)
                for j in range(NF):
                    for g, done in enumerate(("up", "gate")):
                        wait(act, done + "_done", b, j + 1, NF)
                        f(g_b[:, :, j] if g else ffn_up[:, par, :, j],
                          flat(2 + (2 * j + g) % 6).rearrange("p (t n) -> p t n", t=NT), ACT.Copy)\
                            .then_inc(sig(done + "_copied", NF).sem, 1)

            pipeline(act, [(0, ffn_copy_x), (1, ffn_copy_products)])

            wait_all_moved(act, "up_stored")

            def ffn_sigmoid(b, par):
                wait(act, "gate_rounded", b)
                f(sig_f[:, par], gate_i[:, par], ACT.Sigmoid, scale=quant["gate_scale"])\
                    .then_inc(sig("sigmoid_done").sem, 1)

            pipeline(act, [(0, ffn_sigmoid)])

            def ffn_round_up(b, par):
                wait_moved(act, "up_loaded", b, par)
                wait_previous(act, "v_ready", b)
                f(up_i, up_f[:, par], ACT.Copy, scale=quant["up_mult"]).then_inc(sig("up_rounded").sem, 1)

            pipeline(act, [(0, ffn_round_up)])

            def copy2(out_ap, first, name, after, j=1, per=1):
                def step(b, par):
                    wait(act, after, b, j, per)
                    f(out_ap, flat(first, 2), ACT.Copy).then_inc(sig(name, per).sem, 1)
                return step

            def cos_copy_q(p):
                def step(b, par):
                    wait(act, "cos_q_done", b, p + 1, NP)
                    if p >= 2:
                        wait(act, "cos_q_normed", b, p - 1, NP)
                    f(cos_q[:, p], flat(p % 2), ACT.Copy)
                    f(cos_sq[:, p % 2], flat(p % 2), ACT.Square).then_inc(sig("cos_q_squared", NP).sem, 1)
                return step

            def cos_exp(t):
                def step(b, par):
                    wait(act, "cos_shifted", b, t + 1, NT)
                    f(cos_s[:, t % 2], cos_s[:, t % 2], ACT.Exp).then_inc(sig("cos_exp_done", NT).sem, 1)
                return step

            def cos_copy_pt(t):
                def step(b, par):
                    wait(act, "cos_turned", b, t + 1, NT)
                    f(cos_pt.rearrange("p a b -> p (a b)"), flat(2, 2), ACT.Copy)
                    f(cos_p0[0:H], flat(4)[0:H, 0:P], ACT.Copy).then_inc(sig("cos_pt_copied", NT).sem, 1)
                return step

            def cos_copy_o(t):
                def step(b, par):
                    wait(act, "cos_out_done", b, t + 1, NT)
                    if t == 0:
                        wait_previous(act, "y6_ready", b)
                    f(cos_o[:, t], flat(4)[:, C:2 * C], ACT.Copy).then_inc(sig("cos_o_copied", NT).sem, 1)
                return step

            def met_copy_o(c):
                def step(b, par):
                    wait(act, "met_weighted", b, 8 * c + 8, 16)
                    f(met_o[:, :, c * P:(c + 1) * P], flat(7).rearrange("p (t n) -> p t n", t=NT), ACT.Copy)\
                        .then_inc(sig("met_o_copied", 2).sem, 1)
                return step

            def all_of(ap):
                return ap.rearrange("p a b -> p (a b)")

            pipeline(act, [(2, copy2(all_of(cos_vw[:, 0:4]), 2, "cos_vw_copied", "cos_vw_done", 1, 2)),
                           (3, copy2(all_of(xt5), 2, "cos_x_copied", "cos_x_turned")),
                           (2, copy2(all_of(cos_vw[:, 4:8]), 2, "cos_vw_copied", "cos_vw_done", 2, 2)),
                           (1, copy2(all_of(met_p), 5, "met_p_ready", "met_projected")),
                           (2, copy2(all_of(xt4), 5, "met_x_copied", "met_x_turned")),
                           (1, copy2(all_of(met_pr), 5, "met_pr_ready", "met_p_turned")),
                           (2, cos_copy_q(0)),
                           (1, copy2(all_of(met_q), 5, "met_q_ready", "met_q_done")),
                           *[(2, cos_copy_q(p)) for p in range(1, 5)],
                           (0, copy2(all_of(xt3), 5, "dn_copied", "dn_turned")),
                           *[(2, cos_copy_q(p)) for p in range(5, NP)],
                           (2, cos_exp(0)), (2, cos_exp(1)), (2, cos_copy_pt(0)), (2, cos_copy_o(0)),
                           (2, cos_exp(2)), (2, cos_copy_pt(1)), (1, met_copy_o(0)), (2, cos_copy_o(1)),
                           (2, cos_exp(3)), (2, cos_copy_pt(2)), (2, cos_copy_o(2)), (1, met_copy_o(1)),
                           (2, cos_copy_pt(3)),
                           (1, copy2(all_of(met_ot), 5, "met_ot_ready", "met_o_turned")),
                           (2, cos_copy_o(3))])

        @block.gpsimd
        def _(pool):
            g = nc.gpsimd
            g.memset(neghalf, -0.5).then_inc(ev("constants_set"), 1)
            pool.wait_ge(ev("constants_set"), 1)
            pool.wait_ge(ev("null_k_floored"), 1)
            g.tensor_tensor(null_n, null_n, neghalf[:, 0:1], ALU.pow).then_inc(ev("null_k_rnormed"), 1)
            pool.wait_ge(ev("prep_done"), 3)

            def rstd(name, var):
                def step(b, par):
                    wait(pool, name + "_stats", b)
                    g.tensor_tensor(var[0], var[1], neghalf[:, 0:NT], ALU.pow)\
                        .then_inc(sig(name + "_rstd").sem, 1)
                return step

            pipeline(pool, [(0, rstd("lin", (lin_rs, lin_rs))), (1, rstd("xat", (xat_rs, xat_rs)))])

            for name in ("x", "up", "gate", "t", "v"):
                pool.wait_ge(ev("peak_found"), QUANTIZED[name])
                g.partition_all_reduce(quant[name + "_all"], quant[name + "_max"], P, bass.bass_isa.ReduceOp.max)\
                    .then_inc(ev("peak_shared"), 1)

            g.memset(cos_kb, 0.0).then_inc(ev("pads_cleared"), 1)
            g.memset(cos_vb, 0.0).then_inc(ev("pads_cleared"), 1)

            def cos_norms(b, par):
                wait(pool, "cos_floored", b)
                for t in range(NT):
                    g.tensor_tensor(cos_nn[:, t, 0:H], cos_nn[:, t, 0:H], neghalf[:, 0:H], ALU.pow)\
                        .then_inc(sig("cos_rnormed", NT).sem, 1)

            def cos_o_rstd(t):
                def step(b, par):
                    rs = norms["cos_o"][2][:, t:t + 1]
                    wait(pool, "cos_o_stats", b, t + 1, NT)
                    g.tensor_tensor(rs, rs, neghalf[:, 0:1], ALU.pow).then_inc(sig("cos_o_rstd", NT).sem, 1)
                return step

            def loop2_rstd(name):
                return rstd(name, (norms[name][2], norms[name][2]))

            pipeline(pool, [(2, loop2_rstd("met")), (3, cos_o_rstd(3)), (2, loop2_rstd("met2")),
                            (3, loop2_rstd("cos")), (0, loop2_rstd("dn")), (3, loop2_rstd("spec")),
                            (2, cos_norms), (2, cos_o_rstd(0)), (2, cos_o_rstd(1)), (2, cos_o_rstd(2))])

        @block.vector
        def _(dve):
            v = nc.vector
            line = Line(dve, "vector_prep")
            link = line.link
            dve.wait_ge(ev("ctx_t_ready"), 1)
            for c in range(NC):
                v.tensor_copy(ctx_t2[:, c], ctx_t[:, c].unsqueeze(2).broadcast_to([P, B, 2, TC]))\
                    .then_inc(ev("ctx_t2_ready"), 1)
            dve.wait_ge(ev("xat_k_biased"), 1)
            for c in range(NC):
                for h in range(GH):
                    last = v.tensor_scalar(kbd[:, c, :, h], kt[:, c], w["head16"][:, h:h + 1], None, ALU.mult)
            last.then_inc(ev("kbd_ready"), 1)
            link(v.tensor_scalar(gk, w["q_scale"], w["k_scale"], 8.0, ALU.mult, ALU.mult))
            for p in range(NP):
                dve.wait_ge(ev("cos_k_normed"), p + 1)
                v.tensor_scalar(krn[:, p % 2], flat(6 + p % 2), 1e-24, None, ALU.max)\
                    .then_inc(ev("cos_k_floored"), 1)
                dve.wait_ge(ev("cos_k_rooted"), p + 1)
                link(v.reciprocal(krn[:, p % 2], krn[:, p % 2]))
                if p >= 2:
                    dve.wait_ge(moved("ck_stored", p % 2), 16 * (p // 2))
                v.scalar_tensor_tensor(out=kst[:, p % 2], in0=kraw[:, p % 2], scalar=gk, in1=krn[:, p % 2],
                                       op0=ALU.mult, op1=ALU.mult).then_inc(ev("cos_k_scaled"), 1)
            dve.wait_ge(ev("xat_v_projected"), 1)
            v.tensor_tensor(vtmp, rows2(4, 4), w["xat_bv"].unsqueeze(1).broadcast_to([P, B, C]), ALU.add)\
                .then_inc(ev("xat_v_biased"), 1)
            dve.wait_ge(ev("xat_v_biased"), 1)
            vb = vbd.rearrange("p a b c -> p (a b) c")
            v.tensor_tensor(vb[:, :, 0:2 * HD], vtmp.rearrange("p a (b c) -> p (a b) c", c=2 * HD),
                            w["pair16"][:, 0:2 * HD].unsqueeze(1).broadcast_to([P, B * NP, 2 * HD]), ALU.mult)
            v.tensor_copy(vb[:, :, 2 * HD:], w["pair16"][:, 2 * HD:].unsqueeze(1).broadcast_to([P, B * NP, 2]))
            dve.wait_ge(loaded["pack_ffn"], 16)
            for name, before in (("w_up", None), ("w_gate", "w_up"), ("w_down", "w_gate")):
                src = w[name].rearrange("p a (b c) -> p (a b) c", c=BLK)
                n = NF * C // BLK
                link(v.tensor_reduce(qmag, src, AX.X, ALU.max, apply_absolute_value=True))
                link(v.tensor_scalar(qmag, qmag, 1.0 / 7.0, 1e-12, ALU.mult, ALU.max))
                link(v.reciprocal(qrec, qmag))
                if before:
                    dve.wait_ge(ev("weight_turned"), WEIGHTS[before])
                q = wq.rearrange("p (a b) -> p a b", b=BLK)
                link(v.tensor_tensor(q, src, qrec.unsqueeze(2).broadcast_to([P, n, BLK]), ALU.mult))
                link(v.tensor_scalar(q, q, MAGIC, None, ALU.add))
                link(v.tensor_scalar(q, q, MAGIC, None, ALU.subtract))
                v.tensor_tensor(q, q, qmag.unsqueeze(2).broadcast_to([P, n, BLK]), ALU.mult)\
                    .then_inc(ev("weight_quantized"), 1)
                dve.wait_ge(ev("weight_quantized"), WEIGHTS[name])
            dve.wait_ge(loaded["pack_l1"], 16)
            for c in range(NC):
                v.tensor_scalar(w["cos_wq"][:, c], w["cos_wq"][:, c], w["cos_gn"][:, c:c + 1], None, ALU.mult)
            link(v.tensor_tensor(null_k, w["null_row"], w["null_row"], ALU.mult))
            link(v.tensor_reduce(null_n, null_k, AX.X, ALU.add))
            v.tensor_scalar(null_n, null_n, 1e-24, None, ALU.max).then_inc(ev("null_k_floored"), 1)
            link(v.tensor_tensor(null_k, w["null_row"], w["q_row"], ALU.mult))
            link(v.scalar_tensor_tensor(out=null_k, in0=null_k, scalar=8.0, in1=w["k_row"], op0=ALU.mult,
                                        op1=ALU.mult))
            dve.wait_ge(ev("null_k_rnormed"), 1)
            link(v.tensor_scalar(null_k, null_k, null_n, None, ALU.mult))
            dve.wait_ge(ev("weight_turned"), WEIGHTS["w_down"])
            for c in range(NC):
                link(v.tensor_tensor(null_p, w["cos_wq"][:, c].rearrange("p (h k) -> p h k", h=H),
                                     null_k.unsqueeze(1).broadcast_to([P, H, CD]), ALU.mult))
                link(v.tensor_reduce(null_wq[:, c], null_p, AX.X, ALU.add))
            v.memset(spare, 0.0).then_inc(ev("prep_done"), 1)
            dve.wait_ge(ev("spec_product"), 1)
            dve.wait_ge(ev("weight_copied"), WEIGHTS["w_down"])
            v.memset(small, 0.0).then_inc(ev("prep_done"), 1)
            dve.wait_ge(ev("prep_done"), 3)

            lin = Chain(dve, sem("vector_lin"), 10)
            xat = Chain(dve, sem("vector_xat"), 13)

            def norm_stats(name, chain, r, st, mv, rs):
                for t in range(NT - 1):
                    v.bn_stats(st[:, t], r[:, t])
                chain.link(v.bn_stats(st[:, NT - 1], r[:, NT - 1]))
                v.memset(spare, 0.0)
                for t in range(NT - 1):
                    v.bn_aggr(mv[:, t], st[:, t])
                chain.link(v.bn_aggr(mv[:, NT - 1], st[:, NT - 1]))
                v.tensor_scalar(rs, mv[:, :, 1:2].rearrange("p a b -> p (a b)"), EPS, None, ALU.add)\
                    .then_inc(sig(name + "_stats").sem, 1)

            def normalize(name, b, y, r, mv, rs):
                wait(dve, name + "_rstd", b)
                for t in range(NT):
                    last = v.tensor_scalar(y[:, t], r[:, t], mv[:, t, 0:1], rs[:, t:t + 1],
                                           ALU.subtract, ALU.mult)
                return last

            def lin_q_features(b, par):
                lin.begin(b)
                wait(dve, "lin_q_biased", b)
                v.tensor_scalar(lin_eq, lin_zq, 0.0, None, ALU.min).then_inc(sig("lin_q_negative").sem, 1)
                wait(dve, "lin_q_exp", b)
                v.scalar_tensor_tensor(out=lin_q, in0=lin_zq, scalar=0.0, in1=lin_eq, op0=ALU.max,
                                       op1=ALU.add).then_inc(sig("lin_q_ready").sem, 1)

            def lin_bias_kv(t):
                def step(b, par):
                    wait(dve, "lin_kv_projected", b, t + 1, NT)
                    v.tensor_tensor(lin_z[:, t], flat(t % 2), w["lin_bkv"], ALU.add)\
                        .then_inc(sig("lin_kv_biased", NT).sem, 1)
                return step

            def lin_k_features(b, par):
                wait(dve, "lin_kv_biased", b, NT, NT)
                v.tensor_scalar(lin_ek, lin_z[:, :, 0:C], 0.0, None, ALU.min)\
                    .then_inc(sig("lin_k_negative").sem, 1)
                wait(dve, "lin_k_exp", b)
                v.scalar_tensor_tensor(out=lin_k, in0=lin_z[:, :, 0:C], scalar=0.0, in1=lin_ek, op0=ALU.max,
                                       op1=ALU.add).then_inc(sig("lin_k_ready").sem, 1)

            def lin_mask_state(b, par):
                wait(dve, "lin_state_done", b)
                for c in range(NC):
                    v.tensor_tensor(lin_kv[:, c, 0:P], flat(2)[:, c * P:(c + 1) * P], w["blk32"], ALU.mult)
                    last = v.tensor_scalar(lin_kv[:, c, P:], w["blk32"][:, 0:P:LD], flat(2)[:, C + c:C + c + 1],
                                           None, ALU.mult)
                last.then_inc(sig("lin_kv_ready").sem, 1)

            def lin_finish(b, par):
                for t in range(NT):
                    wait(dve, "lin_out_done", b, t + 1, NT)
                    o = flat((3, 0, 1, 2)[t])[:, 0:264].rearrange("p (c n) -> p c n", c=NC)
                    lin.link(v.tensor_scalar(lin_den[:, t % 2], o[:, :, P:], 1e-6, None, ALU.add))
                    lin.link(v.reciprocal(lin_den[:, t % 2], lin_den[:, t % 2]))
                    v.tensor_tensor(lin_r[:, t].rearrange("p (c h d) -> p c h d", c=NC, h=P // LD),
                                    o[:, :, 0:P].rearrange("p c (h d) -> p c h d", d=LD),
                                    lin_den[:, t % 2].unsqueeze(3).broadcast_to([P, NC, P // LD, LD]),
                                    ALU.mult).then_inc(sig("lin_scaled", NT).sem, 1)
                wait(dve, "lin_scaled", b, NT, NT)
                v.tensor_tensor(lin_r, lin_r, lin_x[:, par], ALU.add).then_inc(sig("lin_added").sem, 1)
                wait(dve, "lin_added", b)
                norm_stats("lin", lin, lin_r, lin_st, lin_mv, lin_rs)
                normalize("lin", b, y1[:, par], lin_r, lin_mv, lin_rs).then_inc(sig("y1_ready").sem, 1)
                lin.end()

            def xat_shift(t):
                def step(b, par):
                    if t == 0:
                        xat.begin(b)
                    wait(dve, "xat_scored", b, t + 1, NT)
                    if t >= 2:
                        wait(dve, "xat_probs_turned", b, t - 1, NT)
                    s = flat(4, 2).rearrange("p (h k) -> p h k", k=TC)
                    mx = xat_mx[:, t % 2]
                    xat.link(v.tensor_reduce(mx, s, AX.X, ALU.max))
                    v.tensor_tensor(xat_s[:, t % 2], s, mx.unsqueeze(2).broadcast_to([P, H, TC]),
                                    ALU.subtract).then_inc(sig("xat_shifted", NT).sem, 1)
                return step

            def xat_normalize(t):
                def step(b, par):
                    wait(dve, "xat_weighted", b, t + 1, NT)
                    o = flat(6)[:, 0:NP * 34].rearrange("p (a n) -> p a n", a=NP)
                    rec = xat_rec.rearrange("p (a n) -> p a n", a=NP)
                    xat.link(v.reciprocal(rec, o[:, :, 2 * HD:]))
                    v.tensor_tensor(xat_o[:, t].rearrange("p (a h d) -> p a h d", a=NP, h=2),
                                    o[:, :, 0:2 * HD].rearrange("p a (h d) -> p a h d", h=2),
                                    rec.unsqueeze(3).broadcast_to([P, NP, 2, HD]),
                                    ALU.mult).then_inc(sig("xat_normed", NT).sem, 1)
                return step

            def xat_finish(b, par):
                xat.link(v.tensor_tensor(xat_r, y1[:, par], w["xat_bo"].unsqueeze(1).broadcast_to([P, NT, C]), ALU.add))
                wait(dve, "xat_out_projected", b)
                v.tensor_tensor(xat_r, rows2(4), xat_r, ALU.add).then_inc(sig("xat_out_added").sem, 1)
                wait(dve, "xat_out_added", b)
                norm_stats("xat", xat, xat_r, xat_st, xat_mv, xat_rs)
                wait_previous(dve, "x3_stored", b, 16)
                normalize("xat", b, y2[:, par], xat_r, xat_mv, xat_rs).then_inc(sig("y2_ready").sem, 1)
                wait(dve, "y2_ready", b)
                xat.link(v.tensor_reduce(quant["tmp"], y2[:, par], AX.XY, ALU.max, apply_absolute_value=True))
                xat.link(v.tensor_tensor(quant["x_max"], quant["x_max"], quant["tmp"], ALU.max))
                xat.end()

            pipeline(dve, [(0, lin_q_features), (1, xat_shift(0)), (0, lin_bias_kv(0)), (0, lin_bias_kv(1)),
                           (0, lin_bias_kv(2)), (0, lin_bias_kv(3)), (1, xat_shift(1)), (0, lin_k_features),
                           (1, xat_shift(2)), (1, xat_normalize(0)), (1, xat_shift(3)),
                           (1, xat_normalize(1)), (0, lin_mask_state), (1, xat_normalize(2)),
                           (1, xat_normalize(3)), (0, lin_finish), (1, xat_finish)])

            def peak(name):
                v.tensor_copy(quant[name + "_max"], quant[name + "_max"]).then_inc(ev("peak_found"), 1)

            def scale(name, raw):
                dve.wait_ge(ev("peak_shared"), QUANTIZED[name])
                link(v.tensor_scalar(quant[name + "_scale"], quant[name + "_all"], raw, 1.0 / QMAX,
                                     ALU.mult, ALU.mult))
                link(v.tensor_scalar(quant[name + "_scale"], quant[name + "_scale"], 1e-12, None, ALU.max))
                link(v.reciprocal(quant[name + "_mult"], quant[name + "_scale"]))
                v.tensor_scalar(quant[name + "_mult"], quant[name + "_mult"], raw, None, ALU.mult)\
                    .then_inc(ev("scale_ready"), 1)
                dve.wait_ge(ev("scale_ready"), QUANTIZED[name])

            peak("x")
            scale("x", 1.0)
            ffn = Chain(dve, sem("vector_ffn"), 1)

            def ffn_round_x(b, par):
                wait_moved(dve, "ffn_x_loaded", b, par)
                v.tensor_scalar(ffn_x[:, par], ffn_x[:, par], quant["x_mult"], MAGIC, ALU.mult, ALU.add)\
                    .then_inc(sig("ffn_x_scaled").sem, 1)
                wait(dve, "ffn_x_scaled", b)
                v.tensor_scalar(ffn_x[:, par], ffn_x[:, par], MAGIC, None, ALU.subtract)\
                    .then_inc(sig("ffn_x_rounded").sem, 1)

            def ffn_peaks(b, par):
                ffn.begin(b)
                wait(dve, "up_copied", b, NF, NF)
                v.tensor_reduce(peaks[:, 0:1], ffn_up[:, par].rearrange("p a b c -> p (a b c)"), AX.X, ALU.max,
                                apply_absolute_value=True)
                wait(dve, "gate_copied", b, NF, NF)
                v.memset(spare, 0.0)
                v.tensor_reduce(peaks[:, 1:2], at_cols(gated, b), AX.X, ALU.max,
                                apply_absolute_value=True).then_inc(sig("ffn_peaked").sem, 1)
                wait(dve, "ffn_peaked", b)
                ffn.link(v.tensor_tensor(small[:, 2:4], small[:, 2:4], peaks[:, 0:2], ALU.max))
                ffn.end()

            pipeline(dve, [(0, ffn_round_x), (1, ffn_peaks)])
            peak("up")
            peak("gate")
            scale("up", quant["x_scale"])
            scale("gate", quant["x_scale"])
            link(v.tensor_scalar(quant["t_raw"], quant["gate_scale"], 1.0 / 65536.0, None, ALU.mult))
            wait_all_moved(dve, "up_stored")

            second = Chain(dve, None, 2, after=ffn)

            def gate_round(b, par):
                wait_back(dve, "t_ready", b, 2)
                v.tensor_scalar(gate_i[:, par], at_cols(gated, b), quant["gate_mult"], None, ALU.mult)\
                    .then_inc(sig("gate_rounded").sem, 1)

            def gate_product(b, par):
                second.begin(b)
                wait(dve, "sigmoid_done", b)
                v.tensor_scalar(sig_i[:, par], sig_f[:, par], 65536.0, 65535.0, ALU.mult, ALU.min)\
                    .then_inc(sig("sigmoid_rounded").sem, 1)
                wait(dve, "sigmoid_rounded", b)
                v.tensor_tensor(at_cols(gated, b), gate_i[:, par], sig_i[:, par], ALU.mult)\
                    .then_inc(sig("t_ready").sem, 1)
                wait(dve, "t_ready", b)
                v.memset(spare, 0.0)
                second.link(v.tensor_reduce(quant["tmp"], at_cols(gated, b), AX.X, ALU.max,
                                            apply_absolute_value=True))
                second.link(v.tensor_tensor(quant["t_max"], quant["t_max"], quant["tmp"], ALU.max))
                second.end()

            pipeline(dve, [(0, gate_round), (1, gate_product)])
            peak("t")
            scale("t", quant["t_raw"])
            link(v.tensor_tensor(quant["v_raw"], quant["t_scale"], quant["up_scale"], ALU.mult))
            third = Chain(dve, None, 3, after=second)

            def product(b, par):
                third.begin(b)
                third.link(v.tensor_scalar(t_i, at_cols(gated, b), quant["t_mult"], None, ALU.mult))
                wait(dve, "up_rounded", b)
                wait_moved(dve, "v_stored", b, par, 2)
                v.tensor_tensor(v_f[:, par], t_i, up_i, ALU.mult).then_inc(sig("v_ready").sem, 1)
                wait(dve, "v_ready", b)
                third.link(v.tensor_reduce(quant["tmp"], v_f[:, par], AX.X, ALU.max, apply_absolute_value=True))
                third.link(v.tensor_tensor(quant["v_max"], quant["v_max"], quant["tmp"], ALU.max))
                third.end()

            pipeline(dve, [(0, product)])
            peak("v")
            scale("v", quant["v_raw"])

            dn, met = Chain(dve, None, 2, after=third), Chain(dve, None, 2, after=lin)
            cos, spec = Chain(dve, None, 29, after=xat), Chain(dve, sem("vector_spec"), 3)
            met_end, cos_end = Chain(dve, sem("vector_met_end"), 5), Chain(dve, sem("vector_cos_end"), 5)

            def stats(name, chain, rows):
                norm_stats(name, chain, rows, *norms[name])

            def scaled_rows(name, b, y, rows):
                return normalize(name, b, y, rows, norms[name][1], norms[name][2])

            def dn_round(t):
                def step(b, par):
                    dve.wait_ge(moved("v_loaded", t % 2), at_tile("v", b, t))
                    v.tensor_scalar(dn_v[:, t % 2], dn_v[:, t % 2], quant["v_mult"], MAGIC, ALU.mult, ALU.add)\
                        .then_inc(sig("dn_v_scaled", NT).sem, 1)
                    wait(dve, "dn_v_scaled", b, t + 1, NT)
                    v.tensor_scalar(dn_v[:, t % 2], dn_v[:, t % 2], MAGIC, None, ALU.subtract)\
                        .then_inc(sig("dn_v_rounded", NT).sem, 1)
                return step

            def dn_add(b, par):
                dn.begin(b)
                wait(dve, "dn_projected", b, NT, NT)
                wait_moved(dve, "dn_x_loaded", b, par)
                dn_r = dn_x[:, par]
                v.scalar_tensor_tensor(out=dn_r, in0=rows2(5), scalar=quant["v_scale"], in1=dn_r,
                                       op0=ALU.mult, op1=ALU.add).then_inc(sig("dn_added").sem, 1)
                wait(dve, "dn_added", b)
                stats("dn", dn, dn_r)

            def dn_finish(b, par):
                scaled_rows("dn", b, y3[:, par], dn_x[:, par]).then_inc(sig("y3_ready").sem, 1)
                dn.end()

            def met_mask_queries(c):
                def step(b, par):
                    if c == 0:
                        met.begin(b)
                        wait(dve, "met_q_ready", b)
                    else:
                        wait(dve, "met_scored", b, 8, 16)
                    for h in range(GH):
                        last = v.tensor_scalar(met_qh[:, h], met_q[:, c], w["mhead16"][:, h:h + 1], None, ALU.mult)
                    last.then_inc(sig("met_qh_ready", 2).sem, 1)
                return step

            def met_mask_states(b, par):
                wait(dve, "met_state_done", b)
                n = (NT - 1) * P
                met.link(v.tensor_tensor(
                    met_st, bank(5, 2)[:, :, 0:n].rearrange("p c (t n) -> p c t n", t=NT - 1),
                    w["blk16"].unsqueeze(1).unsqueeze(1).broadcast_to([P, NC, NT - 1, P]), ALU.mult))
                met.link(v.tensor_tensor(met_st[:, :, 1], met_st[:, :, 1], met_st[:, :, 0], ALU.add))
                v.tensor_tensor(met_st[:, :, 2], met_st[:, :, 2], met_st[:, :, 1], ALU.add)\
                    .then_inc(sig("met_states_ready").sem, 1)
                met.end()

            def met_mask(n):
                def step(b, par):
                    wait(dve, "met_scored", b, n + 1, 16)
                    if n >= 2:
                        wait(dve, "met_weighted", b, n - 1, 16)
                    v.tensor_tensor(met_s[:, n % 2], flat(5 + n % 2).rearrange("p (h n) -> p h n", h=4),
                                    w["causal"].unsqueeze(1).broadcast_to([P, 4, P]), ALU.mult)\
                        .then_inc(sig("met_masked", 16).sem, 1)
                return step

            def met_add(b, par):
                met_end.begin(b)
                wait(dve, "met_mixed", b)
                v.tensor_tensor(met_r, rows2(5), y3[:, par], ALU.add).then_inc(sig("met_added").sem, 1)
                wait(dve, "met_added", b)
                stats("met", met_end, met_r)

            def met_norm(b, par):
                met_end.link(scaled_rows("met", b, y4[:, par], met_r))
                stats("met2", met_end, y4[:, par])

            def met_norm2(b, par):
                scaled_rows("met2", b, xn4, y4[:, par]).then_inc(sig("xn4_ready").sem, 1)
                met_end.end()

            def cos_floor(b, par):
                cos.begin(b)
                wait(dve, "cos_q_normed", b, NP, NP)
                nn = flat(4)[:, 0:NT * 32].rearrange("p (t n) -> p t n", t=NT)
                v.tensor_scalar(cos_nn[:, :, 0:H], nn[:, :, 0:H], 1e-24, None, ALU.max)
                v.tensor_copy(cos_nn[:, :, H:], nn[:, :, H:]).then_inc(sig("cos_floored").sem, 1)
                wait(dve, "cos_floored", b)

            def heads(t):
                return cos_s[:, t % 2, 0:H * TC].rearrange("p (h k) -> p h k", h=H), cos_s[:, t % 2, H * TC:]

            def cos_scale(t):
                def step(b, par):
                    s, s0 = heads(t)
                    rn = cos_nn[:, t, 0:H]
                    wait(dve, "cos_rnormed", b, t + 1, NT)
                    wait(dve, "cos_scored", b, t + 1, NT)
                    if t >= 2:
                        wait(dve, "cos_turned", b, t - 1, NT)
                    v.tensor_tensor(s0, cos_nn[:, t, H:], rn, ALU.mult)
                    v.tensor_tensor(s, flat(0, 2).rearrange("p (h k) -> p h k", h=H),
                                    rn.unsqueeze(2).broadcast_to([P, H, TC]), ALU.mult)\
                        .then_inc(sig("cos_scaled", NT).sem, 1)
                return step

            def cos_max(t):
                def step(b, par):
                    s, s0 = heads(t)
                    mx = cos_mx[:, t % 2]
                    wait(dve, "cos_scaled", b, t + 1, NT)
                    cos.link(v.tensor_reduce(mx, s, AX.X, ALU.max))
                    cos.link(v.tensor_tensor(mx, mx, s0, ALU.max))
                return step

            def cos_shift(t):
                def step(b, par):
                    s, s0 = heads(t)
                    mx = cos_mx[:, t % 2]
                    v.tensor_tensor(s0, s0, mx, ALU.subtract)
                    v.tensor_tensor(s, s, mx.unsqueeze(2).broadcast_to([P, H, TC]), ALU.subtract)\
                        .then_inc(sig("cos_shifted", NT).sem, 1)
                return step

            def cos_sum(t):
                def step(b, par):
                    s, s0 = heads(t)
                    mx = cos_mx[:, t % 2]
                    wait(dve, "cos_exp_done", b, t + 1, NT)
                    cos.link(v.tensor_reduce(mx, s, AX.X, ALU.add))
                    cos.link(v.tensor_tensor(mx, mx, s0, ALU.add))
                    cos.link(v.reciprocal(mx, mx))
                return step

            def cos_divide(t):
                def step(b, par):
                    s, s0 = heads(t)
                    mx = cos_mx[:, t % 2]
                    v.tensor_tensor(s0, s0, mx, ALU.mult)
                    v.tensor_tensor(s, s, mx.unsqueeze(2).broadcast_to([P, H, TC]), ALU.mult)\
                        .then_inc(sig("cos_probs_ready", NT).sem, 1)
                return step

            def cos_o_stats(t, chain):
                st, mv, rs = norms["cos_o"]

                def step(b, par):
                    if chain is cos_end:
                        chain.begin(b)
                    wait(dve, "cos_o_copied", b, t + 1, NT)
                    chain.link(v.bn_stats(st[:, t], cos_o[:, t]))
                    v.memset(spare, 0.0)
                    chain.link(v.bn_aggr(mv[:, t], st[:, t]))
                    v.tensor_scalar(rs[:, t:t + 1], mv[:, t, 1:2], EPS, None, ALU.add)\
                        .then_inc(sig("cos_o_stats", NT).sem, 1)
                return step

            def cos_o_add(t, chain):
                st, mv, rs = norms["cos_o"]

                def step(b, par):
                    wait(dve, "cos_o_rstd", b, t + 1, NT)
                    chain.link(v.scalar_tensor_tensor(out=cos_o[:, t], in0=cos_o[:, t], scalar=mv[:, t, 0:1],
                                                      in1=w["cos_go"], op0=ALU.subtract, op1=ALU.mult))
                    v.scalar_tensor_tensor(out=cos_o[:, t], in0=cos_o[:, t], scalar=rs[:, t:t + 1],
                                           in1=y4[:, par, t], op0=ALU.mult, op1=ALU.add)\
                        .then_inc(sig("cos_added", NT).sem, 1)
                    if t == NT - 1:
                        cos_end_added(b)
                    else:
                        v.memset(spare, 0.0)
                return step

            def cos_end_added(b):
                wait(dve, "cos_added", b, NT, NT)
                stats("cos", cos_end, cos_r)

            def cos_finish(b, par):
                scaled_rows("cos", b, y5, cos_r).then_inc(sig("y5_ready").sem, 1)
                wait(dve, "y5_ready", b)
                cos_end.end()

            def spec_add(b, par):
                spec.begin(b)
                spec.link(v.tensor_tensor(spec_r, y5, w["spec_b"].unsqueeze(1).broadcast_to([P, NT, C]), ALU.add))
                wait(dve, "spec_done", b)
                v.tensor_tensor(spec_r, rows2(0), spec_r, ALU.add).then_inc(sig("spec_added").sem, 1)
                wait(dve, "spec_added", b)
                stats("spec", spec, spec_r)

            def spec_finish(b, par):
                wait_previous(dve, "y_stored", b, 16)
                scaled_rows("spec", b, y6, spec_r).then_inc(sig("y6_ready").sem, 1)
                spec.end()

            def cos_slots_end(b, par):
                cos.end()

            def tile_steps(lo, t, ln):
                return [*[(2, cos_scale(t + 2))] * (t < 2), (1, met_mask(lo)),
                        *[(2, cos_max(t + 2))] * (t < 2), (1, met_mask(lo + 1)),
                        *[(2, cos_shift(t + 2))] * (t < 2), (1, met_mask(lo + 2)),
                        (2, cos_sum(t + 1)), (1, met_mask(lo + 3)), (2, cos_divide(t + 1)),
                        (2, cos_o_stats(ln, cos))]

            pipeline(dve, [(2, met_add), (0, dn_round(0)), (3, cos_o_stats(3, cos_end)), (0, dn_round(1)),
                           (2, met_norm), (3, cos_o_add(3, cos_end)), (0, dn_round(2)),
                           (2, met_norm2), (3, cos_finish), (0, dn_round(3)),
                           (0, dn_add), (3, spec_add), (0, dn_finish), (3, spec_finish),
                           (1, met_mask_queries(0)), (1, met_mask_states),
                           (2, cos_floor), (2, cos_scale(0)), (2, cos_max(0)), (1, met_mask(0)), (2, cos_shift(0)),
                           (2, cos_scale(1)), (2, cos_max(1)), (1, met_mask(1)), (2, cos_shift(1)),
                           (2, cos_sum(0)), (1, met_mask(2)), (2, cos_divide(0)), (1, met_mask(3)),
                           *tile_steps(4, 0, 0), (1, met_mask_queries(1)), (2, cos_o_add(0, cos)),
                           *tile_steps(8, 1, 1), (2, cos_o_add(1, cos)),
                           *tile_steps(12, 2, 2), (2, cos_o_add(2, cos)), (2, cos_slots_end)])


def kernel(**inputs):
    import concourse.bacc as bacc
    from concourse.bass_utils import run_bass_kernel_spmd

    a = {k: np.asarray(v) for k, v in inputs.items()}

    def rows(m):
        return m.reshape(-1, P, m.shape[-1]).transpose(1, 0, 2)

    def per_channel(vec):
        return vec.reshape(-1, P).T

    def on_all(vec):
        return np.broadcast_to(vec, (P, vec.shape[0]))

    def blocks(m):
        big = np.zeros((P, NC, P), m.dtype)
        for h in range(H):
            c, r = h // GH, h % GH * HD
            big[r:r + HD, c, r:r + HD] = m[h]
        return big

    p = np.arange(P)
    angle = 2 * np.pi * np.outer(np.arange(C), np.arange(C)) / C
    dft_r, dft_i = np.cos(angle).astype(np.float32), -np.sin(angle).astype(np.float32)
    f32 = lambda m: m.astype(np.float32)
    wkv = a["L1_xattn_Wkv"]
    null_v = np.zeros((P, NP, H), np.float32)
    for q in range(NP):
        null_v[:CD, q, 2 * q] = a["L1_xattn_null_kv"][1]
        null_v[CD:, q, 2 * q + 1] = a["L1_xattn_null_kv"][1]
    parts = {
        "ident": np.eye(P, dtype=np.float32),
        "ones": np.ones((P, P), np.float32),
        "lin_wq": rows(a["L0_attn_Wq"]),
        "lin_wkv": rows(np.concatenate([a["L0_attn_Wk"], a["L0_attn_Wv"]], 1)),
        "lin_bq": per_channel(a["L0_attn_bq"]),
        "lin_bkv": on_all(np.concatenate([a["L0_attn_bk"], a["L0_attn_bv"]])),
        "xat_wq": rows(a["L0_xattn_Wq"].T), "xat_bq": per_channel(a["L0_xattn_bq"]),
        "xat_wo": rows(a["L0_xattn_Wo"].T), "xat_bo": on_all(a["L0_xattn_bo"]),
        "blk32": f32(p[:, None] // LD == p // LD),
        "ctx": rows(a["ctx_1024"].reshape(B * TC, C)),
        "xat_wk": rows(a["L0_xattn_Wk"].T), "xat_bk": per_channel(a["L0_xattn_bk"]),
        "xat_wv": rows(a["L0_xattn_Wv"].T), "xat_bv": on_all(a["L0_xattn_bv"]),
        "head16": f32(p[:, None] // HD == np.arange(GH)),
        "pair16": f32(p[:, None] // CD == np.r_[np.arange(2 * HD) // HD, 0, 1]),
        "cos_wk": rows(wkv[:, :INNER]), "cos_wv": rows(wkv[:, INNER:]),
        "q_scale": np.tile(a["L1_xattn_q_scale"], 2)[:, None],
        "k_scale": np.tile(a["L1_xattn_k_scale"], 2)[:, None],
        "blk64": f32(p[:, None] // CD == p // CD),
        "null_row": on_all(a["L1_xattn_null_kv"][0]), "q_row": on_all(a["L1_xattn_q_scale"]),
        "k_row": on_all(a["L1_xattn_k_scale"]),
        "w_up": rows(a["L0_ffn_w_up"]), "w_gate": rows(a["L0_ffn_w_gate"]),
        "w_down": rows(a["L0_ffn_w_down"]),
        "met_wp": rows(a["L1_attn_W_proj"].T), "cos_wq": rows(a["L1_xattn_Wq"]),
        "cos_gn": per_channel(a["L1_xattn_g_norm"]), "cos_wo": rows(a["L1_xattn_Wout"]),
        "cos_go": on_all(a["L1_xattn_g_out"]), "half64": f32(p[:, None] // CD == np.arange(2)),
        "blk16": f32(p[:, None] // HD == p // HD), "causal": f32(p[:, None] <= p),
        "spec_b": on_all(a["L1_ffn_bias"]), "mhead16": f32(p[:, None] // HD == np.arange(GH)),
        "met_pt": blocks(a["L1_attn_pre_metric_nkk"].transpose(0, 2, 1)),
        "met_tt": blocks(a["L1_attn_transforms_nkk"].transpose(0, 2, 1)),
        "met_wm": rows(a["L1_attn_W_mixer"].T), "null_v": null_v,
        "dft_r": rows(dft_r), "dft_i": rows(dft_i), "dft_ni": rows(-dft_i),
        "spec_wr": rows(a["L1_ffn_w_freq_real"]), "spec_wi": rows(a["L1_ffn_w_freq_imag"]),
    }
    arrays = {"x": np.ascontiguousarray(a["x"])}
    for name, pack in PACKS.items():
        arrays[name] = np.ascontiguousarray(
            np.concatenate([parts[n].reshape(P, -1) for n, _ in pack], 1).astype(np.float32))

    nc = bacc.Bacc("TRN2", target_bir_lowering=False, num_devices=1)
    args = [nc.dram_tensor(n, m.shape, F32, kind="ExternalInput").ap() for n, m in arrays.items()]
    args.append(nc.dram_tensor("y", (B, T, C), F32, kind="ExternalOutput").ap())
    decoder(nc, *args)
    result = run_bass_kernel_spmd(nc, [arrays], core_ids=[0])
    return result.results[0]["y"]
```

```python
import numpy as np
import concourse.bass as bass
from concourse import mybir
from contextlib import ExitStack

F32 = mybir.dt.float32
I16 = mybir.dt.int16
U16 = mybir.dt.uint16
ALU = mybir.AluOpType
ACT = mybir.ActivationFunctionType
AX = mybir.AxisListType

P = 128
B, T, C = 8, 512, 256
NT = T // P
NC = C // P
TC = 64
LD = 32
H = 16
HD = C // H
GH = P // HD
FF = 768
NF = FF // P
BLK = 32
CD = 64
INNER = H * CD
NP = H // 2
EPS = 1e-5
QMAX = 32767.0
MAGIC = 12582912.0


class Batch:

    def __init__(self, off, reg=None):
        self.off, self.reg = off, reg

    def lin(self, k, c):
        return k * self.off + c if self.reg is None else self.reg * (2 * k) + (k * self.off + c)

    def half(self, k, c):
        return (k * (self.off // 2) + c if self.reg is None
                else self.reg * k + (k * (self.off // 2) + c))

    def before(self, n):
        return self.reg is None and self.off < n

    def first(self):
        return self.reg is None and self.off == 0

    def last(self):
        return self.reg is None and self.off == B - 1


class Signal:

    def __init__(self, sem, per, base=0):
        self.sem, self.per, self.base = sem, per, base

    def at(self, b, j):
        return b.lin(self.per, self.base + j)


CONTINUES = {
    "ffn_x_turned": "lin_x_turned", "ffn_x_copied": "lin_x_copied",
    "dn_turned": "lin_y_turned", "dn_copied": "lin_y_copied", "y3_ready": "y1_ready", "y5_ready": "y2_ready",
    "met_q_done": "lin_q_projected", "met_q_ready": "lin_q_ready", "met_state_done": "lin_state_done",
    "met_states_ready": "lin_kv_ready", "met_added": "lin_added", "met_stats": "lin_stats",
    "met_rstd": "lin_rstd", "met_projected": "xat_q_projected", "met_p_ready": "xat_q_biased",
    "dn_projected": "lin_kv_projected", "dn_v_scaled": "lin_kv_biased", "dn_v_rounded": "lin_scaled",
    "cos_scored": "xat_scored", "cos_exp_done": "xat_exp_done",
    "cos_turned": "xat_probs_turned", "cos_pt_copied": "xat_probs_copied",
    "cos_out_done": "xat_weighted", "cos_o_copied": "xat_normed", "spec_done": "xat_out_projected",
    "spec_added": "xat_out_added", "cos_stats": "xat_stats", "cos_rstd": "xat_rstd",
    "y_stored": "x3_stored", "ffn_peaked": "lin_q_negative",
    "sigmoid_done": "lin_q_exp", "up_rounded": "lin_k_ready", "ffn_x_scaled": "lin_k_exp",
    "cos_x_turned": "xat_o_turned", "cos_x_copied": "xat_o_copied", "cos_probs_ready": "lin_out_done",
}
MOVES_ON = {"ffn_x_loaded": ("x_loaded", 1), "up_loaded": ("x_loaded", 2), "dn_x_loaded": ("x_loaded", 3),
            "up_stored": ("ck_stored", 1), "v_stored": ("ck_stored", 2)}


class Chain:

    def __init__(self, eng, sem, per, after=None):
        self.eng, self.per = eng, per
        self.base = after.base + B * after.per if after else 0
        self.sem = after.sem if after else sem

    def begin(self, b):
        self.b, self.j = b, 0

    def link(self, ins):
        self.j += 1
        ins.then_inc(self.sem, 1)
        self.eng.wait_ge(self.sem, self.b.lin(self.per, self.base + self.j))

    def end(self):
        assert self.j == self.per, (self.sem, self.j, self.per)


def pipeline(eng, steps):
    last = max(s for s, _ in steps)
    first = last // 2 * 2 + 2

    def peeled(n):
        for skew, fn in steps:
            if 0 <= n - skew < B:
                fn(Batch(n - skew), (n - skew) % 2)

    for n in range(first):
        peeled(n)
    with eng.Fori(first // 2, B // 2) as i:
        for half in range(2):
            for skew, fn in steps:
                fn(Batch(half - skew, i), (half - skew) % 2)
    for n in range(B, B + last):
        peeled(n)


class Arena:

    def __init__(self, tensor, words):
        self.t, self.words, self.at, self.top = tensor, words, 0, 0

    def take(self, *dims, dtype=F32):
        n = int(np.prod(dims))
        words = n if dtype == F32 else (n + 1) // 2
        a = self.t[:, self.at:self.at + words]
        self.at += words
        self.top = max(self.top, self.at)
        assert self.at <= self.words, (self.at, self.words)
        if dtype != F32:
            a = a.bitcast(dtype)
        names = "abcdef"[:len(dims)]
        if len(dims) > 1:
            kw = {x: d for x, d in zip(names, dims)}
            a = a.rearrange(f"p ({' '.join(names)}) -> p {' '.join(names)}", **kw)
        return a


PACK_IDENT = [("ident", (P,)), ("ones", (P,))]
PACK_LIN = [("lin_wq", (NC, C)), ("lin_wkv", (NC, 2 * C)), ("lin_bq", (NC,)), ("lin_bkv", (2 * C,)),
            ("xat_wq", (NC, C)), ("xat_bq", (NC,)), ("xat_wo", (NC, C)), ("xat_bo", (C,)),
            ("blk32", (P,))]
PACK_CTX = [("ctx", (B * TC // P, C))]
PACK_KEY = [("xat_wk", (NC, C)), ("xat_bk", (NC,)), ("cos_wk", (NC, INNER)), ("head16", (GH,)),
            ("q_scale", (1,)), ("k_scale", (1,)), ("heads", (NP, H))]
PACK_VAL = [("head_rows", (NP, P)), ("xat_wv", (NC, C)), ("xat_bv", (C,)), ("pair16", (2 * HD + 2,)),
            ("cos_wv", (NC, INNER)),
            ("null_row", (CD,)), ("q_row", (CD,)), ("k_row", (CD,))]
PACK_FFN = [("w_up", (NF, C)), ("w_gate", (NF, C)), ("w_down", (NC, FF))]
PACK_L1 = [("met_wp", (NC, C)), ("cos_wq", (NC, INNER)), ("cos_gn", (NC,)), ("cos_wo", (NP, C)),
           ("cos_go", (C,)), ("half64", (2,)), ("blk16", (P,)), ("causal", (P,)), ("spec_b", (C,)),
           ("mhead16", (GH,))]
PACK_PREP = [("met_pt", (NC, P)), ("met_tt", (NC, P)), ("met_wm", (NC, C)), ("null_v", (NP, H)),
             ("dft_r", (NC, C)), ("dft_i", (NC, C)), ("dft_ni", (NC, C)),
             ("spec_wr", (NC, C)), ("spec_wi", (NC, C))]
PACKS = {"pack_ident": PACK_IDENT, "pack_lin": PACK_LIN, "pack_ctx": PACK_CTX,
         "pack_key": PACK_KEY, "pack_val": PACK_VAL, "pack_ffn": PACK_FFN,
         "pack_l1": PACK_L1, "pack_prep": PACK_PREP}


def width(pack):
    return sum(int(np.prod(d)) for _, d in pack)


def decoder(nc, x_in, pack_ident, pack_lin, pack_ctx, pack_key, pack_val, pack_ffn, pack_l1,
            pack_prep, out):
    x_rows = x_in.rearrange("b (t p) c -> b p t c", p=P)
    out_rows = out.rearrange("b (t p) c -> b p t c", p=P)
    ctx = ExitStack()
    with ctx:
        def sem(name):
            return ctx.enter_context(nc.semaphore(name))

        x3_d = nc.dram_tensor("x3_scratch", (B, P, NT * C), F32).ap()
        up_d = nc.dram_tensor("up_scratch", (B, P, NF * T), F32).ap()
        v_d = nc.dram_tensor("v_scratch", (B, NT * P, NF * P), F32).ap()
        ck_d = nc.dram_tensor("ck_scratch", (P, NP, B * TC), F32).ap()
        cv_d = nc.dram_tensor("cv_scratch", (P, NP, B * TC), F32).ap()

        WORDS = 53200
        arena_t = ctx.enter_context(nc.sbuf_tensor("arena", [P, WORDS], F32))
        ar = Arena(arena_t, WORDS)
        ps = ctx.enter_context(nc.psum_tensor("ps", [P, 8, 512], F32))

        def take_pack(pack):
            base = ar.at
            views = {n: ar.take(*d) for n, d in pack}
            return arena_t[:, base:ar.at], views

        def bank(k, n=1):
            return ps[:, k:k + n, :]

        ident_all, w = take_pack(PACK_IDENT)
        ident = w["ident"]
        small = ar.take(64)
        quant = {n: small[:, k:k + 1] for k, n in enumerate(
            ["tmp", "x_max", "up_max", "gate_max", "t_max", "v_max", "floor",
             "x_all", "up_all", "gate_all", "t_all", "v_all",
             "x_scale", "up_scale", "gate_scale", "t_scale", "v_scale",
             "x_mult", "up_mult", "gate_mult", "t_mult", "v_mult", "t_raw", "v_raw"])}
        peaks = small[:, 32:34]
        neghalf = ar.take(64)
        spare = ar.take(1)
        wup_t = ar.take(NC, FF)
        kraw_rest = arena_t[:, ar.at:ar.at + (NP - 2) * B * TC].rearrange("p (a b) -> p a b", b=B * TC)
        wgate_t = ar.take(NC, FF)
        wdown_t = ar.take(NF, C)
        l1_all, w1 = take_pack(PACK_L1)
        w.update(w1)
        met_m = ar.take(NC, P)
        met_wo = ar.take(NC, C)
        spec_m = ar.take(NC, C)
        null_w = ar.take(C)
        null_wq = ar.take(NC, H)
        keep = ar.at

        kbd = ar.take(NC, B, GH, TC)
        vbd = ar.take(B, NP, 2 * HD + 2)
        lin_all, w2 = take_pack(PACK_LIN)
        w.update(w2)
        loop1 = ar.at
        ctx_all, w3 = take_pack(PACK_CTX)
        w.update(w3)
        key_all, w6 = take_pack(PACK_KEY)
        w.update(w6)
        val_all, w7 = take_pack(PACK_VAL)
        w.update(w7)
        prep_all, w4 = take_pack(PACK_PREP)
        w.update(w4)
        ffn_all, w5 = take_pack(PACK_FFN)
        w.update(w5)
        ctx_t = ar.take(NC, B, TC)
        ctx_t2 = ar.take(NC, B, 2, TC)
        kt = ar.take(NC, B, TC)
        vst = kt.rearrange("p a b c -> p a (b c)")
        kraw = ar.take(2, B * TC)
        ksq = ar.take(2, B * TC)
        krn = ar.take(B * TC)
        kst = ar.take(2, B * TC)
        qmag = ar.take(NF * C // BLK)
        qrec = ar.take(NF * C // BLK)
        vtmp = ar.take(B, C)
        at_r = ar.take(NC, C)
        at_i = ar.take(NC, C)
        gk = ar.take(1)
        null_k = ar.take(CD)
        null_n = ar.take(1)
        null_p = vtmp.rearrange("p a b -> p (a b)")[:, 0:INNER].rearrange("p (h k) -> p h k", h=H)
        ar.at = loop1
        lin_x = ar.take(2, NT, C)
        lin_xt = ar.take(2, NC, T)
        lin_zq = ar.take(NC, T)
        lin_eq = ar.take(NC, T)
        lin_q = ar.take(NC, T)
        lin_z = ar.take(NT, 2 * C)
        lin_ek = ar.take(NT, C)
        lin_k = ar.take(NT, C)
        lin_kv = ar.take(NC, P + P // LD)
        lin_den = ar.take(2, NC, P // LD)
        lin_r = ar.take(NT, C)
        y1 = ar.take(2, NT, C)
        xt1 = ar.take(NC, T)
        xat_q = ar.take(NC, T)
        xat_s = ar.take(2, H, TC)
        xat_mx = ar.take(2, H)
        xat_pt = ar.take(NP, P)
        xat_rec = ar.take(H)
        xat_o = ar.take(NT, C)
        xat_ot = ar.take(NC, T)
        xat_r = ar.take(NT, C)
        y2 = ar.take(2, NT, C)
        lin_st = ar.take(NT, 6)
        lin_mv = ar.take(NT, 2)
        lin_rs = ar.take(NT)
        xat_st = ar.take(NT, 6)
        xat_mv = ar.take(NT, 2)
        xat_rs = ar.take(NT)
        ar.at = keep
        gated = ar.take(B, NT * NF * P)
        passes = ar.at
        ffn_x = ar.take(2, NT, C)
        ffn_xt = ar.take(2, NC, T)
        ffn_up = ar.take(2, NT, NF, P)
        ar.at = passes
        gate_i = ar.take(2, NF * T, dtype=I16)
        sig_f = ar.take(2, NF * T)
        sig_i = ar.take(2, NF * T, dtype=U16)
        passes_end = ar.at
        ar.at = passes
        up_i = ar.take(2, NF * T, dtype=I16)
        t_i = ar.take(2, NF * T, dtype=I16)
        ar.at = passes_end - NF * T
        up_f = ar.take(2, NF * T)
        ar.at = keep
        dn_v = ar.take(NT, NF, P)
        dn_x = ar.take(2, NT, C)
        y3 = ar.take(2, NT, C)
        xt3 = ar.take(NC, T)
        met_p = ar.take(NC, T)
        met_pr = ar.take(NT, C)
        met_q = ar.take(NC, T)
        met_qh = ar.take(GH, T)
        met_st = ar.take(NC, NT - 1, P)
        met_s = ar.take(2, 4, P)
        met_o = ar.take(NT, C)
        met_ot = ar.take(NC, T)
        met_r = ar.take(NT, C)
        y4 = ar.take(2, NT, C)
        xn4 = met_r
        xt4 = ar.take(NC, T)
        cos_kb = ar.take(2, NP, P)
        cos_vb = ar.take(2, NP, P)
        cos_vw = ar.take(NP, C)
        cos_q = ar.take(NP, T)
        cos_sq = ar.take(2, T)
        cos_nn = ar.take(NT, 2 * H)
        cos_s = ar.take(2, H * TC + H)
        cos_mx = ar.take(2, H)
        cos_pt = ar.take(NP, P)
        cos_p0 = ar.take(P)
        cos_o = ar.take(NT, C)
        cos_r = spec_r = cos_o
        y5 = ar.take(NT, C)
        xt5 = cos_q[:, 0:NC]
        y6 = ar.take(NT, C)
        norms = {n: (ar.take(NT, 6), ar.take(NT, 2), ar.take(NT)) for n in
                 ("dn", "met", "met2", "cos_o", "cos", "spec")}
        sems = {}

        def ev(name):
            if name not in sems:
                sems[name] = sem(name)
            return sems[name]

        loaded = {n: sem(f"{n}_loaded") for n in PACKS}
        sigs = {}

        def sig(name, per=1):
            if name not in sigs:
                if name in CONTINUES:
                    before = sig(CONTINUES[name], per)
                    sigs[name] = Signal(before.sem, per, before.base + B * per)
                else:
                    sigs[name] = Signal(sem(name), per)
            assert sigs[name].per == per, name
            return sigs[name]

        def wait(eng, name, b, j=None, per=1):
            s = sig(name, per)
            eng.wait_ge(s.sem, s.at(b, per if j is None else j))

        def wait_previous(eng, name, b, per=1):
            if not b.first():
                eng.wait_ge(sig(name, per).sem, sig(name, per).at(b, 0))

        QUANTIZED = {n: k + 1 for k, n in enumerate(("x", "up", "gate", "t", "v"))}
        WEIGHTS = {n: k + 1 for k, n in enumerate(("w_up", "w_gate", "w_down"))}

        def moved(name, par):
            return ev(f"{MOVES_ON.get(name, (name, 0))[0]}_{par}")

        def moved_before(name):
            return 16 * (B // 2) * MOVES_ON.get(name, (name, 0))[1]

        def wait_moved(eng, name, b, par, back=0):
            if not b.before(back):
                eng.wait_ge(moved(name, par), b.half(16, moved_before(name) + 16 - 8 * back))

        def wait_all_moved(eng, name):
            for par in range(2):
                eng.wait_ge(moved(name, par), moved_before(name) + 16 * (B // 2))

        def wait_back(eng, name, b, back, per=1):
            if not b.before(back):
                eng.wait_ge(sig(name, per).sem, sig(name, per).at(b, per * (1 - back)))

        def wait_next(eng, name, b, j=1, per=1):
            if not b.last():
                eng.wait_ge(sig(name, per).sem, sig(name, per).at(b, per + j))

        def at_batch(ap, b):
            return ap[b.off] if b.reg is None else ap[bass.ds(b.lin(1, 0), 1)].squeeze(0)

        def at_cols(ap, b):
            return ap[:, b.off] if b.reg is None else ap[:, bass.ds(b.lin(1, 0), 1)].squeeze(1)

        block = ctx.enter_context(nc.Block())

        class Line:

            def __init__(self, eng, name):
                self.eng, self.sem, self.n = eng, sem(name), 0

            def link(self, ins):
                self.n += 1
                ins.then_inc(self.sem, 1)
                self.eng.wait_ge(self.sem, self.n)

        def rows2(k, n=2):
            return bank(k, n).rearrange("p a (b c) -> p (a b) c", c=C)

        def heads(t):
            return cos_s[:, t % 2, 0:H * TC].rearrange("p (h k) -> p h k", h=H), cos_s[:, t % 2, H * TC:]

        def flat(k, n=1):
            return bank(k, n).rearrange("p a c -> p (a c)")

        LIN_BANKS = (0, 3, 1, 2)

        @block.sync
        def _(sp):
            for sbuf, dram, name in ((ctx_all, pack_ctx, "pack_ctx"), (ident_all, pack_ident, "pack_ident"),
                                     (key_all, pack_key, "pack_key"), (ffn_all, pack_ffn, "pack_ffn"),
                                     (val_all, pack_val, "pack_val"), (prep_all, pack_prep, "pack_prep"),
                                     (l1_all, pack_l1, "pack_l1"), (lin_all, pack_lin, "pack_lin")):
                sp.dma_start(sbuf, dram).then_inc(loaded[name], 16)
            for p in range(NP):
                sp.wait_ge(ev("cos_k_scaled"), p + 1)
                sp.dma_start(ck_d[:, p, :], kst[:, p % 2, :]).then_inc(moved("ck_stored", p % 2), 16)

            def load_x(b, par):
                if b.first():
                    sp.wait_ge(ev("ctx_transposed"), 1)
                elif b.before(2):
                    sp.wait_ge(ev("prep_done"), 3)
                    wait_all_moved(sp, "ck_stored")
                    wait_all_moved(sp, "cv_stored")
                wait_back(sp, "y1_ready", b, 2)
                sp.dma_start(lin_x[:, par], at_batch(x_rows, b)).then_inc(moved("x_loaded", par), 16)

            def store_x3(b, par):
                wait(sp, "y2_ready", b)
                sp.dma_start(at_batch(x3_d, b), y2[:, par]).then_inc(sig("x3_stored", 16).sem, 16)

            pipeline(sp, [(0, load_x), (2, store_x3)])
            sp.wait_ge(sig("x3_stored", 16).sem, 16 * B)

            sp.wait_ge(ev("scale_ready"), QUANTIZED["x"])

            def ffn_load_x(b, par):
                wait_back(sp, "ffn_x_turned", b, 2)
                sp.dma_start(ffn_x[:, par].rearrange("p a b -> p (a b)"), at_batch(x3_d, b))\
                    .then_inc(moved("ffn_x_loaded", par), 16)

            def ffn_store_up(b, par):
                wait(sp, "up_copied", b, NF, NF)
                sp.dma_start(at_batch(up_d, b), ffn_up[:, par].rearrange("p a b c -> p (a b c)"))\
                    .then_inc(moved("up_stored", par), 16)

            pipeline(sp, [(0, ffn_load_x), (2, ffn_store_up)])
            wait_all_moved(sp, "up_stored")
            sp.wait_ge(ev("scale_ready"), QUANTIZED["up"])

            def ffn_load_up(b, par):
                wait_back(sp, "up_rounded", b, 2)
                if not b.before(1) and b.before(2):
                    sp.wait_ge(ev("scale_ready"), QUANTIZED["t"])
                sp.dma_start(up_f[:, 1 - par], at_batch(up_d, b)).then_inc(moved("up_loaded", par), 16)

            v_rows = v_d.rearrange("b (t p) n -> b p t n", t=NT)

            def ffn_store_v(b, par):
                wait(sp, "v_ready", b)
                sp.dma_start(at_batch(v_rows, b), at_cols(gated, b).rearrange("p (t n) -> p t n", t=NT))\
                    .then_inc(moved("v_stored", par), 16)

            pipeline(sp, [(0, ffn_load_up), (1, ffn_store_v)])
            wait_all_moved(sp, "v_stored")

            sp.wait_ge(ev("scale_ready"), QUANTIZED["v"])

            def dn_load(b, par):
                wait_back(sp, "y3_ready", b, 2)
                sp.dma_start(dn_x[:, par].rearrange("p a b -> p (a b)"), at_batch(x3_d, b))\
                    .then_inc(moved("dn_x_loaded", par), 16)
                if b.first():
                    return
                wait_previous(sp, "dn_projected", b, NT)
                sp.dma_start(dn_v.rearrange("p a b c -> p a (b c)"), at_batch(v_rows, b))\
                    .then_inc(moved("v_loaded", par), 16)

            def cos_load(b, par):
                at = bass.ds(b.lin(TC, 0) if b.reg is None else sp.snap(b.lin(TC, 0)), TC)
                if b.first():
                    sp.wait_ge(ev("pads_cleared"), 2)
                wait_back(sp, "cos_scored", b, 2, NT)
                for lo, hi in ((0, CD), (CD, P)):
                    sp.dma_start(cos_kb[lo:hi, par, :, lo:hi], ck_d[lo:hi, :, at])\
                        .then_inc(moved("cos_kv_loaded", par), 16)
                    sp.dma_start(cos_vb[lo:hi, par, :, lo:hi], cv_d[lo:hi, :, at])\
                        .then_inc(moved("cos_kv_loaded", par), 16)

            def store_y(b, par):
                wait(sp, "y6_ready", b)
                sp.dma_start(at_batch(out_rows, b), y6).then_inc(sig("y_stored", 16).sem, 16)

            pipeline(sp, [(2, cos_load), (0, dn_load), (3, store_y)])
            sp.wait_ge(sig("y_stored", 16).sem, 2 * 16 * B)

        @block.tensor
        def _(pe):
            mm = nc.tensor.matmul
            tr = nc.tensor.transpose

            pe.wait_ge(loaded["pack_ident"], 16)
            pe.wait_ge(loaded["pack_ctx"], 16)
            for c in range(NC):
                for t in range(NT):
                    last = tr(bank(c)[:, 0, t * P:(t + 1) * P], w["ctx"][:, t, c * P:(c + 1) * P], ident)
            last.then_inc(ev("ctx_transposed"), 1)
            pe.wait_ge(ev("ctx_t_ready"), 1)

            def from_ctx(out_ap, lhs, c0, n=P, rhs=None):
                for k in range(NC):
                    r = mm(out_ap, lhs[:, k, c0:c0 + n], ctx_t[:, k].rearrange("p a b -> p (a b)"),
                           start=k == 0, stop=k == NC - 1)
                return r

            pe.wait_ge(loaded["pack_key"], 16)
            for c in range(NC):
                last = from_ctx(flat(2 + c), w["xat_wk"], c * P)
            last.then_inc(ev("xat_k_projected"), 1)
            def turn(first, name, rows, cols):
                pe.wait_ge(ev("weight_quantized"), WEIGHTS[name])
                for k in range(cols):
                    for r in range(rows):
                        at = (k * rows + r) * P
                        last = tr(flat(first, 3)[:, at:at + P], w[name][:, r, k * P:(k + 1) * P], ident)
                last.then_inc(ev("weight_turned"), 1)

            for p in range(NP + 1):
                if p < NP:
                    if p >= 2:
                        pe.wait_ge(ev("cos_k_squared"), p - 1)
                    from_ctx(flat(4 + p % 2), w["cos_wk"], p * P).then_inc(ev("cos_k_projected"), 1)
                if p >= 1:
                    pe.wait_ge(ev("cos_k_squared"), p)
                    last = mm(flat(6)[0:H], w["heads"][:, p - 1], ksq[:, (p - 1) % 2, :], start=p == 1,
                              stop=p == NP)
            last.then_inc(ev("cos_k_normed"), 1)
            pe.wait_ge(ev("xat_k_biased"), 1)
            turn(0, "w_up", NF, NC)
            pe.wait_ge(ev("weight_copied"), WEIGHTS["w_up"])
            pe.wait_ge(loaded["pack_val"], 16)
            for p in range(NP):
                if p >= 2:
                    pe.wait_ge(ev("cos_v_copied"), p - 1)
                from_ctx(flat(p % 2), w["cos_wv"], p * P).then_inc(ev("cos_v_projected"), 1)
            pe.wait_ge(ev("cos_k_inverted"), 1)
            for p in range(NP):
                if p >= 2:
                    pe.wait_ge(ev("cos_k_scaled"), p - 1)
                mm(flat(6 + p % 2), w["head_rows"][0:H, p], krn[0:H], start=True, stop=True)\
                    .then_inc(ev("cos_k_spread"), 1)
            pe.wait_ge(ev("ctx_t2_ready"), NC)
            pe.wait_ge(ev("cos_k_scaled"), NP)
            for b in range(B):
                for k in range(NC):
                    last = mm(rows2(4, 4)[:, b, :], ctx_t2[:, k, b].rearrange("p a b -> p (a b)"),
                              w["xat_wv"][:, k, :], start=k == 0, stop=k == NC - 1)
            last.then_inc(ev("xat_v_projected"), 1)
            pe.wait_ge(ev("cos_v_copied"), NP)
            turn(0, "w_gate", NF, NC)
            pe.wait_ge(loaded["pack_prep"], 16)
            pe.wait_ge(loaded["pack_l1"], 16)
            for c in range(NC):
                mm(flat(3)[:, c * P:(c + 1) * P], w["met_pt"][:, c], w["met_pt"][:, c], start=True, stop=True)
            for p in range(NP):
                last = mm(flat(3)[0:H, C:2 * C], w["null_v"][:, p, :], w["cos_wo"][:, p, :],
                          start=p == 0, stop=p == NP - 1)
            last.then_inc(ev("metric_product"), 1)
            pe.wait_ge(ev("xat_v_biased"), 1)
            for c in range(NC):
                last = mm(rows2(7, 1)[:, c], w["met_tt"][:, c], w["met_wm"][:, c], start=True, stop=True)
            last.then_inc(ev("mixer_product"), 1)
            for o in range(NC):
                for n, (wt, dft) in enumerate((("spec_wr", "dft_r"), ("spec_wi", "dft_ni"))):
                    for k in range(NC):
                        mm(rows2(5, 1)[:, o], w[wt][:, k, o * P:(o + 1) * P], w[dft][:, k],
                           start=n == k == 0, stop=n == k == 1)
            for o in range(NC):
                for n, (wt, dft) in enumerate((("spec_wr", "dft_i"), ("spec_wi", "dft_r"))):
                    for k in range(NC):
                        last = mm(rows2(6, 1)[:, o], w[wt][:, k, o * P:(o + 1) * P], w[dft][:, k],
                                  start=n == k == 0, stop=n == k == 1)
            last.then_inc(ev("spec_forward"), 1)
            pe.wait_ge(ev("weight_copied"), WEIGHTS["w_gate"])
            turn(0, "w_down", NC, NF)
            pe.wait_ge(ev("spec_forward_copied"), 2)
            for i in range(NC):
                for n, at in enumerate((at_r, at_i)):
                    for k in range(NC):
                        last = mm(rows2(4, 1)[:, i], at[:, k, i * P:(i + 1) * P],
                                  w[("dft_r", "dft_i")[n]][:, k], start=n == k == 0, stop=n == k == 1)
            last.then_inc(ev("spec_product"), 1)

            pe.wait_ge(ev("weight_copied"), WEIGHTS["w_down"])
            pe.wait_ge(loaded["pack_lin"], 16)
            pe.wait_ge(ev("kbd_ready"), 1)

            def lin_turn_x(b, par):
                wait_moved(pe, "x_loaded", b, par)
                if not b.first():
                    pe.wait_ge(sig("lin_scaled", NT).sem, sig("lin_scaled", NT).at(b, -1))
                for c in range(NC):
                    for t in range(NT):
                        last = tr(flat(c)[:, t * P:(t + 1) * P], lin_x[:, par, t, c * P:(c + 1) * P], ident)
                last.then_inc(sig("lin_x_turned").sem, 1)

            def lin_project_q(c):
                def step(b, par):
                    wait_previous(pe, "lin_scaled", b, NT)
                    for k in range(NC):
                        last = mm(flat(2 + c), w["lin_wq"][:, k, c * P:(c + 1) * P], lin_xt[:, par, k],
                                  start=k == 0, stop=k == NC - 1)
                    if c == NC - 1:
                        last.then_inc(sig("lin_q_projected").sem, 1)
                return step

            def lin_project_kv(t):
                def step(b, par):
                    if t == 0:
                        wait(pe, "lin_x_copied", b)
                    if t >= 2:
                        wait(pe, "lin_kv_biased", b, t - 1, NT)
                    for k in range(NC):
                        last = mm(flat(t % 2), lin_xt[:, par, k, t * P:(t + 1) * P], w["lin_wkv"][:, k],
                                  start=k == 0, stop=k == NC - 1)
                    last.then_inc(sig("lin_kv_projected", NT).sem, 1)
                return step

            def lin_state(b, par):
                wait(pe, "lin_k_ready", b)
                wait(pe, "lin_q_biased", b)
                for c in range(NC):
                    for t in range(NT):
                        mm(flat(2)[:, c * P:(c + 1) * P], lin_k[:, t, c * P:(c + 1) * P],
                           lin_z[:, t, C + c * P:C + (c + 1) * P], start=t == 0, stop=t == NT - 1)
                for c in range(NC):
                    for t in range(NT):
                        last = mm(flat(2)[:, C + c:C + c + 1], lin_k[:, t, c * P:(c + 1) * P],
                                  w["ones"][:, 0:1], start=t == 0, stop=t == NT - 1)
                last.then_inc(sig("lin_state_done").sem, 1)

            def lin_out(b, par):
                wait(pe, "lin_kv_ready", b)
                wait(pe, "lin_q_ready", b)
                for t in range(NT):
                    if LIN_BANKS[t] == 3 and not b.first():
                        pe.wait_ge(sig("xat_normed", NT).sem, sig("xat_normed", NT).at(b, -1))
                    for c in range(NC):
                        last = mm(flat(LIN_BANKS[t])[:, c * 132:c * 132 + 132],
                                  lin_q[:, c, t * P:(t + 1) * P], lin_kv[:, c], start=True, stop=True)
                    last.then_inc(sig("lin_out_done", NT).sem, 1)

            def lin_turn_y(b, par):
                wait(pe, "y1_ready", b)
                wait_previous(pe, "xat_o_copied", b)
                for c in range(NC):
                    for t in range(NT):
                        last = tr(flat(6 + c)[:, t * P:(t + 1) * P], y1[:, par, t, c * P:(c + 1) * P], ident)
                last.then_inc(sig("lin_y_turned").sem, 1)

            def xat_project_q(b, par):
                wait(pe, "lin_y_copied", b)
                wait_previous(pe, "xat_out_added", b)
                for c in range(NC):
                    for k in range(NC):
                        last = mm(flat(4 + c), w["xat_wq"][:, k, c * P:(c + 1) * P], xt1[:, k],
                                  start=k == 0, stop=k == NC - 1)
                last.then_inc(sig("xat_q_projected").sem, 1)

            def xat_scores(t):
                def step(b, par):
                    if t == 0:
                        wait(pe, "xat_q_biased", b)
                    else:
                        wait(pe, "xat_shifted", b, t, NT)
                    for c in range(NC):
                        keys = (kbd[:, c, bass.ds(b.lin(1, 0), 1)] if b.reg is not None
                                else kbd[:, c, b.off:b.off + 1])
                        last = mm(flat(4 + c), xat_q[:, c, t * P:(t + 1) * P],
                                  keys.rearrange("p o h k -> p (o h k)"), start=True, stop=True)
                    last.then_inc(sig("xat_scored", NT).sem, 1)
                return step

            def xat_turn_probs(t):
                def step(b, par):
                    wait(pe, "xat_exp_done", b, t + 1, NT)
                    if t == 0:
                        wait(pe, "lin_y_copied", b)
                    for p in range(NP):
                        last = tr(flat(6, 2)[:, p * P:(p + 1) * P],
                                  xat_s[:, t % 2, 2 * p:2 * p + 2].rearrange("p a b -> p (a b)"), ident)
                    last.then_inc(sig("xat_probs_turned", NT).sem, 1)
                return step

            def xat_values(t):
                def step(b, par):
                    wait(pe, "xat_probs_copied", b, t + 1, NT)
                    if t == 0:
                        wait_next(pe, "lin_q_biased", b)
                    else:
                        wait(pe, "xat_normed", b, t, NT)
                    if t == NT - 1:
                        wait_next(pe, "lin_scaled", b, LIN_BANKS.index(3) + 1, NT)
                    for p in range(NP):
                        vals = (vbd[:, bass.ds(b.lin(1, 0), 1), p] if b.reg is not None
                                else vbd[:, b.off:b.off + 1, p])
                        last = mm(flat(3)[:, p * 34:p * 34 + 34], xat_pt[:, p],
                                  vals.rearrange("p o n -> p (o n)"), start=True, stop=True)
                    last.then_inc(sig("xat_weighted", NT).sem, 1)
                return step

            def xat_turn_o(b, par):
                wait(pe, "xat_normed", b, NT, NT)
                for c in range(NC):
                    for t in range(NT):
                        last = tr(flat(6 + c)[:, t * P:(t + 1) * P], xat_o[:, t, c * P:(c + 1) * P], ident)
                last.then_inc(sig("xat_o_turned").sem, 1)

            def xat_project_o(b, par):
                wait(pe, "xat_o_copied", b)
                for t in range(NT):
                    for k in range(NC):
                        last = mm(rows2(4)[:, t], xat_ot[:, k, t * P:(t + 1) * P], w["xat_wo"][:, k],
                                  start=k == 0, stop=k == NC - 1)
                last.then_inc(sig("xat_out_projected").sem, 1)

            pipeline(pe, [(0, lin_turn_x), (2, xat_turn_o), (0, lin_project_kv(0)), (2, xat_project_o),
                          (1, lin_turn_y), (0, lin_project_kv(1)), (0, lin_project_kv(2)),
                          (1, xat_project_q), (0, lin_project_kv(3)), (1, xat_scores(0)),
                          (0, lin_project_q(0)), (1, xat_scores(1)),
                          (1, xat_turn_probs(0)), (0, lin_project_q(1)), (1, xat_scores(2)), (1, xat_values(0)),
                          (1, xat_turn_probs(1)), (1, xat_scores(3)), (1, xat_values(1)),
                          (1, xat_turn_probs(2)), (0, lin_state), (1, xat_values(2)),
                          (1, xat_turn_probs(3)), (0, lin_out), (1, xat_values(3))])

            def ffn_turn_x(b, par):
                wait(pe, "ffn_x_rounded", b)
                wait_previous(pe, "ffn_x_copied", b)
                for c in range(NC):
                    for t in range(NT):
                        last = tr(flat(c)[:, t * P:(t + 1) * P], ffn_x[:, par, t, c * P:(c + 1) * P], ident)
                last.then_inc(sig("ffn_x_turned").sem, 1)

            def ffn_up_gate(b, par):
                wait(pe, "ffn_x_copied", b)
                for wt, done in ((wup_t, "up"), (wgate_t, "gate")):
                    for j in range(NF):
                        if done == "gate":
                            wait(pe, "up_copied", b, j + 1, NF)
                        elif not b.first():
                            wait(pe, "gate_copied", b, j + 1 - NF, NF)
                        for k in range(NC):
                            last = mm(flat(2 + j), wt[:, k, j * P:(j + 1) * P], ffn_xt[:, par, k],
                                      start=k == 0, stop=k == NC - 1)
                        last.then_inc(sig(done + "_done", NF).sem, 1)

            pipeline(pe, [(0, ffn_turn_x), (1, ffn_up_gate)])

            pe.wait_ge(ev("scale_ready"), QUANTIZED["v"])

            def turn_rows(first, rows, done):
                for c in range(NC):
                    for t in range(NT):
                        last = tr(flat(first + c)[:, t * P:(t + 1) * P], rows[:, t, c * P:(c + 1) * P], ident)
                last.then_inc(sig(done).sem, 1)

            def dn_project(b, par):
                wait_back(pe, "met_added", b, 2)
                wait_previous(pe, "dn_copied", b)
                for t in range(NT):
                    wait(pe, "dn_v_rounded", b, t + 1, NT)
                    for j in range(NF):
                        last = mm(rows2(5)[:, t], dn_v[:, t, j], wdown_t[:, j], start=j == 0, stop=j == NF - 1)
                    last.then_inc(sig("dn_projected", NT).sem, 1)

            def dn_turn(b, par):
                wait(pe, "y3_ready", b)
                wait_previous(pe, "met_states_ready", b)
                turn_rows(5, y3[:, par], "dn_turned")

            def met_project(b, par):
                wait(pe, "dn_copied", b)
                wait_next(pe, "dn_added", b)
                for c in range(NC):
                    for k in range(NC):
                        last = mm(flat(5 + c), w["met_wp"][:, k, c * P:(c + 1) * P], xt3[:, k],
                                  start=k == 0, stop=k == NC - 1)
                last.then_inc(sig("met_projected").sem, 1)

            def met_turn_p(b, par):
                wait(pe, "met_p_ready", b)
                wait_previous(pe, "met_x_copied", b)
                for t in range(NT):
                    for c in range(NC):
                        last = tr(rows2(5)[:, t, c * P:(c + 1) * P], met_p[:, c, t * P:(t + 1) * P], ident)
                last.then_inc(sig("met_p_turned").sem, 1)

            def met_queries(b, par):
                wait(pe, "met_pr_ready", b)
                for c in range(NC):
                    last = mm(flat(5 + c), met_m[:, c], met_p[:, c], start=True, stop=True)
                last.then_inc(sig("met_q_done").sem, 1)

            def met_state(b, par):
                wait(pe, "met_q_ready", b)
                for c in range(NC):
                    for t in range(NT - 1):
                        rows = met_pr[:, t, c * P:(c + 1) * P]
                        last = mm(flat(5 + c)[:, t * P:(t + 1) * P], rows, rows, start=True, stop=True)
                last.then_inc(sig("met_state_done").sem, 1)

            def met_scores(n):
                c, t, half = n // 8, n // 2 % 4, n % 2

                def step(b, par):
                    if n == 0:
                        wait(pe, "met_states_ready", b)
                        wait_next(pe, "dn_copied", b)
                    if n % 8 == 0:
                        wait(pe, "met_qh_ready", b, c + 1, 2)
                    if n >= 2:
                        wait(pe, "met_masked", b, n - 1, 16)
                    mm(flat(5 + half), met_p[:, c, t * P:(t + 1) * P],
                       met_qh[:, 4 * half:4 * half + 4, t * P:(t + 1) * P], start=True, stop=True)\
                        .then_inc(sig("met_scored", 16).sem, 1)
                return step

            def met_out(n):
                c, t, half = n // 8, n // 2 % 4, n % 2

                def step(b, par):
                    if n == 8:
                        wait(pe, "met_o_copied", b, 1, 2)
                    if n == 0:
                        wait_previous(pe, "met_o_copied", b, 2)
                    o = flat(7)[:, t * P:(t + 1) * P]
                    if half == 0 and t > 0:
                        mm(o, met_q[:, c, t * P:(t + 1) * P], met_st[:, c, t - 1], start=True, stop=False,
                           skip_group_check=True)
                    wait(pe, "met_masked", b, n + 1, 16)
                    for i in range(4):
                        h = 4 * half + i
                        last = mm(o[:, h * HD:(h + 1) * HD], met_s[:, n % 2, i],
                                  met_pr[:, t, c * P + h * HD:c * P + (h + 1) * HD],
                                  start=t == 0 and h == 0, stop=h == GH - 1, skip_group_check=True)
                    last.then_inc(sig("met_weighted", 16).sem, 1)
                return step

            def met_turn_o(b, par):
                wait(pe, "met_o_copied", b, 2, 2)
                turn_rows(5, met_o, "met_o_turned")

            def met_mix(b, par):
                wait(pe, "met_ot_ready", b)
                for t in range(NT):
                    for k in range(NC):
                        last = mm(rows2(5)[:, t], met_ot[:, k, t * P:(t + 1) * P], met_wo[:, k],
                                  start=k == 0, stop=k == NC - 1)
                last.then_inc(sig("met_mixed").sem, 1)

            def met_turn_x(b, par):
                wait(pe, "xn4_ready", b)
                wait_next(pe, "met_p_ready", b)
                turn_rows(5, xn4, "met_x_turned")

            def cos_vw_half(n):
                def step(b, par):
                    if n == 0:
                        pe.wait_ge(moved("cos_kv_loaded", par), b.half(64, 64))
                        wait_previous(pe, "cos_pt_copied", b, NT)
                    else:
                        wait(pe, "cos_vw_copied", b, 1, 2)
                        wait_previous(pe, "cos_x_copied", b)
                    for i in range(4):
                        last = mm(rows2(2)[:, i], cos_vb[:, par, 4 * n + i], w["cos_wo"][:, 4 * n + i],
                                  start=True, stop=True)
                    last.then_inc(sig("cos_vw_done", 2).sem, 1)
                return step

            def cos_nulls(b, par):
                wait(pe, "met_x_copied", b)
                wait_previous(pe, "cos_o_copied", b, NT)
                for t in range(NT):
                    for k in range(NC):
                        mm(flat(4)[:, t * 32 + H:t * 32 + 2 * H], xt4[:, k, t * P:(t + 1) * P], null_wq[:, k],
                           start=k == 0, stop=k == NC - 1)

            def cos_query(p):
                def step(b, par):
                    if p == 0:
                        wait_previous(pe, "spec_added", b)
                    if 2 <= p < NP:
                        wait(pe, "cos_q_squared", b, p - 1, NP)
                    if p < NP:
                        for k in range(NC):
                            last = mm(flat(p % 2), w["cos_wq"][:, k, p * P:(p + 1) * P], xt4[:, k],
                                      start=k == 0, stop=k == NC - 1)
                        last.then_inc(sig("cos_q_done", NP).sem, 1)
                    if p >= 1:
                        q = p - 1
                        wait(pe, "cos_q_squared", b, p, NP)
                        for t in range(NT):
                            last = mm(flat(4)[:, t * 32 + 2 * q:t * 32 + 2 * q + 2],
                                      cos_sq[:, q % 2, t * P:(t + 1) * P], w["half64"], start=True, stop=True)
                        last.then_inc(sig("cos_q_normed", NP).sem, 1)
                return step

            def cos_scores(t):
                def step(b, par):
                    if t:
                        wait(pe, "cos_scaled", b, t, NT)
                    for p in range(NP):
                        last = mm(flat(0, 2)[:, p * P:(p + 1) * P], cos_q[:, p, t * P:(t + 1) * P],
                                  cos_kb[:, par, p], start=True, stop=True)
                    last.then_inc(sig("cos_scored", NT).sem, 1)
                return step

            def cos_turn(t):
                def step(b, par):
                    wait(pe, "cos_probs_ready", b, t + 1, NT)
                    if t == 0:
                        wait(pe, "cos_vw_copied", b, 2, 2)
                        wait(pe, "cos_floored", b)
                    else:
                        wait(pe, "cos_o_copied", b, t, NT)
                    for p in range(NP):
                        tr(flat(2, 2)[:, p * P:(p + 1) * P], cos_s[:, t % 2, p * P:(p + 1) * P], ident)
                    tr(flat(4)[0:H, 0:P], cos_s[:, t % 2, H * TC:], ident)\
                        .then_inc(sig("cos_turned", NT).sem, 1)
                return step

            def cos_out(t):
                def step(b, par):
                    wait(pe, "cos_pt_copied", b, t + 1, NT)
                    for p in range(NP):
                        mm(flat(4)[:, C:2 * C], cos_pt[:, p], cos_vw[:, p], start=p == 0, stop=False)
                    mm(flat(4)[:, C:2 * C], cos_p0[0:H], null_w[0:H], start=False, stop=True)\
                        .then_inc(sig("cos_out_done", NT).sem, 1)
                return step

            def cos_turn_x(b, par):
                wait(pe, "y5_ready", b)
                wait_next(pe, "cos_vw_copied", b, 1, 2)
                turn_rows(2, y5, "cos_x_turned")

            def spec_project(b, par):
                wait(pe, "cos_x_copied", b)
                for t in range(NT):
                    for k in range(NC):
                        last = mm(rows2(0)[:, t], xt5[:, k, t * P:(t + 1) * P], spec_m[:, k],
                                  start=k == 0, stop=k == NC - 1)
                last.then_inc(sig("spec_done").sem, 1)

            def quarter(lo):
                out_steps = []
                for n in range(lo, lo + 4):
                    out_steps.append((1, met_scores(n)))
                    if n:
                        out_steps.append((1, met_out(n - 1)))
                return out_steps

            pipeline(pe, [(2, cos_vw_half(0)), (0, dn_project), (3, cos_turn_x), (1, met_project),
                          (2, cos_vw_half(1)), (2, met_turn_x), (3, spec_project), (1, met_turn_p),
                          (2, cos_nulls), (2, cos_query(0)), (1, met_queries),
                          (2, cos_query(1)), (2, cos_query(2)), (1, met_state), (2, cos_query(3)),
                          (2, cos_query(4)), (0, dn_turn), *[(2, cos_query(p)) for p in range(5, NP + 1)],
                          (2, cos_scores(0)), *quarter(0)[:4], (2, cos_scores(1)), *quarter(0)[4:], *quarter(4)[:4],
                          (2, cos_turn(0)), (2, cos_scores(2)), *quarter(4)[4:6], (2, cos_out(0)), *quarter(4)[6:],
                          (2, cos_turn(1)), (2, cos_scores(3)), *quarter(8)[:2], (2, cos_out(1)), *quarter(8)[2:],
                          (2, cos_turn(2)), (1, met_scores(12)), (1, met_out(11)), (2, cos_out(2)),
                          *quarter(12)[2:], (1, met_out(15)),
                          (2, cos_turn(3)), (1, met_turn_o), (2, cos_out(3)), (1, met_mix)])

        @block.scalar
        def _(act):
            f = nc.scalar.activation

            def copy_weight(name, dst):
                act.wait_ge(ev("weight_turned"), WEIGHTS[name])
                f(dst.rearrange("p a b -> p (a b)"), flat(0, 3), ACT.Copy).then_inc(ev("weight_copied"), 1)

            act.wait_ge(ev("ctx_transposed"), 1)
            f(ctx_t.rearrange("p a b c -> p (a b c)"), flat(0, 2), ACT.Copy).then_inc(ev("ctx_t_ready"), 1)
            act.wait_ge(ev("xat_k_projected"), 1)
            for c in range(NC):
                last = f(kt[:, c].rearrange("p a b -> p (a b)"), flat(2 + c), ACT.Identity,
                         bias=w["xat_bk"][:, c:c + 1])
            last.then_inc(ev("xat_k_biased"), 1)
            for p in range(NP):
                act.wait_ge(ev("cos_k_projected"), p + 1)
                f(kraw[:, p] if p < 2 else kraw_rest[:, p - 2], flat(4 + p % 2), ACT.Copy)
                f(ksq[:, p % 2], flat(4 + p % 2), ACT.Square).then_inc(ev("cos_k_squared"), 1)
            act.wait_ge(ev("cos_k_floored"), 1)
            f(krn[0:H], krn[0:H], ACT.Sqrt).then_inc(ev("cos_k_rooted"), 1)
            copy_weight("w_up", wup_t)
            act.wait_ge(ev("kbd_ready"), 1)
            for p in range(NP):
                act.wait_ge(ev("cos_v_projected"), p + 1)
                if p >= 2:
                    act.wait_ge(moved("cv_stored", p % 2), 16 * (p // 2))
                f(vst[:, p % 2], flat(p % 2), ACT.Copy).then_inc(ev("cos_v_copied"), 1)
                act.wait_ge(ev("cos_v_copied"), p + 1)
                act.dma_start(cv_d[:, p, :], vst[:, p % 2]).then_inc(moved("cv_stored", p % 2), 16)
            act.wait_ge(ev("cos_k_scaled"), NP)
            copy_weight("w_gate", wgate_t)
            act.wait_ge(ev("metric_product"), 1)
            f(met_m.rearrange("p a b -> p (a b)"), flat(3)[:, 0:C], ACT.Copy, scale=HD ** -0.5)
            f(null_w[0:H, :], flat(3)[0:H, C:2 * C], ACT.Copy)
            act.wait_ge(ev("mixer_product"), 1)
            f(met_wo.rearrange("p a b -> p (a b)"), flat(7), ACT.Copy)
            act.wait_ge(ev("spec_forward"), 1)
            f(at_r.rearrange("p a b -> p (a b)"), flat(5), ACT.Copy).then_inc(ev("spec_forward_copied"), 1)
            f(at_i.rearrange("p a b -> p (a b)"), flat(6), ACT.Copy).then_inc(ev("spec_forward_copied"), 1)
            copy_weight("w_down", wdown_t)
            act.wait_ge(ev("spec_product"), 1)
            f(spec_m.rearrange("p a b -> p (a b)"), flat(4), ACT.Copy, scale=1.0 / C).then_inc(ev("prep_done"), 1)
            act.wait_ge(ev("prep_done"), 3)

            def lin_copy_x(b, par):
                wait(act, "lin_x_turned", b)
                f(lin_xt[:, par].rearrange("p a b -> p (a b)"), flat(0, 2), ACT.Copy)\
                    .then_inc(sig("lin_x_copied").sem, 1)

            def lin_bias_q(b, par):
                wait(act, "lin_q_projected", b)
                for c in range(NC):
                    last = f(lin_zq[:, c], flat(2 + c), ACT.Identity, bias=w["lin_bq"][:, c:c + 1])
                last.then_inc(sig("lin_q_biased").sem, 1)

            def lin_exp_q(b, par):
                wait(act, "lin_q_negative", b)
                f(lin_eq, lin_eq, ACT.Exp).then_inc(sig("lin_q_exp").sem, 1)

            def lin_exp_k(b, par):
                wait(act, "lin_k_negative", b)
                f(lin_ek, lin_ek, ACT.Exp).then_inc(sig("lin_k_exp").sem, 1)

            def lin_copy_y(b, par):
                wait(act, "lin_y_turned", b)
                f(xt1.rearrange("p a b -> p (a b)"), flat(6, 2), ACT.Copy)\
                    .then_inc(sig("lin_y_copied").sem, 1)

            def xat_bias_q(b, par):
                wait(act, "xat_q_projected", b)
                for c in range(NC):
                    last = f(xat_q[:, c], flat(4 + c), ACT.Identity, bias=w["xat_bq"][:, c:c + 1])
                last.then_inc(sig("xat_q_biased").sem, 1)

            def xat_exp(t):
                def step(b, par):
                    wait(act, "xat_shifted", b, t + 1, NT)
                    s = xat_s[:, t % 2].rearrange("p a b -> p (a b)")
                    f(s, s, ACT.Exp, scale=HD ** -0.5).then_inc(sig("xat_exp_done", NT).sem, 1)
                return step

            def xat_copy_probs(t):
                def step(b, par):
                    wait(act, "xat_probs_turned", b, t + 1, NT)
                    f(xat_pt.rearrange("p a b -> p (a b)"), flat(6, 2), ACT.Copy)\
                        .then_inc(sig("xat_probs_copied", NT).sem, 1)
                return step

            def xat_copy_o(b, par):
                wait(act, "xat_o_turned", b)
                f(xat_ot.rearrange("p a b -> p (a b)"), flat(6, 2), ACT.Copy)\
                    .then_inc(sig("xat_o_copied").sem, 1)

            pipeline(act, [(0, lin_copy_x), (2, xat_copy_o), (1, lin_copy_y), (1, xat_bias_q),
                           (1, xat_exp(0)), (0, lin_exp_k),
                           (1, xat_exp(1)), (0, lin_bias_q), (1, xat_copy_probs(0)), (0, lin_exp_q), (1, xat_exp(2)),
                           (1, xat_copy_probs(1)), (1, xat_exp(3)),
                           (1, xat_copy_probs(2)), (1, xat_copy_probs(3))])

            act.wait_ge(ev("scale_ready"), QUANTIZED["x"])

            def ffn_copy_x(b, par):
                wait(act, "ffn_x_turned", b)
                f(ffn_xt[:, par].rearrange("p a b -> p (a b)"), flat(0, 2), ACT.Copy)\
                    .then_inc(sig("ffn_x_copied").sem, 1)

            def ffn_copy_products(b, par):
                wait_moved(act, "up_stored", b, par, 2)
                wait_back(act, "ffn_peaked", b, 2)
                g_b = at_cols(gated, b).rearrange("p (t j n) -> p t j n", t=NT, j=NF)
                for done in ("up", "gate"):
                    for j in range(NF):
                        wait(act, done + "_done", b, j + 1, NF)
                        f(g_b[:, :, j] if done == "gate" else ffn_up[:, par, :, j],
                          flat(2 + j).rearrange("p (t n) -> p t n", t=NT), ACT.Copy)\
                            .then_inc(sig(done + "_copied", NF).sem, 1)

            pipeline(act, [(0, ffn_copy_x), (1, ffn_copy_products)])

            wait_all_moved(act, "up_stored")

            act.wait_ge(ev("scale_ready"), QUANTIZED["gate"])

            def gate_round(b, par):
                wait_back(act, "t_ready", b, 2)
                f(gate_i[:, par], at_cols(gated, b), ACT.Copy, scale=quant["gate_mult"])\
                    .then_inc(sig("gate_rounded").sem, 1)

            def ffn_sigmoid(b, par):
                wait(act, "gate_rounded", b)
                f(sig_f[:, par], gate_i[:, par], ACT.Sigmoid, scale=quant["gate_scale"])\
                    .then_inc(sig("sigmoid_done").sem, 1)

            pipeline(act, [(1, ffn_sigmoid), (0, gate_round)])
            act.wait_ge(ev("scale_ready"), QUANTIZED["t"])

            def ffn_round_t(b, par):
                wait_back(act, "v_ready", b, 2)
                f(t_i[:, par], at_cols(gated, b), ACT.Copy, scale=quant["t_mult"])\
                    .then_inc(sig("t_rounded").sem, 1)


            def ffn_round_up(b, par):
                wait_moved(act, "up_loaded", b, par)
                f(up_i[:, par], up_f[:, 1 - par], ACT.Copy, scale=quant["up_mult"]).then_inc(sig("up_rounded").sem, 1)

            pipeline(act, [(0, ffn_round_t), (0, ffn_round_up)])

            wait_all_moved(act, "v_stored")

            def copy2(out_ap, first, name, after, j=1, per=1):
                def step(b, par):
                    wait(act, after, b, j, per)
                    f(out_ap, flat(first, 2), ACT.Copy).then_inc(sig(name, per).sem, 1)
                return step

            def cos_copy_q(p):
                def step(b, par):
                    wait(act, "cos_q_done", b, p + 1, NP)
                    if p >= 2:
                        wait(act, "cos_q_normed", b, p - 1, NP)
                    f(cos_q[:, p], flat(p % 2), ACT.Copy)
                    f(cos_sq[:, p % 2], flat(p % 2), ACT.Square).then_inc(sig("cos_q_squared", NP).sem, 1)
                return step

            def cos_exp(t):
                def step(b, par):
                    wait(act, "cos_shifted" if t < 2 else "cos_shifted_late", b, t % 2 + 1, 2)
                    f(cos_s[:, t % 2], cos_s[:, t % 2], ACT.Exp).then_inc(sig("cos_exp_done", NT).sem, 1)
                return step

            def cos_copy_pt(t):
                def step(b, par):
                    wait(act, "cos_turned", b, t + 1, NT)
                    f(cos_pt.rearrange("p a b -> p (a b)"), flat(2, 2), ACT.Copy)
                    f(cos_p0[0:H], flat(4)[0:H, 0:P], ACT.Copy).then_inc(sig("cos_pt_copied", NT).sem, 1)
                return step

            def cos_copy_o(t):
                def step(b, par):
                    wait(act, "cos_out_done", b, t + 1, NT)
                    if t == 0:
                        wait_previous(act, "y6_ready", b)
                    f(cos_o[:, t], flat(4)[:, C:2 * C], ACT.Copy).then_inc(sig("cos_o_copied", NT).sem, 1)
                return step

            def met_copy_o(c):
                def step(b, par):
                    wait(act, "met_weighted", b, 8 * c + 8, 16)
                    f(met_o[:, :, c * P:(c + 1) * P], flat(7).rearrange("p (t n) -> p t n", t=NT), ACT.Copy)\
                        .then_inc(sig("met_o_copied", 2).sem, 1)
                return step

            def all_of(ap):
                return ap.rearrange("p a b -> p (a b)")

            pipeline(act, [(2, copy2(all_of(cos_vw[:, 0:4]), 2, "cos_vw_copied", "cos_vw_done", 1, 2)),
                           (3, copy2(all_of(xt5), 2, "cos_x_copied", "cos_x_turned")),
                           (1, copy2(all_of(met_p), 5, "met_p_ready", "met_projected")),
                           (2, copy2(all_of(cos_vw[:, 4:8]), 2, "cos_vw_copied", "cos_vw_done", 2, 2)),
                           (2, copy2(all_of(xt4), 5, "met_x_copied", "met_x_turned")),
                           (1, copy2(all_of(met_pr), 5, "met_pr_ready", "met_p_turned")),
                           (2, cos_copy_q(0)),
                           (1, copy2(all_of(met_q), 5, "met_q_ready", "met_q_done")),
                           *[(2, cos_copy_q(p)) for p in range(1, 5)],
                           (0, copy2(all_of(xt3), 5, "dn_copied", "dn_turned")),
                           *[(2, cos_copy_q(p)) for p in range(5, NP)],
                           (2, cos_exp(0)), (2, cos_exp(1)), (2, cos_copy_pt(0)), (2, cos_copy_o(0)),
                           (2, cos_exp(2)), (2, cos_copy_pt(1)), (1, met_copy_o(0)), (2, cos_copy_o(1)),
                           (2, cos_exp(3)), (2, cos_copy_pt(2)), (2, cos_copy_o(2)), (1, met_copy_o(1)),
                           (2, cos_copy_pt(3)),
                           (1, copy2(all_of(met_ot), 5, "met_ot_ready", "met_o_turned")),
                           (2, cos_copy_o(3))])

        @block.gpsimd
        def _(pool):
            g = nc.gpsimd
            g.memset(neghalf, -0.5).then_inc(ev("constants_set"), 1)
            pool.wait_ge(ev("constants_set"), 1)
            pool.wait_ge(ev("null_k_floored"), 1)
            g.tensor_tensor(null_n, null_n, neghalf[:, 0:1], ALU.pow).then_inc(ev("null_k_rnormed"), 1)
            pool.wait_ge(ev("prep_done"), 3)

            def rstd(name, var):
                def step(b, par):
                    wait(pool, name + "_stats", b)
                    g.tensor_tensor(var[0], var[1], neghalf[:, 0:NT], ALU.pow)\
                        .then_inc(sig(name + "_rstd").sem, 1)
                return step

            pipeline(pool, [(1, rstd("lin", (lin_rs, lin_rs))), (2, rstd("xat", (xat_rs, xat_rs)))])

            for name in ("x", "up", "gate", "t", "v"):
                pool.wait_ge(ev("peak_found"), QUANTIZED[name])
                g.partition_all_reduce(quant[name + "_all"], quant[name + "_max"], P, bass.bass_isa.ReduceOp.max)\
                    .then_inc(ev("peak_shared"), 1)

            wait_all_moved(pool, "v_stored")
            g.memset(cos_kb, 0.0).then_inc(ev("pads_cleared"), 1)
            g.memset(cos_vb, 0.0).then_inc(ev("pads_cleared"), 1)

            def cos_norms(b, par):
                wait(pool, "cos_floored", b)
                for t in range(NT):
                    g.tensor_tensor(cos_nn[:, t, 0:H], cos_nn[:, t, 0:H], neghalf[:, 0:H], ALU.pow)\
                        .then_inc(sig("cos_rnormed", NT).sem, 1)

            def cos_shift(t):
                def step(b, par):
                    s, s0 = heads(t)
                    mx = cos_mx[:, t % 2]
                    wait(pool, "cos_maxed", b, t + 1, NT)
                    g.tensor_tensor(s0, s0, mx, ALU.subtract)
                    g.tensor_tensor(s, s, mx.unsqueeze(2).broadcast_to([P, H, TC]), ALU.subtract)\
                        .then_inc(sig("cos_shifted_late", 2).sem, 1)
                return step

            def cos_o_rstd(t):
                def step(b, par):
                    rs = norms["cos_o"][2][:, t:t + 1]
                    wait(pool, "cos_o_stats", b, t + 1, NT)
                    g.tensor_tensor(rs, rs, neghalf[:, 0:1], ALU.pow).then_inc(sig("cos_o_rstd", NT).sem, 1)
                return step

            def loop2_rstd(name):
                return rstd(name, (norms[name][2], norms[name][2]))

            pipeline(pool, [(3, cos_o_rstd(3)), (2, loop2_rstd("met")), (3, loop2_rstd("cos")),
                            (2, loop2_rstd("met2")), (0, loop2_rstd("dn")), (3, loop2_rstd("spec")),
                            (2, cos_norms), (2, cos_shift(2)), (2, cos_o_rstd(0)),
                            (2, cos_shift(3)), (2, cos_o_rstd(1)), (2, cos_o_rstd(2))])

        @block.vector
        def _(dve):
            v = nc.vector
            line = Line(dve, "vector_prep")
            link = line.link
            dve.wait_ge(ev("ctx_t_ready"), 1)
            for c in range(NC):
                v.tensor_copy(ctx_t2[:, c], ctx_t[:, c].unsqueeze(2).broadcast_to([P, B, 2, TC]))\
                    .then_inc(ev("ctx_t2_ready"), 1)

            def quantize(name):
                q = w[name].rearrange("p a (b c) -> p (a b) c", c=BLK)
                n = NF * C // BLK
                link(v.tensor_reduce(qmag, q, AX.X, ALU.max, apply_absolute_value=True))
                link(v.tensor_scalar(qmag, qmag, 1.0 / 7.0, 1e-12, ALU.mult, ALU.max))
                link(v.reciprocal(qrec, qmag))
                link(v.tensor_tensor(q, q, qrec.unsqueeze(2).broadcast_to([P, n, BLK]), ALU.mult))
                link(v.tensor_scalar(q, q, MAGIC, None, ALU.add))
                link(v.tensor_scalar(q, q, MAGIC, None, ALU.subtract))
                v.tensor_tensor(q, q, qmag.unsqueeze(2).broadcast_to([P, n, BLK]), ALU.mult)\
                    .then_inc(ev("weight_quantized"), 1)
                dve.wait_ge(ev("weight_quantized"), WEIGHTS[name])

            dve.wait_ge(loaded["pack_ffn"], 16)
            quantize("w_up")
            dve.wait_ge(ev("xat_k_biased"), 1)
            for c in range(NC):
                for h in range(GH):
                    last = v.tensor_scalar(kbd[:, c, :, h], kt[:, c], w["head16"][:, h:h + 1], None, ALU.mult)
            last.then_inc(ev("kbd_ready"), 1)
            link(v.tensor_scalar(gk, w["q_scale"], w["k_scale"], 8.0, ALU.mult, ALU.mult))
            dve.wait_ge(ev("cos_k_normed"), 1)
            v.tensor_scalar(krn[0:H], flat(6)[0:H], 1e-24, None, ALU.max).then_inc(ev("cos_k_floored"), 1)
            dve.wait_ge(ev("cos_k_rooted"), 1)
            v.reciprocal(krn[0:H], krn[0:H]).then_inc(ev("cos_k_inverted"), 1)
            quantize("w_gate")
            for p in range(NP):
                dve.wait_ge(ev("cos_k_spread"), p + 1)
                if p >= 2:
                    dve.wait_ge(moved("ck_stored", p % 2), 16 * (p // 2))
                v.scalar_tensor_tensor(out=kst[:, p % 2], in0=kraw[:, p] if p < 2 else kraw_rest[:, p - 2],
                                       scalar=gk, in1=flat(6 + p % 2), op0=ALU.mult, op1=ALU.mult)\
                    .then_inc(ev("cos_k_scaled"), 1)
            quantize("w_down")
            dve.wait_ge(ev("xat_v_projected"), 1)
            v.tensor_tensor(vtmp, rows2(4, 4), w["xat_bv"].unsqueeze(1).broadcast_to([P, B, C]), ALU.add)\
                .then_inc(ev("xat_v_biased"), 1)
            dve.wait_ge(ev("xat_v_biased"), 1)
            vb = vbd.rearrange("p a b c -> p (a b) c")
            v.tensor_tensor(vb[:, :, 0:2 * HD], vtmp.rearrange("p a (b c) -> p (a b) c", c=2 * HD),
                            w["pair16"][:, 0:2 * HD].unsqueeze(1).broadcast_to([P, B * NP, 2 * HD]), ALU.mult)
            v.tensor_copy(vb[:, :, 2 * HD:], w["pair16"][:, 2 * HD:].unsqueeze(1).broadcast_to([P, B * NP, 2]))
            dve.wait_ge(loaded["pack_l1"], 16)
            for c in range(NC):
                v.tensor_scalar(w["cos_wq"][:, c], w["cos_wq"][:, c], w["cos_gn"][:, c:c + 1], None, ALU.mult)
            link(v.tensor_tensor(null_k, w["null_row"], w["null_row"], ALU.mult))
            link(v.tensor_reduce(null_n, null_k, AX.X, ALU.add))
            v.tensor_scalar(null_n, null_n, 1e-24, None, ALU.max).then_inc(ev("null_k_floored"), 1)
            link(v.tensor_tensor(null_k, w["null_row"], w["q_row"], ALU.mult))
            link(v.scalar_tensor_tensor(out=null_k, in0=null_k, scalar=8.0, in1=w["k_row"], op0=ALU.mult,
                                        op1=ALU.mult))
            dve.wait_ge(ev("null_k_rnormed"), 1)
            link(v.tensor_scalar(null_k, null_k, null_n, None, ALU.mult))
            for c in range(NC):
                link(v.tensor_tensor(null_p, w["cos_wq"][:, c].rearrange("p (h k) -> p h k", h=H),
                                     null_k.unsqueeze(1).broadcast_to([P, H, CD]), ALU.mult))
                link(v.tensor_reduce(null_wq[:, c], null_p, AX.X, ALU.add))
            v.memset(spare, 0.0).then_inc(ev("prep_done"), 1)
            dve.wait_ge(ev("spec_product"), 1)
            dve.wait_ge(ev("weight_copied"), WEIGHTS["w_down"])
            v.memset(small, 0.0).then_inc(ev("prep_done"), 1)
            dve.wait_ge(ev("prep_done"), 3)

            lin, lin_end = Chain(dve, sem("vector_lin"), 8), Chain(dve, sem("vector_lin_end"), 2)
            xat, xat_end = Chain(dve, sem("vector_xat"), 8), Chain(dve, sem("vector_xat_end"), 5)

            def norm_stats(name, chain, r, st, mv, rs):
                for t in range(NT - 1):
                    v.bn_stats(st[:, t], r[:, t])
                chain.link(v.bn_stats(st[:, NT - 1], r[:, NT - 1]))
                v.memset(spare, 0.0)
                for t in range(NT - 1):
                    v.bn_aggr(mv[:, t], st[:, t])
                chain.link(v.bn_aggr(mv[:, NT - 1], st[:, NT - 1]))
                v.tensor_scalar(rs, mv[:, :, 1:2].rearrange("p a b -> p (a b)"), EPS, None, ALU.add)\
                    .then_inc(sig(name + "_stats").sem, 1)

            def normalize(name, b, y, r, mv, rs):
                wait(dve, name + "_rstd", b)
                for t in range(NT):
                    last = v.tensor_scalar(y[:, t], r[:, t], mv[:, t, 0:1], rs[:, t:t + 1],
                                           ALU.subtract, ALU.mult)
                return last

            def lin_q_negative(b, par):
                wait(dve, "lin_q_biased", b)
                v.tensor_scalar(lin_eq, lin_zq, 0.0, None, ALU.min).then_inc(sig("lin_q_negative").sem, 1)

            def lin_q_features(b, par):
                wait(dve, "lin_q_exp", b)
                v.scalar_tensor_tensor(out=lin_q, in0=lin_zq, scalar=0.0, in1=lin_eq, op0=ALU.max,
                                       op1=ALU.add).then_inc(sig("lin_q_ready").sem, 1)

            def lin_bias_kv(t):
                def step(b, par):
                    wait(dve, "lin_kv_projected", b, t + 1, NT)
                    v.tensor_tensor(lin_z[:, t], flat(t % 2), w["lin_bkv"], ALU.add)\
                        .then_inc(sig("lin_kv_biased", NT).sem, 1)
                return step

            def lin_k_negative(b, par):
                wait(dve, "lin_kv_biased", b, NT, NT)
                v.tensor_scalar(lin_ek, lin_z[:, :, 0:C], 0.0, None, ALU.min)\
                    .then_inc(sig("lin_k_negative").sem, 1)

            def lin_k_features(b, par):
                wait(dve, "lin_k_exp", b)
                v.scalar_tensor_tensor(out=lin_k, in0=lin_z[:, :, 0:C], scalar=0.0, in1=lin_ek, op0=ALU.max,
                                       op1=ALU.add).then_inc(sig("lin_k_ready").sem, 1)

            def lin_mask_state(b, par):
                wait(dve, "lin_state_done", b)
                for c in range(NC):
                    v.tensor_tensor(lin_kv[:, c, 0:P], flat(2)[:, c * P:(c + 1) * P], w["blk32"], ALU.mult)
                    last = v.tensor_scalar(lin_kv[:, c, P:], w["blk32"][:, 0:P:LD], flat(2)[:, C + c:C + c + 1],
                                           None, ALU.mult)
                last.then_inc(sig("lin_kv_ready").sem, 1)

            def lin_scale(t):
                def step(b, par):
                    if t == 0:
                        lin.begin(b)
                    wait(dve, "lin_out_done", b, t + 1, NT)
                    o = flat(LIN_BANKS[t])[:, 0:264].rearrange("p (c n) -> p c n", c=NC)
                    lin.link(v.tensor_scalar(lin_den[:, t % 2], o[:, :, P:], 1e-6, None, ALU.add))
                    lin.link(v.reciprocal(lin_den[:, t % 2], lin_den[:, t % 2]))
                    v.tensor_tensor(lin_r[:, t].rearrange("p (c h d) -> p c h d", c=NC, h=P // LD),
                                    o[:, :, 0:P].rearrange("p c (h d) -> p c h d", d=LD),
                                    lin_den[:, t % 2].unsqueeze(3).broadcast_to([P, NC, P // LD, LD]),
                                    ALU.mult).then_inc(sig("lin_scaled", NT).sem, 1)
                    if t == NT - 1:
                        lin.end()
                return step

            def lin_add(b, par):
                lin_end.begin(b)
                wait(dve, "lin_scaled", b, NT, NT)
                v.tensor_tensor(lin_r, lin_r, lin_x[:, par], ALU.add).then_inc(sig("lin_added").sem, 1)
                wait(dve, "lin_added", b)
                norm_stats("lin", lin_end, lin_r, lin_st, lin_mv, lin_rs)
                lin_end.end()

            def lin_finish(b, par):
                normalize("lin", b, y1[:, par], lin_r, lin_mv, lin_rs).then_inc(sig("y1_ready").sem, 1)

            def xat_shift(t):
                def step(b, par):
                    if t == 0:
                        xat.begin(b)
                    wait(dve, "xat_scored", b, t + 1, NT)
                    if t >= 2:
                        wait(dve, "xat_probs_turned", b, t - 1, NT)
                    s = flat(4, 2).rearrange("p (h k) -> p h k", k=TC)
                    mx = xat_mx[:, t % 2]
                    xat.link(v.tensor_reduce(mx, s, AX.X, ALU.max))
                    v.tensor_tensor(xat_s[:, t % 2], s, mx.unsqueeze(2).broadcast_to([P, H, TC]),
                                    ALU.subtract).then_inc(sig("xat_shifted", NT).sem, 1)
                return step

            def xat_normalize(t):
                def step(b, par):
                    wait(dve, "xat_weighted", b, t + 1, NT)
                    o = flat(3)[:, 0:NP * 34].rearrange("p (a n) -> p a n", a=NP)
                    rec = xat_rec.rearrange("p (a n) -> p a n", a=NP)
                    xat.link(v.reciprocal(rec, o[:, :, 2 * HD:]))
                    v.tensor_tensor(xat_o[:, t].rearrange("p (a h d) -> p a h d", a=NP, h=2),
                                    o[:, :, 0:2 * HD].rearrange("p a (h d) -> p a h d", h=2),
                                    rec.unsqueeze(3).broadcast_to([P, NP, 2, HD]),
                                    ALU.mult).then_inc(sig("xat_normed", NT).sem, 1)
                    if t == NT - 1:
                        xat.end()
                return step

            def xat_add(b, par):
                xat_end.begin(b)
                xat_end.link(v.tensor_tensor(xat_r, y1[:, par], w["xat_bo"].unsqueeze(1).broadcast_to([P, NT, C]), ALU.add))
                wait(dve, "xat_out_projected", b)
                v.tensor_tensor(xat_r, rows2(4), xat_r, ALU.add).then_inc(sig("xat_out_added").sem, 1)
                wait(dve, "xat_out_added", b)
                norm_stats("xat", xat_end, xat_r, xat_st, xat_mv, xat_rs)

            def xat_finish(b, par):
                wait_previous(dve, "x3_stored", b, 16)
                normalize("xat", b, y2[:, par], xat_r, xat_mv, xat_rs).then_inc(sig("y2_ready").sem, 1)

            def xat_peak(b, par):
                wait(dve, "y2_ready", b)
                xat_end.link(v.tensor_reduce(quant["tmp"], y2[:, par], AX.XY, ALU.max, apply_absolute_value=True))
                xat_end.link(v.tensor_tensor(quant["x_max"], quant["x_max"], quant["tmp"], ALU.max))
                xat_end.end()

            pipeline(dve, [(1, lin_add), (0, lin_bias_kv(0)), (1, lin_finish), (2, xat_add),
                           (0, lin_bias_kv(1)), (0, lin_bias_kv(2)), (2, xat_finish), (0, lin_bias_kv(3)),
                           (1, xat_shift(0)), (0, lin_k_negative), (1, xat_shift(1)),
                           (0, lin_k_features), (0, lin_q_negative), (1, xat_shift(2)), (0, lin_q_features),
                           (1, xat_normalize(0)), (1, xat_shift(3)), (1, xat_normalize(1)),
                           (0, lin_mask_state), (1, xat_normalize(2)), *[(0, lin_scale(t)) for t in range(NT)],
                           (1, xat_normalize(3)), (2, xat_peak)])

            def peak(name):
                v.tensor_copy(quant[name + "_max"], quant[name + "_max"]).then_inc(ev("peak_found"), 1)

            def scale(name, raw):
                dve.wait_ge(ev("peak_shared"), QUANTIZED[name])
                link(v.tensor_scalar(quant[name + "_scale"], quant[name + "_all"], raw, 1.0 / QMAX,
                                     ALU.mult, ALU.mult))
                link(v.tensor_scalar(quant[name + "_scale"], quant[name + "_scale"], 1e-12, None, ALU.max))
                link(v.reciprocal(quant[name + "_mult"], quant[name + "_scale"]))
                v.tensor_scalar(quant[name + "_mult"], quant[name + "_mult"], raw, None, ALU.mult)\
                    .then_inc(ev("scale_ready"), 1)
                dve.wait_ge(ev("scale_ready"), QUANTIZED[name])

            peak("x")
            scale("x", 1.0)
            ffn = Chain(dve, sem("vector_ffn"), 1)

            def ffn_round_x(b, par):
                wait_moved(dve, "ffn_x_loaded", b, par)
                v.tensor_scalar(ffn_x[:, par], ffn_x[:, par], quant["x_mult"], MAGIC, ALU.mult, ALU.add)\
                    .then_inc(sig("ffn_x_scaled").sem, 1)
                wait(dve, "ffn_x_scaled", b)
                v.tensor_scalar(ffn_x[:, par], ffn_x[:, par], MAGIC, None, ALU.subtract)\
                    .then_inc(sig("ffn_x_rounded").sem, 1)

            def ffn_peaks(b, par):
                ffn.begin(b)
                wait(dve, "up_copied", b, NF, NF)
                v.tensor_reduce(peaks[:, 0:1], ffn_up[:, par].rearrange("p a b c -> p (a b c)"), AX.X, ALU.max,
                                apply_absolute_value=True)
                wait(dve, "gate_copied", b, NF, NF)
                v.memset(spare, 0.0)
                v.tensor_reduce(peaks[:, 1:2], at_cols(gated, b), AX.X, ALU.max,
                                apply_absolute_value=True).then_inc(sig("ffn_peaked").sem, 1)
                wait(dve, "ffn_peaked", b)
                ffn.link(v.tensor_tensor(small[:, 2:4], small[:, 2:4], peaks[:, 0:2], ALU.max))
                ffn.end()

            pipeline(dve, [(0, ffn_round_x), (2, ffn_peaks)])
            peak("up")
            peak("gate")
            scale("up", quant["x_scale"])
            scale("gate", quant["x_scale"])
            link(v.tensor_scalar(quant["t_raw"], quant["gate_scale"], 1.0 / 65536.0, None, ALU.mult))
            wait_all_moved(dve, "up_stored")

            t_peaks = Chain(dve, None, 2, after=ffn)

            def gate_product(b, par):
                t_peaks.begin(b)
                wait(dve, "sigmoid_done", b)
                v.tensor_scalar(sig_i[:, par], sig_f[:, par], 65536.0, 65535.0, ALU.mult, ALU.min)\
                    .then_inc(sig("sigmoid_rounded").sem, 1)
                wait(dve, "sigmoid_rounded", b)
                v.tensor_tensor(at_cols(gated, b), gate_i[:, par], sig_i[:, par], ALU.mult)\
                    .then_inc(sig("t_ready").sem, 1)
                wait(dve, "t_ready", b)
                v.memset(spare, 0.0)
                t_peaks.link(v.tensor_reduce(quant["tmp"], at_cols(gated, b), AX.X, ALU.max,
                                            apply_absolute_value=True))
                t_peaks.link(v.tensor_tensor(quant["t_max"], quant["t_max"], quant["tmp"], ALU.max))
                t_peaks.end()

            pipeline(dve, [(0, gate_product)])
            peak("t")
            scale("t", quant["t_raw"])
            link(v.tensor_tensor(quant["v_raw"], quant["t_scale"], quant["up_scale"], ALU.mult))
            v_peaks = Chain(dve, None, 2, after=t_peaks)

            def product(b, par):
                v_peaks.begin(b)
                wait(dve, "t_rounded", b)
                wait(dve, "up_rounded", b)
                v.tensor_tensor(at_cols(gated, b), t_i[:, par], up_i[:, par], ALU.mult).then_inc(sig("v_ready").sem, 1)
                wait(dve, "v_ready", b)
                v.memset(spare, 0.0)
                v_peaks.link(v.tensor_reduce(quant["tmp"], at_cols(gated, b), AX.X, ALU.max,
                                             apply_absolute_value=True))
                v_peaks.link(v.tensor_tensor(quant["v_max"], quant["v_max"], quant["tmp"], ALU.max))
                v_peaks.end()

            pipeline(dve, [(0, product)])
            peak("v")
            scale("v", quant["v_raw"])

            wait_all_moved(dve, "v_stored")

            dn, met = Chain(dve, None, 2, after=v_peaks), Chain(dve, None, 2, after=lin)
            cos, spec = Chain(dve, None, 25, after=xat), Chain(dve, sem("vector_spec"), 3)
            met_end, cos_end = Chain(dve, None, 5, after=lin_end), Chain(dve, None, 5, after=xat_end)

            def stats(name, chain, rows):
                norm_stats(name, chain, rows, *norms[name])

            def scaled_rows(name, b, y, rows):
                return normalize(name, b, y, rows, norms[name][1], norms[name][2])

            def dn_round(t):
                def step(b, par):
                    wait_moved(dve, "v_loaded", b, par, 0 if par else 2)
                    v.tensor_scalar(dn_v[:, t], dn_v[:, t], quant["v_mult"], MAGIC, ALU.mult, ALU.add)\
                        .then_inc(sig("dn_v_scaled", NT).sem, 1)
                    wait(dve, "dn_v_scaled", b, t + 1, NT)
                    v.tensor_scalar(dn_v[:, t], dn_v[:, t], MAGIC, None, ALU.subtract)\
                        .then_inc(sig("dn_v_rounded", NT).sem, 1)
                return step

            def dn_add(b, par):
                dn.begin(b)
                wait(dve, "dn_projected", b, NT, NT)
                wait_moved(dve, "dn_x_loaded", b, par)
                dn_r = dn_x[:, par]
                v.scalar_tensor_tensor(out=dn_r, in0=rows2(5), scalar=quant["v_scale"], in1=dn_r,
                                       op0=ALU.mult, op1=ALU.add).then_inc(sig("dn_added").sem, 1)
                wait(dve, "dn_added", b)
                stats("dn", dn, dn_r)

            def dn_finish(b, par):
                scaled_rows("dn", b, y3[:, par], dn_x[:, par]).then_inc(sig("y3_ready").sem, 1)
                dn.end()

            def met_mask_queries(c):
                def step(b, par):
                    if c == 0:
                        met.begin(b)
                        wait(dve, "met_q_ready", b)
                    else:
                        wait(dve, "met_scored", b, 8, 16)
                    for h in range(GH):
                        last = v.tensor_scalar(met_qh[:, h], met_q[:, c], w["mhead16"][:, h:h + 1], None, ALU.mult)
                    last.then_inc(sig("met_qh_ready", 2).sem, 1)
                return step

            def met_mask_states(b, par):
                wait(dve, "met_state_done", b)
                n = (NT - 1) * P
                met.link(v.tensor_tensor(
                    met_st, bank(5, 2)[:, :, 0:n].rearrange("p c (t n) -> p c t n", t=NT - 1),
                    w["blk16"].unsqueeze(1).unsqueeze(1).broadcast_to([P, NC, NT - 1, P]), ALU.mult))
                met.link(v.tensor_tensor(met_st[:, :, 1], met_st[:, :, 1], met_st[:, :, 0], ALU.add))
                v.tensor_tensor(met_st[:, :, 2], met_st[:, :, 2], met_st[:, :, 1], ALU.add)\
                    .then_inc(sig("met_states_ready").sem, 1)
                met.end()

            def met_mask(n):
                def step(b, par):
                    wait(dve, "met_scored", b, n + 1, 16)
                    if n >= 2:
                        wait(dve, "met_weighted", b, n - 1, 16)
                    v.tensor_tensor(met_s[:, n % 2], flat(5 + n % 2).rearrange("p (h n) -> p h n", h=4),
                                    w["causal"].unsqueeze(1).broadcast_to([P, 4, P]), ALU.mult)\
                        .then_inc(sig("met_masked", 16).sem, 1)
                return step

            def met_add(b, par):
                met_end.begin(b)
                wait(dve, "met_mixed", b)
                v.tensor_tensor(met_r, rows2(5), y3[:, par], ALU.add).then_inc(sig("met_added").sem, 1)
                wait(dve, "met_added", b)
                stats("met", met_end, met_r)

            def met_norm(b, par):
                met_end.link(scaled_rows("met", b, y4[:, par], met_r))
                stats("met2", met_end, y4[:, par])

            def met_norm2(b, par):
                scaled_rows("met2", b, xn4, y4[:, par]).then_inc(sig("xn4_ready").sem, 1)
                met_end.end()

            def cos_floor(b, par):
                cos.begin(b)
                wait(dve, "cos_q_normed", b, NP, NP)
                nn = flat(4)[:, 0:NT * 32].rearrange("p (t n) -> p t n", t=NT)
                v.tensor_scalar(cos_nn[:, :, 0:H], nn[:, :, 0:H], 1e-24, None, ALU.max)
                v.tensor_copy(cos_nn[:, :, H:], nn[:, :, H:]).then_inc(sig("cos_floored").sem, 1)
                wait(dve, "cos_floored", b)

            def cos_scale(t):
                def step(b, par):
                    s, s0 = heads(t)
                    rn = cos_nn[:, t, 0:H]
                    wait(dve, "cos_rnormed", b, t + 1, NT)
                    wait(dve, "cos_scored", b, t + 1, NT)
                    if t >= 2:
                        wait(dve, "cos_turned", b, t - 1, NT)
                    v.tensor_tensor(s0, cos_nn[:, t, H:], rn, ALU.mult)
                    v.tensor_tensor(s, flat(0, 2).rearrange("p (h k) -> p h k", h=H),
                                    rn.unsqueeze(2).broadcast_to([P, H, TC]), ALU.mult)\
                        .then_inc(sig("cos_scaled", NT).sem, 1)
                return step

            def cos_max(t):
                def step(b, par):
                    s, s0 = heads(t)
                    mx = cos_mx[:, t % 2]
                    wait(dve, "cos_scaled", b, t + 1, NT)
                    cos.link(v.tensor_reduce(mx, s, AX.X, ALU.max))
                    v.tensor_tensor(mx, mx, s0, ALU.max).then_inc(sig("cos_maxed", NT).sem, 1)
                    if t < 2:
                        wait(dve, "cos_maxed", b, t + 1, NT)
                return step

            def cos_shift(t):
                def step(b, par):
                    s, s0 = heads(t)
                    mx = cos_mx[:, t % 2]
                    v.tensor_tensor(s0, s0, mx, ALU.subtract)
                    v.tensor_tensor(s, s, mx.unsqueeze(2).broadcast_to([P, H, TC]), ALU.subtract)\
                        .then_inc(sig("cos_shifted", 2).sem, 1)
                return step

            def cos_sum(t):
                def step(b, par):
                    s, s0 = heads(t)
                    mx = cos_mx[:, t % 2]
                    wait(dve, "cos_exp_done", b, t + 1, NT)
                    cos.link(v.tensor_reduce(mx, s, AX.X, ALU.add))
                    cos.link(v.tensor_tensor(mx, mx, s0, ALU.add))
                    cos.link(v.reciprocal(mx, mx))
                return step

            def cos_divide(t):
                def step(b, par):
                    s, s0 = heads(t)
                    mx = cos_mx[:, t % 2]
                    v.tensor_tensor(s0, s0, mx, ALU.mult)
                    v.tensor_tensor(s, s, mx.unsqueeze(2).broadcast_to([P, H, TC]), ALU.mult)\
                        .then_inc(sig("cos_probs_ready", NT).sem, 1)
                return step

            def cos_o_stats(t, chain):
                st, mv, rs = norms["cos_o"]

                def step(b, par):
                    if chain is cos_end:
                        chain.begin(b)
                    wait(dve, "cos_o_copied", b, t + 1, NT)
                    chain.link(v.bn_stats(st[:, t], cos_o[:, t]))
                    v.memset(spare, 0.0)
                    chain.link(v.bn_aggr(mv[:, t], st[:, t]))
                    v.tensor_scalar(rs[:, t:t + 1], mv[:, t, 1:2], EPS, None, ALU.add)\
                        .then_inc(sig("cos_o_stats", NT).sem, 1)
                return step

            def cos_o_add(t, chain):
                st, mv, rs = norms["cos_o"]

                def step(b, par):
                    wait(dve, "cos_o_rstd", b, t + 1, NT)
                    chain.link(v.scalar_tensor_tensor(out=cos_o[:, t], in0=cos_o[:, t], scalar=mv[:, t, 0:1],
                                                      in1=w["cos_go"], op0=ALU.subtract, op1=ALU.mult))
                    v.scalar_tensor_tensor(out=cos_o[:, t], in0=cos_o[:, t], scalar=rs[:, t:t + 1],
                                           in1=y4[:, par, t], op0=ALU.mult, op1=ALU.add)\
                        .then_inc(sig("cos_added", NT).sem, 1)
                    if t == NT - 1:
                        cos_end_added(b)
                    else:
                        v.memset(spare, 0.0)
                return step

            def cos_end_added(b):
                wait(dve, "cos_added", b, NT, NT)
                stats("cos", cos_end, cos_r)

            def cos_finish(b, par):
                scaled_rows("cos", b, y5, cos_r).then_inc(sig("y5_ready").sem, 1)
                wait(dve, "y5_ready", b)
                cos_end.end()

            def spec_add(b, par):
                spec.begin(b)
                spec.link(v.tensor_tensor(spec_r, y5, w["spec_b"].unsqueeze(1).broadcast_to([P, NT, C]), ALU.add))
                wait(dve, "spec_done", b)
                v.tensor_tensor(spec_r, rows2(0), spec_r, ALU.add).then_inc(sig("spec_added").sem, 1)
                wait(dve, "spec_added", b)
                stats("spec", spec, spec_r)

            def spec_finish(b, par):
                wait_previous(dve, "y_stored", b, 16)
                scaled_rows("spec", b, y6, spec_r).then_inc(sig("y6_ready").sem, 1)
                spec.end()

            def cos_slots_end(b, par):
                cos.end()

            def tile_steps(lo, t, ln):
                return [*[(2, cos_scale(t + 2))] * (t < 2), *[(1, met_mask(lo))] * (lo > 4),
                        *[(2, cos_max(t + 2))] * (t < 2), *[(1, met_mask(lo + 1))] * (lo > 4),
                        (2, cos_sum(t + 1)), (1, met_mask(lo + 2)), (2, cos_divide(t + 1)),
                        (1, met_mask(lo + 3)), *[(1, met_mask_queries(1))] * (lo == 4), (2, cos_o_stats(ln, cos))]

            pipeline(dve, [*[(0, dn_round(t)) for t in range(NT)], (3, cos_o_stats(3, cos_end)), (2, met_add),
                           (3, cos_o_add(3, cos_end)), (2, met_norm), (3, cos_finish), (2, met_norm2),
                           (0, dn_add), (3, spec_add), (0, dn_finish), (3, spec_finish),
                           (1, met_mask_queries(0)), (1, met_mask_states),
                           (2, cos_floor), (1, met_mask(0)), (2, cos_scale(0)), (1, met_mask(1)),
                           (2, cos_max(0)), (2, cos_shift(0)), (1, met_mask(2)), (2, cos_scale(1)),
                           (1, met_mask(3)), (2, cos_sum(0)), (1, met_mask(4)), (2, cos_divide(0)), (1, met_mask(5)), (2, cos_max(1)), (2, cos_shift(1)),
                           *tile_steps(4, 0, 0), (2, cos_o_add(0, cos)),
                           *tile_steps(8, 1, 1), (2, cos_o_add(1, cos)),
                           *tile_steps(12, 2, 2), (2, cos_o_add(2, cos)), (2, cos_slots_end)])


def kernel(**inputs):
    import concourse.bacc as bacc
    from concourse.bass_utils import run_bass_kernel_spmd

    a = {k: np.asarray(v) for k, v in inputs.items()}

    def rows(m):
        return m.reshape(-1, P, m.shape[-1]).transpose(1, 0, 2)

    def per_channel(vec):
        return vec.reshape(-1, P).T

    def on_all(vec):
        return np.broadcast_to(vec, (P, vec.shape[0]))

    def blocks(m):
        big = np.zeros((P, NC, P), m.dtype)
        for h in range(H):
            c, r = h // GH, h % GH * HD
            big[r:r + HD, c, r:r + HD] = m[h]
        return big

    p = np.arange(P)
    angle = 2 * np.pi * np.outer(np.arange(C), np.arange(C)) / C
    dft_r, dft_i = np.cos(angle).astype(np.float32), -np.sin(angle).astype(np.float32)
    f32 = lambda m: m.astype(np.float32)
    wkv = a["L1_xattn_Wkv"]
    null_v = np.zeros((P, NP, H), np.float32)
    for q in range(NP):
        null_v[:CD, q, 2 * q] = a["L1_xattn_null_kv"][1]
        null_v[CD:, q, 2 * q + 1] = a["L1_xattn_null_kv"][1]
    parts = {
        "ident": np.eye(P, dtype=np.float32),
        "ones": np.ones((P, P), np.float32),
        "lin_wq": rows(a["L0_attn_Wq"]),
        "lin_wkv": rows(np.concatenate([a["L0_attn_Wk"], a["L0_attn_Wv"]], 1)),
        "lin_bq": per_channel(a["L0_attn_bq"]),
        "lin_bkv": on_all(np.concatenate([a["L0_attn_bk"], a["L0_attn_bv"]])),
        "xat_wq": rows(a["L0_xattn_Wq"].T), "xat_bq": per_channel(a["L0_xattn_bq"]),
        "xat_wo": rows(a["L0_xattn_Wo"].T), "xat_bo": on_all(a["L0_xattn_bo"]),
        "blk32": f32(p[:, None] // LD == p // LD),
        "ctx": rows(a["ctx_1024"].reshape(B * TC, C)),
        "xat_wk": rows(a["L0_xattn_Wk"].T), "xat_bk": per_channel(a["L0_xattn_bk"]),
        "xat_wv": rows(a["L0_xattn_Wv"].T), "xat_bv": on_all(a["L0_xattn_bv"]),
        "head16": f32(p[:, None] // HD == np.arange(GH)),
        "pair16": f32(p[:, None] // CD == np.r_[np.arange(2 * HD) // HD, 0, 1]),
        "cos_wk": rows(wkv[:, :INNER]), "cos_wv": rows(wkv[:, INNER:]),
        "q_scale": np.tile(a["L1_xattn_q_scale"], 2)[:, None],
        "k_scale": np.tile(a["L1_xattn_k_scale"], 2)[:, None],
        "heads": f32(p[:, None, None] // CD + 2 * np.arange(NP)[:, None] == np.arange(H)),
        "head_rows": f32(p[:, None, None] == 2 * np.arange(NP)[:, None] + p // CD),
        "null_row": on_all(a["L1_xattn_null_kv"][0]), "q_row": on_all(a["L1_xattn_q_scale"]),
        "k_row": on_all(a["L1_xattn_k_scale"]),
        "w_up": rows(a["L0_ffn_w_up"]), "w_gate": rows(a["L0_ffn_w_gate"]),
        "w_down": rows(a["L0_ffn_w_down"]),
        "met_wp": rows(a["L1_attn_W_proj"].T), "cos_wq": rows(a["L1_xattn_Wq"]),
        "cos_gn": per_channel(a["L1_xattn_g_norm"]), "cos_wo": rows(a["L1_xattn_Wout"]),
        "cos_go": on_all(a["L1_xattn_g_out"]), "half64": f32(p[:, None] // CD == np.arange(2)),
        "blk16": f32(p[:, None] // HD == p // HD), "causal": f32(p[:, None] <= p),
        "spec_b": on_all(a["L1_ffn_bias"]), "mhead16": f32(p[:, None] // HD == np.arange(GH)),
        "met_pt": blocks(a["L1_attn_pre_metric_nkk"].transpose(0, 2, 1)),
        "met_tt": blocks(a["L1_attn_transforms_nkk"].transpose(0, 2, 1)),
        "met_wm": rows(a["L1_attn_W_mixer"].T), "null_v": null_v,
        "dft_r": rows(dft_r), "dft_i": rows(dft_i), "dft_ni": rows(-dft_i),
        "spec_wr": rows(a["L1_ffn_w_freq_real"]), "spec_wi": rows(a["L1_ffn_w_freq_imag"]),
    }
    arrays = {"x": np.ascontiguousarray(a["x"])}
    for name, pack in PACKS.items():
        arrays[name] = np.ascontiguousarray(
            np.concatenate([parts[n].reshape(P, -1) for n, _ in pack], 1).astype(np.float32))

    nc = bacc.Bacc("TRN2", target_bir_lowering=False, num_devices=1)
    args = [nc.dram_tensor(n, m.shape, F32, kind="ExternalInput").ap() for n, m in arrays.items()]
    args.append(nc.dram_tensor("y", (B, T, C), F32, kind="ExternalOutput").ap())
    decoder(nc, *args)
    result = run_bass_kernel_spmd(nc, [arrays], core_ids=[0])
    return result.results[0]["y"]
```
